# Optimizing a Trainium2 kernel written in Bass

```python
import numpy as np
import jax
import jax.numpy as jnp

def _softmax(x, axis=-1):
    return jax.nn.softmax(x, axis=axis)

def _gelu(x):
    return jax.nn.gelu(x, approximate=True)

def _silu(x):
    return jax.nn.silu(x)

def _sigmoid(x):
    return jax.nn.sigmoid(x)

def _layernorm(x, axis=-1, eps=1e-05):
    m = jnp.mean(x, axis=axis, keepdims=True)
    v = jnp.var(x, axis=axis, keepdims=True)
    return (x - m) / jnp.sqrt(v + eps)

def _scatter_add(tgt, idx, src, axis=0):
    return tgt.at[idx].add(src)

def _segment_sum(src, seg, n):
    return jax.ops.segment_sum(src, seg, n)
kernel_name = 'mk_adj_resnorm_d4_adj_r2_d67095'

def setup_inputs(seed: int=0):
    np.random.seed(seed)
    _w = jnp.asarray

    def _rec_inputs():
        import jax
        import jax.numpy as jnp
        _gk = jax.random.key(seed)
        x = 7.22e-05 + 1 * jax.random.normal(jax.random.fold_in(_gk, 1), (64, 128, 512), jnp.float32)
        _a = jax.random.bernoulli(jax.random.fold_in(_gk, 2), 0.03125, (128, 128))
        _a = jnp.logical_or(_a, jnp.swapaxes(_a, -1, -2))
        _a = jnp.logical_or(_a, jnp.eye(128, dtype=bool))
        _af = _a.astype(jnp.float32)
        _af = _af * jax.random.uniform(jax.random.fold_in(_gk, 3), (128, 128), jnp.float32, 0.05, 0.108252)
        adj = _af
        return (x, adj)
    x, adj = _rec_inputs()

    def _L0_gnn_setup():
        import jax, jax.numpy as jnp
        import numpy as np

        def _ada_gcn(xn, weight, bias):
            N, B, L = xn.shape
            x_norm = xn / jnp.maximum(jnp.linalg.norm(xn, axis=-1, keepdims=True), 1e-12)
            mean_sim = jnp.einsum('nbl,mbl->nm', x_norm, x_norm) / B
            k = max(int(N * 0.3), 1)
            _, idx = jax.lax.top_k(mean_sim, k + 1)
            rows = jnp.arange(N)[:, None]
            non_self = idx != rows
            order = jnp.cumsum(non_self.astype(jnp.int32), axis=1) - 1
            keep = non_self & (order < k)
            mask = jnp.zeros((N, N), dtype=bool).at[jnp.broadcast_to(rows, idx.shape), idx].set(keep)
            A = jnp.where(mask, mean_sim, jnp.zeros((), mean_sim.dtype))
            deg = A.sum(axis=0)
            dinv = jnp.where(deg > 0, jax.lax.rsqrt(deg), jnp.zeros((), deg.dtype))
            An = dinv[:, None] * A * dinv[None, :]
            xw = jnp.einsum('nbl,lo->nbo', xn, weight)
            out = jnp.einsum('sd,sbl->dbl', An, xw) + bias
            return out
        key = jax.random.key(seed)
        k1, k2 = jax.random.split(key)
        B, L, N = (32, 128, 512)
        x = jax.random.normal(k1, (B, L, N), dtype=jnp.float32)
        limit = float(np.sqrt(6.0 / (L + L)))
        weight = jax.random.uniform(k2, (L, L), dtype=jnp.float32, minval=-limit, maxval=limit)
        bias = jnp.zeros((L,), dtype=jnp.float32)
        return {'x': x, 'weight': weight, 'bias': bias}
    _L0_gnn_all = _L0_gnn_setup()
    _L0_gnn_in = {k: v for k, v in _L0_gnn_all.items() if k in ('bias',)}
    del _L0_gnn_all

    def _L1_gnn_setup():
        import jax, jax.numpy as jnp
        import numpy as np
        EPS = 1e-08

        def _row_stochastic_causal(A, causal_mask):
            A = A * causal_mask
            deg = jnp.maximum(A.sum(axis=-1, keepdims=True), EPS)
            return A / deg
        key = jax.random.key(seed)
        k = jax.random.split(key, 5)
        B, N, D = (4, 1024, 512)
        s = 1.0 / np.sqrt(D)
        h = jax.random.normal(k[0], (B, N, D), dtype=jnp.float32)
        W_lang = jax.random.normal(k[1], (D, D), dtype=jnp.float32) * s
        W_grav = jax.random.normal(k[2], (D, D), dtype=jnp.float32) * s
        W_V = jax.random.normal(k[3], (D, D), dtype=jnp.float32) * s
        W_O = jax.random.normal(k[4], (D, D), dtype=jnp.float32) * s
        causal_mask = jnp.tril(jnp.ones((N, N), dtype=jnp.float32))
        gate_logit = jnp.zeros((), jnp.float32)
        log_sigma = jnp.zeros((), jnp.float32)
        return {'h': h, 'causal_mask': causal_mask, 'W_lang': W_lang, 'W_grav': W_grav, 'W_V': W_V, 'W_O': W_O, 'gate_logit': gate_logit, 'log_sigma': log_sigma}
    _L1_gnn_all = _L1_gnn_setup()
    _L1_gnn_in = {k: v for k, v in _L1_gnn_all.items() if k in ('W_lang', 'W_grav', 'W_V', 'W_O', 'gate_logit', 'log_sigma')}
    del _L1_gnn_all

    def _L2_gnn_setup():
        import jax, jax.numpy as jnp
        import numpy as np

        def _ada_gcn(xn, weight, bias):
            N, B, L = xn.shape
            x_norm = xn / jnp.maximum(jnp.linalg.norm(xn, axis=-1, keepdims=True), 1e-12)
            mean_sim = jnp.einsum('nbl,mbl->nm', x_norm, x_norm) / B
            k = max(int(N * 0.3), 1)
            _, idx = jax.lax.top_k(mean_sim, k + 1)
            rows = jnp.arange(N)[:, None]
            non_self = idx != rows
            order = jnp.cumsum(non_self.astype(jnp.int32), axis=1) - 1
            keep = non_self & (order < k)
            mask = jnp.zeros((N, N), dtype=bool).at[jnp.broadcast_to(rows, idx.shape), idx].set(keep)
            A = jnp.where(mask, mean_sim, jnp.zeros((), mean_sim.dtype))
            deg = A.sum(axis=0)
            dinv = jnp.where(deg > 0, jax.lax.rsqrt(deg), jnp.zeros((), deg.dtype))
            An = dinv[:, None] * A * dinv[None, :]
            xw = jnp.einsum('nbl,lo->nbo', xn, weight)
            out = jnp.einsum('sd,sbl->dbl', An, xw) + bias
            return out
        key = jax.random.key(seed)
        k1, k2 = jax.random.split(key)
        B, L, N = (32, 128, 512)
        x = jax.random.normal(k1, (B, L, N), dtype=jnp.float32)
        limit = float(np.sqrt(6.0 / (L + L)))
        weight = jax.random.uniform(k2, (L, L), dtype=jnp.float32, minval=-limit, maxval=limit)
        bias = jnp.zeros((L,), dtype=jnp.float32)
        return {'x': x, 'weight': weight, 'bias': bias}
    _L2_gnn_all = _L2_gnn_setup()
    _L2_gnn_in = {k: v for k, v in _L2_gnn_all.items() if k in ('bias',)}
    del _L2_gnn_all

    def _L3_gnn_setup():
        import jax, jax.numpy as jnp
        import numpy as np
        DIM = 199
        K_HOP = 3

        def _khop_support(n, k):
            A = np.eye(n, dtype=np.float64)
            idx = np.arange(n)
            A[idx, (idx + 1) % n] = 1.0
            A[(idx + 1) % n, idx] = 1.0
            S = np.linalg.matrix_power(A, k)
            return (S > 0).astype(np.float32)
        key = jax.random.key(seed)
        kx, kk = jax.random.split(key)
        batch, n, f = (128, DIM, 512)
        x = jax.random.normal(kx, (batch, n, f), dtype=jnp.float32)
        support = jnp.asarray(_khop_support(n, K_HOP))
        limit = float(np.sqrt(6.0 / (n + n)))
        kernel = jax.random.uniform(kk, (n, n), minval=-limit, maxval=limit, dtype=jnp.float32)
        bias = jnp.zeros((f,), dtype=jnp.float32)
        return {'x': x, 'support': support, 'kernel': kernel, 'bias': bias}
    _L3_gnn_all = _L3_gnn_setup()
    _L3_gnn_in = {k: v for k, v in _L3_gnn_all.items() if k in ('bias',)}
    del _L3_gnn_all
    return {'x': x, 'adj': adj, 'L0_gnn_bias': _L0_gnn_in['bias'], 'L1_gnn_W_lang': _L1_gnn_in['W_lang'], 'L1_gnn_W_grav': _L1_gnn_in['W_grav'], 'L1_gnn_W_V': _L1_gnn_in['W_V'], 'L1_gnn_W_O': _L1_gnn_in['W_O'], 'L1_gnn_gate_logit': _L1_gnn_in['gate_logit'], 'L1_gnn_log_sigma': _L1_gnn_in['log_sigma'], 'L2_gnn_bias': _L2_gnn_in['bias'], 'L3_gnn_bias': _L3_gnn_in['bias']}

def reference(x, adj, L0_gnn_bias, L1_gnn_W_lang, L1_gnn_W_grav, L1_gnn_W_V, L1_gnn_W_O, L1_gnn_gate_logit, L1_gnn_log_sigma, L2_gnn_bias, L3_gnn_bias):
    import jax
    import jax.numpy as jnp

    def _L0_gnn_ref(x, weight, bias):
        import jax, jax.numpy as jnp
        import numpy as np

        def _ada_gcn(xn, weight, bias):
            N, B, L = xn.shape
            x_norm = xn / jnp.maximum(jnp.linalg.norm(xn, axis=-1, keepdims=True), 1e-12)
            mean_sim = jnp.einsum('nbl,mbl->nm', x_norm, x_norm) / B
            k = max(int(N * 0.3), 1)
            _, idx = jax.lax.top_k(mean_sim, k + 1)
            rows = jnp.arange(N)[:, None]
            non_self = idx != rows
            order = jnp.cumsum(non_self.astype(jnp.int32), axis=1) - 1
            keep = non_self & (order < k)
            mask = jnp.zeros((N, N), dtype=bool).at[jnp.broadcast_to(rows, idx.shape), idx].set(keep)
            A = jnp.where(mask, mean_sim, jnp.zeros((), mean_sim.dtype))
            deg = A.sum(axis=0)
            dinv = jnp.where(deg > 0, jax.lax.rsqrt(deg), jnp.zeros((), deg.dtype))
            An = dinv[:, None] * A * dinv[None, :]
            xw = jnp.einsum('nbl,lo->nbo', xn, weight)
            out = jnp.einsum('sd,sbl->dbl', An, xw) + bias
            return out
        xn = jnp.transpose(x, (2, 0, 1))
        num_levels = 1
        for _ in range(num_levels):
            xn = _ada_gcn(xn, weight, bias)
        return jnp.transpose(xn, (1, 2, 0))

    def _L1_gnn_ref(h, causal_mask, W_lang, W_grav, W_V, W_O, gate_logit, log_sigma):
        import jax, jax.numpy as jnp
        import numpy as np
        EPS = 1e-08

        def _row_stochastic_causal(A, causal_mask):
            A = A * causal_mask
            deg = jnp.maximum(A.sum(axis=-1, keepdims=True), EPS)
            return A / deg
        z_l = jnp.einsum('bnd,ed->bne', h, W_lang)
        z_g = jnp.einsum('bnd,ed->bne', h, W_grav)
        v = jnp.einsum('bnd,ed->bne', h, W_V)
        N = h.shape[-2]
        not_eye = 1.0 - jnp.eye(N, dtype=h.dtype)
        zn = z_l / jnp.maximum(jnp.linalg.norm(z_l, axis=-1, keepdims=True), EPS)
        A_l = jnp.maximum(jnp.einsum('bnd,bmd->bnm', zn, zn), 0.0) * not_eye
        sq = jnp.sum(z_g * z_g, axis=-1, keepdims=True)
        d2 = jnp.maximum(sq + jnp.swapaxes(sq, -1, -2) - 2.0 * jnp.einsum('bnd,bmd->bnm', z_g, z_g), 0.0)
        sigma = jnp.exp(log_sigma)
        A_g = jnp.exp(-d2 / (2.0 * sigma * sigma)) * not_eye
        K_l = _row_stochastic_causal(A_l, causal_mask)
        K_g = _row_stochastic_causal(A_g, causal_mask)
        w_l = jax.nn.sigmoid(gate_logit)
        K = w_l * K_l + (1.0 - w_l) * K_g
        out = jnp.einsum('bnm,bmd->bnd', K, v)
        return jnp.einsum('bnd,ed->bne', out, W_O)

    def _L2_gnn_ref(x, weight, bias):
        import jax, jax.numpy as jnp
        import numpy as np

        def _ada_gcn(xn, weight, bias):
            N, B, L = xn.shape
            x_norm = xn / jnp.maximum(jnp.linalg.norm(xn, axis=-1, keepdims=True), 1e-12)
            mean_sim = jnp.einsum('nbl,mbl->nm', x_norm, x_norm) / B
            k = max(int(N * 0.3), 1)
            _, idx = jax.lax.top_k(mean_sim, k + 1)
            rows = jnp.arange(N)[:, None]
            non_self = idx != rows
            order = jnp.cumsum(non_self.astype(jnp.int32), axis=1) - 1
            keep = non_self & (order < k)
            mask = jnp.zeros((N, N), dtype=bool).at[jnp.broadcast_to(rows, idx.shape), idx].set(keep)
            A = jnp.where(mask, mean_sim, jnp.zeros((), mean_sim.dtype))
            deg = A.sum(axis=0)
            dinv = jnp.where(deg > 0, jax.lax.rsqrt(deg), jnp.zeros((), deg.dtype))
            An = dinv[:, None] * A * dinv[None, :]
            xw = jnp.einsum('nbl,lo->nbo', xn, weight)
            out = jnp.einsum('sd,sbl->dbl', An, xw) + bias
            return out
        xn = jnp.transpose(x, (2, 0, 1))
        num_levels = 1
        for _ in range(num_levels):
            xn = _ada_gcn(xn, weight, bias)
        return jnp.transpose(xn, (1, 2, 0))

    def _L3_gnn_ref(x, support, kernel, bias):
        import jax, jax.numpy as jnp
        import numpy as np
        DIM = 199
        K_HOP = 3

        def _khop_support(n, k):
            A = np.eye(n, dtype=np.float64)
            idx = np.arange(n)
            A[idx, (idx + 1) % n] = 1.0
            A[(idx + 1) % n, idx] = 1.0
            S = np.linalg.matrix_power(A, k)
            return (S > 0).astype(np.float32)
        W = support * kernel
        out = jnp.einsum('bnf,nm->bmf', x, W)
        out = out + bias
        return out
    x = _layernorm(x + _L0_gnn_ref(x, adj, L0_gnn_bias), axis=-1)
    x = _layernorm(x + _L1_gnn_ref(x, adj, L1_gnn_W_lang, L1_gnn_W_grav, L1_gnn_W_V, L1_gnn_W_O, L1_gnn_gate_logit, L1_gnn_log_sigma), axis=-1)
    x = _layernorm(x + _L2_gnn_ref(x, adj, L2_gnn_bias), axis=-1)
    x = _layernorm(x + _L3_gnn_ref(x, adj, adj, L3_gnn_bias), axis=-1)
    return x

_drawn_inputs = setup_inputs


def setup_inputs(seed=0):
    import zlib

    import numpy as np

    out = dict(_drawn_inputs(seed))
    spreads = {'L0_gnn_bias': (0.0, 0.1), 'L2_gnn_bias': (0.0, 0.1), 'L3_gnn_bias': (0.0, 0.1)}
    factors = {}
    for name, (base, spread) in spreads.items():
        noise = np.random.default_rng([zlib.crc32(name.encode()), seed]).standard_normal(out[name].shape)
        drawn = base * np.exp(spread * noise) if base else spread * noise
        out[name] = jnp.asarray(drawn.astype(out[name].dtype))
    for name, factor in factors.items():
        out[name] = (out[name] * factor).astype(out[name].dtype)
    return out
```

```python
from contextlib import ExitStack
from itertools import count

import numpy as np

import concourse.bass as bass
from concourse import mybir

F32 = mybir.dt.float32
F32R = mybir.dt.float32r
ALU = mybir.AluOpType
ACT = mybir.ActivationFunctionType
AX = mybir.AxisListType

P = 128
N = 512
CH = N // P
GRP = 4
SGRP = 8
TOP = max(int(N * 0.3), 1)
LN_EPS = 1e-5
NORM_EPS = 1e-12
EPS = 1e-8
NEVER = -2.0 ** 126
CHOSEN = -2.0 ** 127
TRI = [0, 512, 896, 1152]
TRI_W = 1280

SERIAL = count()



def own_step(eng, passed):
    eng.sem_inc(passed, 1)


class Shared:
    pass


def scope(nc, ctx):
    own = lambda name: f"{name}_{next(SERIAL)}"
    sb = lambda name, shape, dt=F32: ctx.enter_context(nc.sbuf_tensor(own(name), shape, dt))
    ps = lambda name, shape=(P, 512): ctx.enter_context(nc.psum_tensor(own(name), list(shape), F32))
    taken = []

    def sem(name):
        taken.append(nc.alloc_semaphore(own(name)))
        return taken[-1]

    def give_back():
        if taken:
            nc.clear_and_free_semaphores(taken)
            nc.all_engine_barrier()

    ctx.callback(give_back)
    return sb, ps, sem


def over(ap, n):
    return ap.unsqueeze(1).broadcast_to([P, n, ap.shape[1]])


def along(ap, m):
    return ap.unsqueeze(2).broadcast_to([P, ap.shape[1], m])


def constants(nc, ctx, s, adj, bias0, bias2, bias3, gate, log_sigma):
    sb, _, _ = scope(nc, ctx)
    s.ident, s.ones, s.negones = sb("ident", [P, P]), sb("ones", [P, P]), sb("negones", [P, P])
    s.zeros_r = sb("zeros_r", [P, N], F32R)
    s.sel = sb("sel", [2 * SGRP, SGRP, P], F32R)
    s.neghalf = sb("neghalf", [P, GRP])
    s.adj, s.adj_ne = sb("adj_sb", [P, P]), sb("adj_ne", [P, P])
    s.adj2, s.adj2_hi, s.adj2_lo = sb("adj2", [P, P]), sb("adj2_hi", [P, P], F32R), sb("adj2_lo", [P, P], F32R)
    s.b0, s.b2, s.b3 = sb("b0", [P, 1]), sb("b2", [P, 1]), sb("b3", [P, N])
    s.w_l, s.w_g, s.inv_s2 = sb("w_l", [P, 1]), sb("w_g", [P, 1]), sb("inv_s2", [P, 1])
    s.an_hi, s.an_lo = sb("an_hi", [P, CH, N], F32R), sb("an_lo", [P, CH, N], F32R)
    with ExitStack() as c2:
        sb, _, sem = scope(nc, c2)
        sel_a, sel_b = sb("sel_a", [2 * SGRP, SGRP, P]), sb("sel_b", [2 * SGRP, SGRP, P])
        gate_sb, lsig_sb, egate = sb("gate_sb", [P, 1]), sb("lsig_sb", [P, 1]), sb("egate", [P, 2])
        loaded, filled, shaped = sem("c_loaded"), sem("c_filled"), sem("c_shaped")
        act_done, dve_done = sem("c_act_done"), sem("c_dve_done")
        block = c2.enter_context(nc.Block())

        @block.sync
        def _(sp):
            sp.dma_start(s.adj[:], adj).then_inc(loaded, 16)
            sp.dma_start(s.b0[:], bias0.rearrange("(p a) -> p a", a=1)).then_inc(loaded, 16)
            sp.dma_start(s.b2[:], bias2.rearrange("(p a) -> p a", a=1)).then_inc(loaded, 16)
            sp.dma_start(s.b3[:], bias3.rearrange("(a n) -> a n", a=1).broadcast_to([P, N])).then_inc(loaded, 16)
            sp.dma_start(gate_sb[:], gate.broadcast_to([P, 1])).then_inc(loaded, 16)
            sp.dma_start(lsig_sb[:], log_sigma.broadcast_to([P, 1])).then_inc(loaded, 16)

        @block.gpsimd
        def _(pool):
            nc.gpsimd.memset(s.ident[:], 0.0).then_inc(filled, 1)
            nc.gpsimd.memset(s.ones[:], 1.0).then_inc(filled, 1)
            nc.gpsimd.memset(s.negones[:], -1.0).then_inc(filled, 1)
            nc.gpsimd.memset(s.neghalf[:], -0.5).then_inc(filled, 1)
            nc.gpsimd.memset(sel_a[:], 0.0).then_inc(filled, 1)
            nc.gpsimd.memset(sel_b[:], 0.0).then_inc(filled, 1)
            pool.wait_ge(filled, 6)
            nc.gpsimd.affine_select(out=s.ident[:], in_=s.ident[:], compare_op=ALU.not_equal, fill=1.0,
                                    base=0, pattern=[[-1, P]], channel_multiplier=1).then_inc(shaped, 1)
            for part, base in ((sel_a, 0), (sel_b, -SGRP)):
                nc.gpsimd.affine_select(out=part[:], in_=part[:], compare_op=ALU.not_equal, fill=1.0,
                                        base=base, pattern=[[-1, SGRP], [0, P]],
                                        channel_multiplier=1).then_inc(shaped, 1)

        @block.scalar
        def _(act):
            act.wait_ge(loaded, 96)
            nc.scalar.activation(egate[:, 0:1], gate_sb[:], ACT.Exp, scale=-1.0).then_inc(act_done, 1)
            nc.scalar.activation(s.inv_s2[:], lsig_sb[:], ACT.Exp, scale=-2.0).then_inc(act_done, 1)

        @block.vector
        def _(dve):
            nc.vector.memset(s.zeros_r[:].bitcast(F32), 0.0)
            dve.wait_ge(shaped, 3)
            nc.vector.tensor_tensor(s.sel[:], sel_a[:], sel_b[:], ALU.add)
            dve.wait_ge(loaded, 96)
            nc.vector.scalar_tensor_tensor(out=s.adj_ne[:], in0=s.ident[:], scalar=-1.0, in1=s.ones[:],
                                           op0=ALU.mult, op1=ALU.add).then_inc(dve_done, 1)
            nc.vector.tensor_tensor(s.adj2[:], s.adj[:], s.adj[:], ALU.mult).then_inc(dve_done, 1)
            dve.wait_ge(dve_done, 2)
            nc.vector.tensor_tensor(s.adj_ne[:], s.adj_ne[:], s.adj[:], ALU.mult)
            nc.vector.tensor_copy(s.adj2_hi[:], s.adj2[:]).then_inc(dve_done, 1)
            dve.wait_ge(dve_done, 3)
            nc.vector.tensor_tensor(s.adj2_lo[:], s.adj2[:], s.adj2_hi[:].bitcast(F32), ALU.subtract)
            dve.wait_ge(act_done, 2)
            nc.vector.tensor_scalar(egate[:, 1:2], egate[:, 0:1], 1.0, None, ALU.add).then_inc(dve_done, 1)
            dve.wait_ge(dve_done, 4)
            nc.vector.reciprocal(s.w_l[:], egate[:, 1:2]).then_inc(dve_done, 1)
            dve.wait_ge(dve_done, 5)
            nc.vector.tensor_scalar(s.w_g[:], s.w_l[:], -1.0, 1.0, ALU.mult, ALU.add)


def first_norms(nc, s, x, xres, n2):
    nb = x.shape[0]
    with ExitStack() as ctx:
        sb, ps, sem = scope(nc, ctx)
        sq = sb("sq", [P, 4, N])
        sums = ps("sums", [P, CH, nb])
        loaded = [sem(f"x_loaded{k}") for k in range(4)]
        squared, summed = sem("squared"), sem("summed")
        xv = x.rearrange("b l n -> l b n")
        block = ctx.enter_context(nc.Block())

        @block.sync
        def _(sp):
            with sp.Fori(0, nb // 8) as t:
                for k in range(4):
                    pair = sp.snap(8 * t + 2 * k)
                    sp.wait_ge(squared, 8 * t + 2 * k + 2)
                    sp.dma_start(xres[:, bass.ds(pair, 2), :], xv[:, bass.ds(pair, 2), :]).then_inc(loaded[k], 16)

        @block.scalar
        def _(act):
            act.sem_inc(squared, 8)
            with act.Fori(0, nb // 8) as t:
                for k in range(8):
                    if k % 2 == 0:
                        act.wait_ge(loaded[k // 2], 16 * (t + 1))
                    act.wait_ge(summed, 8 * t + k + 1)
                    nc.scalar.activation(sq[:, k % 4, :], xres[:, bass.ds(8 * t + k, 1), :].rearrange("p a n -> p (a n)"),
                                         ACT.Square).then_inc(squared, 1)
            act.wait_ge(summed, nb + 4)
            nc.scalar.activation(n2, sums[:], ACT.Copy)

        @block.tensor
        def _(pe):
            pe.sem_inc(summed, 4)
            with pe.Fori(0, nb // 8) as t:
                for k in range(8):
                    pe.wait_ge(squared, 8 + 8 * t + k + 1)
                    for c in range(CH):
                        mm = nc.tensor.matmul(sums[:, c, bass.ds(8 * t + k, 1)], sq[:, k % 4, c * P:(c + 1) * P],
                                              s.ones[:, 0:1], start=True, stop=True)
                    mm.then_inc(summed, 1)


def norm_rows(nc, s, n2, rows, spill_hi, spill_lo):
    nb = n2.shape[2]
    with ExitStack() as ctx:
        sb, ps, sem = scope(nc, ctx)
        nrm, inv = sb("nrm", [P, CH, nb]), sb("inv", [P, CH, nb])
        r_hi, r_lo = sb("r_hi", [nb, N], F32R), sb("r_lo", [nb, N], F32R)
        turned_ps = ps("turned_ps", [nb, N])
        rooted, dve_done, turned, spilt, back = (sem(x) for x in ("rooted", "r_dve", "turned", "spilt", "back"))
        block = ctx.enter_context(nc.Block())

        @block.scalar
        def _(act):
            nc.scalar.activation(nrm[:], n2, ACT.Sqrt).then_inc(rooted, 1)

        @block.vector
        def _(dve):
            dve.wait_ge(rooted, 1)
            nc.vector.tensor_scalar(nrm[:], nrm[:], NORM_EPS, None, ALU.max).then_inc(dve_done, 1)
            dve.wait_ge(dve_done, 1)
            nc.vector.reciprocal(inv[:], nrm[:]).then_inc(dve_done, 1)
            dve.wait_ge(turned, 1)
            nc.vector.tensor_copy(r_hi[:], turned_ps[:]).then_inc(dve_done, 1)
            dve.wait_ge(dve_done, 3)
            nc.vector.tensor_tensor(r_lo[:], turned_ps[:], r_hi[:].bitcast(F32), ALU.subtract).then_inc(dve_done, 1)

        @block.tensor
        def _(pe):
            pe.wait_ge(dve_done, 2)
            for c in range(CH):
                mm = nc.tensor.transpose(turned_ps[:, c * P:(c + 1) * P], inv[:, c, :], s.ident[:])
            mm.then_inc(turned, 1)

        @block.sync
        def _(sp):
            sp.wait_ge(dve_done, 4)
            sp.dma_start(spill_hi, r_hi[:].bitcast(F32)).then_inc(spilt, 16)
            sp.dma_start(spill_lo, r_lo[:].bitcast(F32)).then_inc(spilt, 16)
            sp.wait_ge(spilt, 32)
            for k, spill in enumerate((spill_hi, spill_lo)):
                sp.dma_start(rows[k * SGRP:(k + 1) * SGRP].bitcast(F32),
                             spill.rearrange("(g j) n -> j g n", j=SGRP)).then_inc(back, 16)
            sp.wait_ge(back, 32)


def similarity(nc, s, xres, rows, hh, hl, source):
    nb = xres.shape[1]
    hh_at = [hh[0][:, 0:512], hh[1][:, 0:384], hh[2][:, 0:256], hh[1][:, 384:512]]
    with ExitStack() as ctx:
        sb, ps, sem = scope(nc, ctx)
        xn, hi, lo = sb("xn", [P, 4, N]), sb("xn_hi", [P, 4, N], F32R), sb("xn_lo", [P, 4, N], F32R)
        scale = ps("scale")
        loaded = [sem(f"x_loaded{k}") for k in range(4)]
        scale_ready, normed, hi_ready, lo_ready = (sem(x) for x in ("scale_ready", "normed", "hi_ready", "lo_ready"))
        summed = sem("summed")
        passed = sem("passed")
        block = ctx.enter_context(nc.Block())

        if source is not None:
            sv = source.rearrange("b l n -> l b n")

            @block.sync
            def _(sp):
                with sp.Fori(0, nb // 8) as t:
                    for k in range(4):
                        pair = sp.snap(8 * t + 2 * k)
                        sp.wait_ge(normed, 8 * t + 2 * k + 2)
                        sp.dma_start(xres[:, bass.ds(pair, 2), :], sv[:, bass.ds(pair, 2), :]).then_inc(loaded[k], 16)

        @block.vector
        def _(dve):
            dve.sem_inc(normed, 8)
            with dve.Fori(0, nb // SGRP) as t:
                for k in range(SGRP):
                    if source is not None and k % 2 == 0:
                        dve.wait_ge(loaded[k // 2], 16 * (t + 1))
                    dve.wait_ge(scale_ready, 8 * t + k + 1)
                    dve.wait_ge(summed, 8 * t + k + 1)
                    nc.vector.tensor_tensor(xn[:, k % 4, :],
                                            xres[:, bass.ds(8 * t + k, 1), :].rearrange("p a n -> p (a n)"),
                                            scale[:], ALU.mult).then_inc(normed, 1)

        @block.scalar
        def _(act):
            with act.Fori(0, nb // SGRP) as t:
                for k in range(SGRP):
                    act.wait_ge(normed, 8 + 8 * t + k + 1)
                    nc.scalar.activation(hi[:, k % 4, :], xn[:, k % 4, :], ACT.Copy).then_inc(hi_ready, 1)

        @block.gpsimd
        def _(pool):
            with pool.Fori(0, nb // SGRP) as t:
                for k in range(SGRP):
                    pool.wait_ge(hi_ready, 8 * t + k + 1)
                    nc.gpsimd.tensor_tensor(lo[:, k % 4, :], xn[:, k % 4, :], hi[:, k % 4, :].bitcast(F32),
                                            ALU.subtract).then_inc(lo_ready, 1)

        @block.tensor
        def _(pe):
            def spread(t, k):
                pe.wait_ge(normed, 8 + 8 * t + k)
                own_step(pe, passed)
                g = t + k // SGRP if k >= SGRP else t
                nc.tensor.matmul(scale[:], s.sel[:, k % SGRP, :], rows[:, bass.ds(g, 1), :].rearrange("p a n -> p (a n)"),
                                 start=True, stop=True).then_inc(scale_ready, 1)

            def sums(t, k):
                pe.wait_ge(hi_ready, 8 * t + k + 1)
                h, l = hi[:, k % 4, :], lo[:, k % 4, :]
                for c in range(CH):
                    nc.tensor.matmul(hh_at[c], h[:, c * P:(c + 1) * P], h[:, c * P:N], start=False, stop=False,
                                     skip_group_check=True)
                pe.wait_ge(lo_ready, 8 * t + k + 1)
                for c in range(CH):
                    mm = nc.tensor.matmul(hl[c][:], h[:, c * P:(c + 1) * P], l, start=False, stop=False,
                                          skip_group_check=True)
                mm.then_inc(summed, 1)

            pe.sem_inc(summed, 4)
            for bank in (*hh, *hl):
                nc.tensor.matmul(bank[:], s.zeros_r[:, 0:P], s.zeros_r[:], start=True, stop=False,
                                 skip_group_check=True)
            spread(0, 0)
            spread(0, 1)
            turns = nb // SGRP
            with pe.Fori(0, turns - 1) as t:
                for k in range(SGRP):
                    spread(t, k + 2)
                    sums(t, k)
            for k in range(SGRP):
                if k + 2 < SGRP:
                    spread(turns - 1, k + 2)
                sums(turns - 1, k)


def whole_similarity(nc, s, hh, hl, sim, work):
    nb = s.nb
    hh_at = [hh[0][:, 0:512], hh[1][:, 0:384], hh[2][:, 0:256], hh[1][:, 384:512]]
    with ExitStack() as ctx:
        sb, ps, sem = scope(nc, ctx)
        hl_sb, part = sb("hl_sb", [P, CH, N]), sb("part", [P, CH, N])
        turn = ps("turn")
        hl_out, parted, turned, upper, low_turned, lower = (
            sem(x) for x in ("hl_out", "parted", "turned", "upper", "low_turned", "lower"))
        masked, padded = sem("masked"), sem("padded")
        block = ctx.enter_context(nc.Block())

        @block.scalar
        def _(act):
            for c in range(CH):
                nc.scalar.activation(hl_sb[:, c, :], hl[c][:], ACT.Copy, scale=1.0 / nb).then_inc(hl_out, 1)
            for c in range(1, CH):
                act.wait_ge(low_turned, c)
                nc.scalar.activation(sim[:, c, 0:c * P], turn[:, 0:c * P], ACT.Copy).then_inc(lower, 1)

        @block.tensor
        def _(pe):
            pe.wait_ge(hl_out, CH)
            for c in range(CH):
                if c:
                    pe.wait_ge(upper, c)
                for j in range(c, CH):
                    mm = nc.tensor.transpose(turn[:, j * P:(j + 1) * P], hl_sb[:, j, c * P:(c + 1) * P], s.ident[:])
                mm.then_inc(turned, 1)
            pe.wait_ge(upper, CH)
            for c in range(1, CH):
                if c > 1:
                    pe.wait_ge(lower, c - 1)
                for j in range(c):
                    mm = nc.tensor.transpose(turn[:, j * P:(j + 1) * P], sim[:, j, c * P:(c + 1) * P], s.ident[:])
                mm.then_inc(low_turned, 1)

        @block.vector
        def _(dve):
            nc.vector.memset(work[:, :, 0:8], NEVER).then_inc(padded, 1)
            for c in range(CH):
                dve.wait_ge(hl_out, c + 1)
                nc.vector.scalar_tensor_tensor(out=part[:, c, c * P:N], in0=hh_at[c], scalar=1.0 / nb,
                                               in1=hl_sb[:, c, c * P:N], op0=ALU.mult,
                                               op1=ALU.add).then_inc(parted, 1)
            for c in range(CH):
                dve.wait_ge(turned, c + 1)
                dve.wait_ge(parted, c + 1)
                nc.vector.tensor_tensor(sim[:, c, c * P:N], turn[:, c * P:N], part[:, c, c * P:N],
                                        ALU.add).then_inc(upper, 1)
            dve.wait_ge(upper, CH)
            dve.wait_ge(lower, CH - 1)
            for c in range(CH):
                nc.vector.tensor_copy(work[:, c, 8:8 + N], sim[:, c, :]).then_inc(masked, 1)
            for c in range(CH):
                dve.wait_ge(masked, c + 1)
                nc.vector.scalar_tensor_tensor(out=work[:, c, 8 + c * P:8 + (c + 1) * P], in0=s.ident[:],
                                               scalar=NEVER, in1=sim[:, c, c * P:(c + 1) * P],
                                               op0=ALU.mult, op1=ALU.add)


def choose(nc, s, work, weights):
    rounds, rest = TOP // 8, TOP % 8
    with ExitStack() as ctx:
        sb, ps, sem = scope(nc, ctx)
        best = sb("best", [P, CH, 8])
        found, marked, passed = sem("found"), sem("marked"), sem("passed")
        if weights is not None:
            w_dram, dst = weights
            raw = {k: sb(f"raw_{k}", [P, CH, N]) for k in w_dram}
            wo_t = sb("wo_t", [P, CH, N])
            tmp = sb("tmp", [P, 2, N])
            banks = [ps(f"prep{k}") for k in range(2)]
            w_loaded, made, out, hi_ready, lo_ready = (
                sem(x) for x in ("w_loaded", "made", "out", "w_hi_ready", "w_lo_ready"))
        block = ctx.enter_context(nc.Block())

        @block.vector
        def _(dve):
            def mark(c):
                nc.vector.match_replace(work[:, c, :], best[:, c, :], work[:, c, :], CHOSEN).then_inc(marked, 1)

            dve.sem_inc(marked, CH)
            with dve.Fori(0, rounds) as r:
                for c in range(CH):
                    dve.wait_ge(marked, CH * r + c + 1)
                    own_step(dve, passed)
                    nc.vector.max(best[:, c, :], work[:, c, :]).then_inc(found, 1)
                for c in range(CH):
                    dve.wait_ge(found, CH * r + c + 1)
                    own_step(dve, passed)
                    mark(c)
            if rest:
                for c in range(CH):
                    dve.wait_ge(marked, CH * rounds + c + 1)
                    nc.vector.max(best[:, c, :], work[:, c, :]).then_inc(found, 1)
                dve.wait_ge(found, CH * (rounds + 1))
                nc.vector.memset(best[:, :, rest:8], NEVER).then_inc(found, 1)
                dve.wait_ge(found, CH * (rounds + 1) + 1)
                for c in range(CH):
                    mark(c)

        if weights is None:
            return

        jobs = [("turn", None, c) for c in range(CH)]
        jobs += [(name, name, c) for name in ("lang", "grav") for c in range(CH)]
        jobs += [("ov", "ov", c) for c in range(CH)]

        @block.sync
        def _(sp):
            for k in w_dram:
                sp.dma_start(raw[k][:], w_dram[k].rearrange("(c p) n -> p c n", p=P)).then_inc(w_loaded, 16)

        @block.tensor
        def _(pe):
            pe.wait_ge(w_loaded, 16 * len(w_dram))
            for n, (kind, _, c) in enumerate(jobs):
                bank = banks[n % 2]
                if n >= 2:
                    pe.wait_ge(out, n - 1)
                if kind == "turn":
                    for j in range(CH):
                        mm = nc.tensor.transpose(bank[:, j * P:(j + 1) * P], raw["o"][:, j, c * P:(c + 1) * P], s.ident[:])
                elif kind == "ov":
                    for j in range(CH):
                        mm = nc.tensor.matmul(bank[:], raw["v"][:, j, c * P:(c + 1) * P], wo_t[:, j, :],
                                              start=(j == 0), stop=(j == CH - 1))
                else:
                    for j in range(CH):
                        mm = nc.tensor.matmul(bank[:, 0:N - c * P], raw[kind][:, j, c * P:(c + 1) * P],
                                              raw[kind][:, j, c * P:N], start=(j == 0), stop=(j == CH - 1))
                mm.then_inc(made, 1)

        @block.scalar
        def _(act):
            k = 0
            for n, (kind, name, c) in enumerate(jobs):
                bank = banks[n % 2]
                act.wait_ge(made, n + 1)
                if kind == "turn":
                    nc.scalar.activation(wo_t[:, c, :], bank[:], ACT.Copy).then_inc(out, 1)
                    continue
                w = N - c * P if name != "ov" else N
                if k >= 2:
                    act.wait_ge(lo_ready, k - 1)
                if name == "ov":
                    nc.scalar.activation(tmp[:, k % 2, :], bank[:], ACT.Copy).then_inc(out, 1)
                    d = dst[name][0][:, c, :]
                else:
                    if w > P:
                        nc.scalar.activation(tmp[:, k % 2, P:w], bank[:, P:w], ACT.Copy)
                    nc.scalar.activation(tmp[:, k % 2, 0:P], bank[:, 0:P], ACT.Copy, scale=0.5).then_inc(out, 1)
                    d = dst[name][0][:, TRI[c]:TRI[c] + w]
                act.wait_ge(out, n + 1)
                nc.scalar.activation(d, tmp[:, k % 2, 0:w], ACT.Copy).then_inc(hi_ready, 1)
                k += 1

        @block.gpsimd
        def _(pool):
            k = 0
            for kind, name, c in jobs:
                if kind == "turn":
                    continue
                w = N - c * P if name != "ov" else N
                d = [x[:, c, :] if name == "ov" else x[:, TRI[c]:TRI[c] + w] for x in dst[name]]
                pool.wait_ge(hi_ready, k + 1)
                nc.gpsimd.tensor_tensor(d[1], tmp[:, k % 2, 0:w], d[0].bitcast(F32),
                                        ALU.subtract).then_inc(lo_ready, 1)
                k += 1


def normal_adjacency(nc, s, sim, work):
    with ExitStack() as ctx:
        sb, ps, sem = scope(nc, ctx)
        a, an, diag = sb("a", [P, CH, N]), sb("an", [P, CH, N]), sb("diag", [P, CH, P])
        deg, pos, dinv = sb("deg", [P, CH]), sb("pos", [P, CH]), sb("dinv", [P, CH])
        deg_ps, row = ps("deg_ps", [P, CH]), ps("row")
        chosen, summed, dve_done, rooted, spread, hi_ready = (
            sem(x) for x in ("chosen", "deg_summed", "n_dve", "n_rooted", "spread", "n_hi"))
        block = ctx.enter_context(nc.Block())

        @block.vector
        def _(dve):
            for c in range(CH):
                nc.vector.scalar_tensor_tensor(out=a[:, c, :], in0=work[:, c, 8:8 + N], scalar=CHOSEN,
                                               in1=sim[:, c, :], op0=ALU.is_equal,
                                               op1=ALU.mult).then_inc(chosen, 1)
            dve.wait_ge(summed, 1)
            nc.vector.tensor_scalar(deg[:], deg_ps[:], 1e-37, None, ALU.max).then_inc(dve_done, 1)
            nc.vector.tensor_scalar(pos[:], deg_ps[:], 0.0, None, ALU.is_gt).then_inc(dve_done, 1)
            dve.wait_ge(dve_done, 2)
            dve.wait_ge(rooted, 1)
            nc.vector.tensor_tensor(dinv[:], dinv[:], pos[:], ALU.mult).then_inc(dve_done, 1)
            dve.wait_ge(dve_done, 3)
            nc.vector.tensor_tensor(diag[:], over(s.ident[:], CH), along(dinv[:], P), ALU.mult).then_inc(dve_done, 1)
            dve.wait_ge(spread, 1)
            for c in range(CH):
                nc.vector.scalar_tensor_tensor(out=an[:, c, :], in0=a[:, c, :], scalar=dinv[:, c:c + 1],
                                               in1=row[:], op0=ALU.mult, op1=ALU.mult).then_inc(dve_done, 1)
            for c in range(CH):
                dve.wait_ge(hi_ready, c + 1)
                nc.vector.tensor_tensor(s.an_lo[:, c, :], an[:, c, :], s.an_hi[:, c, :].bitcast(F32), ALU.subtract)

        @block.gpsimd
        def _(pool):
            pool.wait_ge(dve_done, 2)
            nc.gpsimd.tensor_tensor(dinv[:], deg[:], s.neghalf[:], ALU.pow).then_inc(rooted, 1)

        @block.tensor
        def _(pe):
            pe.wait_ge(chosen, CH)
            for j in range(CH):
                for c in range(CH):
                    mm = nc.tensor.matmul(deg_ps[:, j:j + 1], a[:, c, j * P:(j + 1) * P], s.ones[:, 0:1],
                                          start=(c == 0), stop=(c == CH - 1))
            mm.then_inc(summed, 1)
            pe.wait_ge(dve_done, 4)
            nc.tensor.matmul(row[:], s.ones[:], diag[:].rearrange("p c n -> p (c n)"),
                             start=True, stop=True).then_inc(spread, 1)

        @block.scalar
        def _(act):
            for c in range(CH):
                act.wait_ge(dve_done, 5 + c)
                nc.scalar.activation(s.an_hi[:, c, :], an[:, c, :], ACT.Copy).then_inc(hi_ready, 1)


def first(g):
    return isinstance(g, int) and g == 0


def statistics(nc, dve, y, stats, mean_var, var_eps, neg_mean, y_ok, stats_ok, n, passed):
    dve.wait_ge(y_ok, n)
    nc.vector.bn_stats(stats, y).then_inc(stats_ok, 1)
    dve.wait_ge(stats_ok, 3 * n - 2)
    own_step(dve, passed)
    nc.vector.bn_aggr(mean_var, stats).then_inc(stats_ok, 1)
    dve.wait_ge(stats_ok, 3 * n - 1)
    nc.vector.tensor_scalar(var_eps, mean_var[:, 1:2], LN_EPS, None, ALU.add)
    nc.vector.tensor_scalar(neg_mean, mean_var[:, 0:1], -1.0, None, ALU.mult).then_inc(stats_ok, 1)


def inverse_root(nc, pool, root, bias, var_eps, neg_mean, neghalf, stats_ok, root_ok, n):
    pool.wait_ge(stats_ok, 3 * n)
    nc.gpsimd.tensor_tensor(root, var_eps, neghalf, ALU.pow).then_inc(root_ok, 1)
    pool.wait_ge(root_ok, 2 * n - 1)
    nc.gpsimd.tensor_tensor(bias, neg_mean, root, ALU.mult).then_inc(root_ok, 1)


HILO = [(0, 0), (0, 1), (1, 0)]


def gnn_layer_pair(nc, s, x, out, u_l, u_g, wov, n2):
    nb = x.shape[0]
    groups = nb // GRP
    with ExitStack() as ctx:
        sb, ps, sem = scope(nc, ctx)
        xin = sb("xin", [P, GRP, N])
        xw_hi, xw_lo = sb("xw_hi", [P, 2, N], F32R), sb("xw_lo", [P, 2, N], F32R)
        ya, xa, xb = sb("ya", [P, 2, N]), sb("xa", [P, GRP, N]), sb("xb", [P, GRP, N])
        st_a, mv_a = sb("st_a", [P, 2, 6]), sb("mv_a", [P, 2, 2])
        ve_a, nm_a, rs_a, nb_a = (sb(n, [P, 2]) for n in ("ve_a", "nm_a", "rs_a", "nb_a"))
        ht = [sb(f"ht_{p}", [P, CH, GRP, P], F32R) for p in ("hi", "lo")]
        y = [sb(f"y_{p}", [P, 2, GRP, 2, P], F32R) for p in ("hi", "lo")]
        v = [sb(f"v_{p}", [P, GRP, N], F32R) for p in ("hi", "lo")]
        m = sb("m", [P, GRP, 2, P])
        prod = sb("prod", [P, GRP, 2, P])
        mnn, q_l, r_l = sb("mnn", [P, GRP, 2]), sb("q_l", [P, GRP]), sb("r_l", [P, GRP])
        dg_r = sb("dg_r", [P, GRP, P])
        a_l, a_g = sb("a_l", [P, GRP, P]), sb("a_g", [P, GRP, P])
        k_l, k_g = sb("k_l", [P, GRP, P]), sb("k_g", [P, GRP, P])
        deg, small = sb("deg_lg", [P, 2, GRP]), sb("small", [P, 8, GRP])
        kt = [sb(f"kt_{p}", [P, GRP, P], F32R) for p in ("hi", "lo")]
        yb, xo, sq = sb("yb", [P, 2, N]), sb("xo", [P, GRP, N]), sb("sq2", [P, GRP, N])
        st_b, mv_b = sb("st_b", [P, 2, 6]), sb("mv_b", [P, 2, 2])
        ve_b, nm_b, rs_b, nb_b = (sb(n, [P, 2]) for n in ("ve_b", "nm_b", "rs_b", "nb_b"))

        tr, yp, mp = [ps("tr0"), ps("tr1")], [ps("y_l"), ps("y_g")], [ps("m0"), ps("m1")]
        ht_ps = xw_ps, l0_ps = ps("xw_ps"), ps("l0_ps")

        x_loaded = [sem(f"x_in{i}") for i in range(GRP)]
        xw_made, xw_hi_ok, xw_lo_ok, l0_made = (sem(n) for n in ("xw_made", "xw_hi_ok", "xw_lo_ok", "l0_made"))
        ya_ok, st_a_ok, rs_a_ok, xa_ok, xb_ok = (
            sem(n) for n in ("ya_ok", "st_a_ok", "rs_a_ok", "xa_ok", "xb_ok"))
        ht_made, ht_hi_ok, ht_lo_ok = (sem(n) for n in ("ht_made", "ht_hi_ok", "ht_lo_ok"))
        y_made, y_hi_ok, y_lo_ok = (sem(n) for n in ("y_made", "y_hi_ok", "y_lo_ok"))
        m_made, m_ok, v_made, v_hi_ok, v_lo_ok = (sem(n) for n in ("m_made", "m_ok", "v_made", "v_hi_ok", "v_lo_ok"))
        prod_ok, mnn_ok, q_ok, r_ok, dgr_ok, ml_t, mg_t, r_row = (
            sem(n) for n in ("prod_ok", "mnn_ok", "q_ok", "r_ok", "dgr_ok", "ml_t", "mg_t", "r_row"))
        sl_ok, ul_ok, kl_ok, tg_ok, cl_ok, eg_ok, kg_ok, sm_ok, ka_ok, k_ok = (
            sem(n) for n in ("sl_ok", "ul_ok", "kl_ok", "tg_ok", "cl_ok", "eg_ok", "kg_ok", "sm_ok", "ka_ok", "k_ok"))
        kt_made, kt_hi_ok, kt_lo_ok, l1_made = (sem(n) for n in ("kt_made", "kt_hi_ok", "kt_lo_ok", "l1_made"))
        yb_ok, st_b_ok, rs_b_ok, xo_ok, sq_ok = (
            sem(n) for n in ("yb_ok", "st_b_ok", "rs_b_ok", "xo_ok", "sq_ok"))
        n2_made, n2_out = sem("n2_made"), sem("n2_out")
        stored = [sem(f"stored{i}") for i in range(GRP)]
        passed = sem("passed")
        block = ctx.enter_context(nc.Block())

        def turns(eng, turn):
            turn(None, 0)
            with eng.Fori(0, groups - 1) as g:
                turn(g, g + 1)
            turn(groups - 1, None)

        @block.sync
        def _(sp):
            def load(b, i):
                sp.dma_start(xin[:, i, :], x[bass.ds(b, 1)].rearrange("a p n -> p (a n)")).then_inc(x_loaded[i], 16)

            def store(b, i):
                sp.dma_start(out[bass.ds(b, 1)].rearrange("a p n -> p (a n)"), xo[:, i, :]).then_inc(stored[i], 16)

            for i in range(GRP):
                load(i, i)
            for i in range(GRP):
                sp.wait_ge(ya_ok, i + 1)
                load(GRP + i, i)
            with sp.Fori(0, groups - 2) as g:
                for i in range(GRP):
                    at = sp.snap(g * GRP + 2 * GRP + i)
                    sp.wait_ge(ya_ok, GRP * g + GRP + i + 1)
                    load(at, i)
                for i in range(GRP):
                    at = sp.snap(g * GRP + i)
                    sp.wait_ge(xo_ok, 2 + GRP * g + i + 1)
                    store(at, i)
            for g in (groups - 2, groups - 1):
                for i in range(GRP):
                    sp.wait_ge(xo_ok, 2 + GRP * g + i + 1)
                    store(g * GRP + i, i)
            for i in range(GRP):
                sp.wait_ge(stored[i], 16 * (groups + 1))

        @block.tensor
        def _(pe):
            def turn(g, ga):
                def hturn(i):
                    pe.wait_ge(xa_ok, GRP * ga + i + 1)
                    if i == 0:
                        pe.wait_ge(xw_lo_ok, 1 + GRP * (ga + 1))
                    elif i == 1:
                        pe.wait_ge(ya_ok, GRP * (ga + 1))
                    else:
                        pe.wait_ge(ht_lo_ok, GRP * ga + i - 1)
                    for c in range(CH):
                        mm = nc.tensor.transpose(ht_ps[i % 2][:, c * P:(c + 1) * P], xa[:, i, c * P:(c + 1) * P], s.ident[:])
                    mm.then_inc(ht_made, 1)

                def xw(i):
                    pe.wait_ge(x_loaded[i], 16 * (ga + 1))
                    pe.wait_ge(xw_lo_ok, GRP * ga + i + 1)
                    if i == 0 and not first(ga):
                        pe.wait_ge(ht_lo_ok, GRP * ga - 1)
                    for c in range(CH):
                        mm = nc.tensor.matmul(xw_ps[:, c * P:(c + 1) * P], xin[:, i, c * P:(c + 1) * P], s.adj[:],
                                              start=True, stop=True)
                    mm.then_inc(xw_made, 1)

                def l0(i):
                    pe.wait_ge(xw_hi_ok, GRP * ga + i + 1)
                    pe.wait_ge(xw_lo_ok, 1 + GRP * ga + i + 1)
                    if not first(ga) or i:
                        pe.wait_ge(ya_ok, GRP * ga + i)
                    if i == 0 and not first(ga):
                        pe.wait_ge(ht_lo_ok, GRP * ga)
                    xwp, anp = (xw_hi, xw_lo), (s.an_hi, s.an_lo)
                    for c in range(CH):
                        for n, (a, b) in enumerate(HILO):
                            mm = nc.tensor.matmul(l0_ps[:], xwp[a][:, i % 2, c * P:(c + 1) * P], anp[b][:, c, :],
                                                  start=(c == 0 and n == 0), stop=(c == CH - 1 and n == 2))
                    mm.then_inc(l0_made, 1)

                def yprod(c):
                    if c == 0:
                        pe.wait_ge(ht_hi_ok, GRP * (g + 1))
                        pe.wait_ge(ht_lo_ok, GRP * (g + 1))
                    for k, u in enumerate((u_l, u_g)):
                        if c == 0:
                            pe.wait_ge(v_lo_ok, GRP * (g + 1))
                        else:
                            pe.wait_ge(y_lo_ok, 8 * g + 2 * (c - 1) + k + 1)
                        for r in range(c + 1):
                            for n, (a, b) in enumerate(HILO):
                                at = TRI[r] + (c - r) * P
                                mm = nc.tensor.matmul(yp[k][:], u[a][:, at:at + P],
                                                      ht[b][:, r, :, :].rearrange("p i n -> p (i n)"),
                                                      start=(r == 0 and n == 0), stop=(r == c and n == 2))
                        mm.then_inc(y_made, 1)

                def mprod(c):
                    pe.wait_ge(y_hi_ok, 8 * g + 2 * (c + 1))
                    pe.wait_ge(y_lo_ok, 8 * g + 2 * (c + 1))
                    if c == 0:
                        pe.wait_ge(yb_ok, GRP * (g + 1))
                    for i in range(GRP):
                        for n, (a, b) in enumerate(HILO):
                            mm = nc.tensor.matmul(mp[i // 2][:, (i % 2) * 256:(i % 2) * 256 + 256], ht[a][:, c, i, :],
                                                  y[b][:, c % 2, i, :, :].rearrange("p k n -> p (k n)"),
                                                  start=(c == 0 and n == 0 and i % 2 == 0),
                                                  stop=(c == CH - 1 and n == 2), skip_group_check=True)
                    mm.then_inc(m_made, 1)

                def vprod(i):
                    if i < 2:
                        pe.wait_ge(y_lo_ok, 8 * g + 6 + i + 1)
                    else:
                        pe.wait_ge(v_lo_ok, GRP + GRP * g + i - 1)
                    for c in range(CH):
                        for n, (a, b) in enumerate(HILO):
                            mm = nc.tensor.matmul(yp[i % 2][:], ht[a][:, c, i, :], wov[b][:, c, :],
                                                  start=(c == 0 and n == 0), stop=(c == CH - 1 and n == 2))
                    mm.then_inc(v_made, 1)

                def m_l_turned():
                    pe.wait_ge(m_ok, 2 * (g + 1))
                    pe.wait_ge(kt_lo_ok, g + 1)
                    for i in range(GRP):
                        mm = nc.tensor.transpose(tr[0][:, i * P:(i + 1) * P], m[:, i, 0, :], s.ident[:])
                    mm.then_inc(ml_t, 1)

                def m_g_turned():
                    pe.wait_ge(prod_ok, g + 1)
                    pe.wait_ge(n2_out, g + 1)
                    for i in range(GRP):
                        nc.tensor.matmul(tr[1][:, i * P:(i + 1) * P], m[:, i, 1, :], s.ident[:],
                                         start=(i == 0), stop=False, skip_group_check=True)
                    nc.tensor.matmul(tr[1][:], s.negones[:], prod[:, :, 1, :],
                                     start=False, stop=True, skip_group_check=True).then_inc(mg_t, 1)

                def r_rows():
                    pe.wait_ge(dgr_ok, g + 1)
                    nc.tensor.matmul(mp[0][:], s.ones[:], dg_r[:].rearrange("p i n -> p (i n)"),
                                     start=True, stop=True).then_inc(r_row, 1)

                def k_turned():
                    pe.wait_ge(k_ok, GRP * (g + 1))
                    for i in range(GRP):
                        mm = nc.tensor.transpose(tr[0][:, i * P:(i + 1) * P], k_g[:, i, :], s.ident[:])
                    mm.then_inc(kt_made, 1)

                def l1(i):
                    if i == 0:
                        pe.wait_ge(kt_hi_ok, g + 1)
                        pe.wait_ge(kt_lo_ok, 1 + g + 1)
                    if i >= 2:
                        pe.wait_ge(yb_ok, GRP + GRP * g + i - 1)
                    for n, (a, b) in enumerate(HILO):
                        mm = nc.tensor.matmul(mp[i % 2][:], kt[a][:, i, :], v[b][:, i, :], start=(n == 0), stop=(n == 2))
                    mm.then_inc(l1_made, 1)

                A, B = ga is not None, g is not None
                for i in range(GRP):
                    if A:
                        xw(i)
                    if B:
                        yprod(i)
                    if A:
                        l0(i)
                    if B and i >= 1:
                        mprod(i - 1)
                if B:
                    vprod(0)
                    mprod(3)
                    vprod(1)
                    m_l_turned()
                    m_g_turned()
                    vprod(2)
                    r_rows()
                    vprod(3)
                if A:
                    hturn(0)
                    hturn(1)
                if B:
                    pe.wait_ge(tg_ok, GRP * (g + 1))
                    squares(g, 0)
                    k_turned()
                if A:
                    hturn(2)
                    hturn(3)
                if B:
                    squares(g, 1)
                    for i in range(GRP):
                        l1(i)

            def squares(g, half):
                pe.wait_ge(sq_ok, GRP * g + 2 * half + 2)
                for i in (2 * half, 2 * half + 1):
                    for c in range(CH):
                        mm = nc.tensor.matmul(tr[1][:, GRP * c + i:GRP * c + i + 1], sq[:, i, c * P:(c + 1) * P],
                                              s.ones[:, 0:1], start=True, stop=True)
                mm.then_inc(n2_made, 1)

            turns(pe, turn)
            pe.wait_ge(n2_out, 1 + groups)
            squares(groups, 0)
            squares(groups, 1)

        @block.scalar
        def _(act):
            copy = lambda o, i: nc.scalar.activation(o, i, ACT.Copy)

            def turn(g, ga):
                def ht_hi(i):
                    act.wait_ge(ht_made, GRP * ga + i + 1)
                    act.wait_ge(v_made, GRP * (ga + 1))
                    copy(ht[0][:, :, i, :], ht_ps[i % 2][:].rearrange("p (c n) -> p c n", c=CH)).then_inc(ht_hi_ok, 1)

                def xw_hi_(i):
                    act.wait_ge(xw_made, GRP * ga + i + 1)
                    act.wait_ge(l0_made, GRP * ga + i + 1)
                    copy(xw_hi[:, i % 2, :], xw_ps[:]).then_inc(xw_hi_ok, 1)

                def norm_a(i):
                    act.wait_ge(rs_a_ok, 2 * (GRP * ga + i + 1))
                    act.wait_ge(xb_ok, GRP * ga + i + 1)
                    nc.scalar.activation(xa[:, i, :], ya[:, i % 2, :], ACT.Identity, scale=rs_a[:, i % 2:i % 2 + 1],
                                         bias=nb_a[:, i % 2:i % 2 + 1]).then_inc(xa_ok, 1)

                def y_hi(c):
                    for k in range(2):
                        act.wait_ge(y_made, 8 * g + 2 * c + k + 1)
                        act.wait_ge(m_made, CH * g + c + 1)
                        copy(y[0][:, c % 2, :, k, :], yp[k][:].rearrange("p (i n) -> p i n", i=GRP)).then_inc(y_hi_ok, 1)

                def v_hi(i):
                    act.wait_ge(v_made, GRP + GRP * g + i + 1)
                    copy(v[0][:, i, :], yp[i % 2][:]).then_inc(v_hi_ok, 1)

                def m_out():
                    act.wait_ge(m_made, 2 + CH * (g + 1))
                    for k in range(2):
                        copy(m[:, 2 * k:2 * k + 2, :, :].rearrange("p i k n -> p (i k n)"), mp[k][:]).then_inc(m_ok, 1)

                def exp_g():
                    act.wait_ge(cl_ok, g + 1)
                    nc.scalar.activation(a_g[:], a_g[:], ACT.Exp, scale=s.inv_s2[:, 0:1]).then_inc(eg_ok, 1)

                def kt_hi():
                    act.wait_ge(kt_made, g + 1)
                    copy(kt[0][:].rearrange("p i n -> p (i n)"), tr[0][:]).then_inc(kt_hi_ok, 1)

                def norm_b(i):
                    act.wait_ge(rs_b_ok, 2 * (GRP * g + i + 1))
                    act.wait_ge(stored[i], 16 * (g + 1))
                    nc.scalar.activation(xo[:, i, :], yb[:, i % 2, :], ACT.Identity, scale=rs_b[:, i % 2:i % 2 + 1],
                                         bias=nb_b[:, i % 2:i % 2 + 1]).then_inc(xo_ok, 1)

                def square(i):
                    act.wait_ge(xo_ok, 2 + GRP * g + i + 1)
                    nc.scalar.activation(sq[:, i, :], xo[:, i, :], ACT.Square).then_inc(sq_ok, 1)

                A, B = ga is not None, g is not None
                for i in range(GRP):
                    if A:
                        xw_hi_(i)
                    if B:
                        y_hi(i)
                    if A and i >= 1:
                        norm_a(i - 1)
                if B:
                    v_hi(0)
                    m_out()
                if A:
                    norm_a(GRP - 1)
                if B:
                    v_hi(1)
                    v_hi(2)
                    exp_g()
                    v_hi(3)
                if A:
                    ht_hi(0)
                    ht_hi(1)
                if B:
                    kt_hi()
                if A:
                    ht_hi(2)
                    ht_hi(3)
                if B:
                    sums_out(g)
                    for i in range(GRP):
                        norm_b(i)
                        if i >= 1:
                            square(i - 1)
                    square(3)

            def sums_out(g):
                act.wait_ge(n2_made, 2 * (g + 1))
                nc.scalar.activation(n2[:, :, bass.ds(GRP * g, GRP)], tr[1][:, 0:GRP * CH].rearrange(
                    "p (c i) -> p c i", c=CH), ACT.Copy).then_inc(n2_out, 1)

            act.sem_inc(l0_made, 2)
            act.sem_inc(m_made, 2)
            act.sem_inc(v_made, GRP)
            act.sem_inc(xo_ok, 2)
            act.sem_inc(n2_out, 1)
            for i in range(GRP):
                act.sem_inc(stored[i], 16)
            turns(act, turn)
            sums_out(groups)

        @block.gpsimd
        def _(pool):
            def turn(g, ga):
                if g is not None:
                    for i in range(GRP):
                        pool.wait_ge(xa_ok, GRP * g + i + 1)
                        pool.wait_ge(yb_ok, GRP * g + i + 1)
                        own_step(pool, passed)
                        nc.gpsimd.tensor_copy(xb[:, i, :], xa[:, i, :]).then_inc(xb_ok, 1)
                if ga is not None:
                    for i in range(GRP):
                        j = slice(i % 2, i % 2 + 1)
                        inverse_root(nc, pool, rs_a[:, j], nb_a[:, j], ve_a[:, j], nm_a[:, j],
                                     s.neghalf[:, 0:1], st_a_ok, rs_a_ok, GRP * ga + i + 1)
                if g is not None:
                    pool.wait_ge(q_ok, g + 1)
                    nc.gpsimd.tensor_tensor(r_l[:], q_l[:], s.neghalf[:], ALU.pow).then_inc(r_ok, 1)
                    for i in range(GRP):
                        j = slice(i % 2, i % 2 + 1)
                        inverse_root(nc, pool, rs_b[:, j], nb_b[:, j], ve_b[:, j], nm_b[:, j],
                                     s.neghalf[:, 0:1], st_b_ok, rs_b_ok, GRP * g + i + 1)

            pool.sem_inc(xb_ok, GRP)
            for i in range(GRP):
                nc.gpsimd.memset(sq[:, i, :], 0.0).then_inc(sq_ok, 1)
            turns(pool, turn)

        @block.vector
        def _(dve):
            def lo_part(lo, full, hi, done):
                nc.vector.tensor_tensor(lo, full, hi.bitcast(F32), ALU.subtract).then_inc(done, 1)

            def turn(g, ga):
                def ht_lo(i):
                    dve.wait_ge(ht_hi_ok, GRP * ga + i + 1)
                    lo_part(ht[1][:, :, i, :], ht_ps[i % 2][:].rearrange("p (c n) -> p c n", c=CH), ht[0][:, :, i, :], ht_lo_ok)

                def xw_lo_(i):
                    dve.wait_ge(xw_hi_ok, GRP * ga + i + 1)
                    lo_part(xw_lo[:, i % 2, :], xw_ps[:], xw_hi[:, i % 2, :], xw_lo_ok)

                def residual_a(i):
                    dve.wait_ge(l0_made, 2 + GRP * ga + i + 1)
                    if not first(ga) or i >= 2:
                        dve.wait_ge(xa_ok, GRP * ga + i - 1)
                    nc.vector.scalar_tensor_tensor(out=ya[:, i % 2, :], in0=l0_ps[:], scalar=s.b0[:, 0:1],
                                                   in1=xin[:, i, :], op0=ALU.add, op1=ALU.add).then_inc(ya_ok, 1)
                    j = slice(i % 2, i % 2 + 1)
                    statistics(nc, dve, ya[:, i % 2, :], st_a[:, i % 2, :], mv_a[:, i % 2, :], ve_a[:, j], nm_a[:, j],
                               ya_ok, st_a_ok, GRP * ga + i + 1, passed)

                def y_lo(c):
                    for k in range(2):
                        dve.wait_ge(y_hi_ok, 8 * g + 2 * c + k + 1)
                        lo_part(y[1][:, c % 2, :, k, :], yp[k][:].rearrange("p (i n) -> p i n", i=GRP),
                                y[0][:, c % 2, :, k, :], y_lo_ok)

                def v_lo(i):
                    dve.wait_ge(v_hi_ok, GRP * g + i + 1)
                    lo_part(v[1][:, i, :], yp[i % 2][:], v[0][:, i, :], v_lo_ok)

                def diagonals():
                    dve.wait_ge(m_ok, 2 * (g + 1))
                    m8 = m[:].rearrange("p i k n -> p (i k) n")
                    nc.vector.tensor_tensor(prod[:].rearrange("p i k n -> p (i k) n"), m8, over(s.ident[:], 2 * GRP),
                                            ALU.mult).then_inc(prod_ok, 1)
                    dve.wait_ge(prod_ok, g + 1)
                    nc.vector.tensor_reduce(mnn[:].rearrange("p i k -> p (i k)"),
                                            prod[:].rearrange("p i k n -> p (i k) n"), AX.X, ALU.add).then_inc(mnn_ok, 1)
                    dve.wait_ge(mnn_ok, g + 1)
                    nc.vector.tensor_scalar(q_l[:], mnn[:, :, 0], 2.0, EPS * EPS, ALU.mult, ALU.max).then_inc(q_ok, 1)

                def diag_r():
                    dve.wait_ge(r_ok, g + 1)
                    nc.vector.tensor_tensor(dg_r[:], over(s.ident[:], GRP), along(r_l[:], P), ALU.mult).then_inc(dgr_ok, 1)

                def metric_l():
                    dve.wait_ge(ml_t, g + 1)
                    nc.vector.tensor_tensor(a_l[:], m[:, :, 0, :], tr[0][:].rearrange("p (i n) -> p i n", i=GRP),
                                            ALU.add).then_inc(sl_ok, 1)

                def kernel_l():
                    dve.wait_ge(r_row, g + 1)
                    dve.wait_ge(sl_ok, g + 1)
                    flat = a_l[:].rearrange("p i n -> p (i n)")
                    nc.vector.scalar_tensor_tensor(out=flat, in0=flat, scalar=0.0, in1=mp[0][:],
                                                   op0=ALU.max, op1=ALU.mult).then_inc(ul_ok, 1)
                    dve.wait_ge(ul_ok, g + 1)
                    for i in range(GRP):
                        nc.vector.tensor_tensor_reduce(out=k_l[:, i, :], in0=a_l[:, i, :], in1=s.adj_ne[:], scale=1.0,
                                                       scalar=0.0, op0=ALU.mult, op1=ALU.add,
                                                       accum_out=deg[:, 0, i:i + 1]).then_inc(kl_ok, 1)

                def distances():
                    dve.wait_ge(mg_t, g + 1)
                    for i in range(GRP):
                        nc.vector.scalar_tensor_tensor(out=a_g[:, i, :], in0=m[:, i, 1, :], scalar=mnn[:, i, 1:2],
                                                       in1=tr[1][:, i * P:(i + 1) * P], op0=ALU.subtract,
                                                       op1=ALU.add).then_inc(tg_ok, 1)
                    dve.wait_ge(tg_ok, GRP * (g + 1))
                    nc.vector.tensor_scalar(a_g[:], a_g[:], 0.0, None, ALU.min).then_inc(cl_ok, 1)

                def kernel_g():
                    dve.wait_ge(eg_ok, g + 1)
                    for i in range(GRP):
                        nc.vector.tensor_tensor_reduce(out=k_g[:, i, :], in0=a_g[:, i, :], in1=s.adj_ne[:], scale=1.0,
                                                       scalar=0.0, op0=ALU.mult, op1=ALU.add,
                                                       accum_out=deg[:, 1, i:i + 1]).then_inc(kg_ok, 1)

                def kernel_sum():
                    n = 6 * g
                    dve.wait_ge(kl_ok, GRP * (g + 1))
                    nc.vector.tensor_tensor(small[:, 0, :], r_l[:], deg[:, 0, :], ALU.mult).then_inc(sm_ok, 1)
                    dve.wait_ge(kg_ok, GRP * (g + 1))
                    nc.vector.tensor_scalar(small[:, 1, :], deg[:, 1, :], EPS, None, ALU.max).then_inc(sm_ok, 1)
                    dve.wait_ge(sm_ok, n + 1)
                    nc.vector.tensor_scalar(small[:, 0, :], small[:, 0, :], EPS, None, ALU.max).then_inc(sm_ok, 1)
                    dve.wait_ge(sm_ok, n + 3)
                    nc.vector.reciprocal(small[:, 2:4, :], small[:, 0:2, :]).then_inc(sm_ok, 1)
                    dve.wait_ge(sm_ok, n + 4)
                    nc.vector.scalar_tensor_tensor(out=small[:, 4, :], in0=r_l[:], scalar=s.w_l[:, 0:1],
                                                   in1=small[:, 2, :], op0=ALU.mult, op1=ALU.mult).then_inc(sm_ok, 1)
                    nc.vector.tensor_scalar(small[:, 5, :], small[:, 3, :], s.w_g[:, 0:1], None, ALU.mult).then_inc(sm_ok, 1)
                    dve.wait_ge(sm_ok, n + 6)
                    for i in range(GRP):
                        nc.vector.tensor_scalar(k_l[:, i, :], k_l[:, i, :], small[:, 4, i:i + 1], None,
                                                ALU.mult).then_inc(ka_ok, 1)
                    for i in range(GRP):
                        dve.wait_ge(ka_ok, GRP * g + i + 1)
                        nc.vector.scalar_tensor_tensor(out=k_g[:, i, :], in0=k_g[:, i, :], scalar=small[:, 5, i:i + 1],
                                                       in1=k_l[:, i, :], op0=ALU.mult, op1=ALU.add).then_inc(k_ok, 1)

                def kt_lo():
                    dve.wait_ge(kt_hi_ok, g + 1)
                    lo_part(kt[1][:].rearrange("p i n -> p (i n)"), tr[0][:], kt[0][:].rearrange("p i n -> p (i n)"), kt_lo_ok)

                def residual_b(i):
                    dve.wait_ge(l1_made, GRP * g + i + 1)
                    dve.wait_ge(xb_ok, GRP + GRP * g + i + 1)
                    dve.wait_ge(xo_ok, GRP * g + i + 1)
                    nc.vector.tensor_tensor(yb[:, i % 2, :], mp[i % 2][:], xb[:, i, :], ALU.add).then_inc(yb_ok, 1)
                    dve.wait_ge(yb_ok, GRP + GRP * g + i + 1)
                    j = slice(i % 2, i % 2 + 1)
                    statistics(nc, dve, yb[:, i % 2, :], st_b[:, i % 2, :], mv_b[:, i % 2, :], ve_b[:, j], nm_b[:, j],
                               yb_ok, st_b_ok, GRP * g + i + 1, passed)

                A, B = ga is not None, g is not None
                for i in range(GRP):
                    if A:
                        xw_lo_(i)
                    if B:
                        y_lo(i)
                    if A:
                        residual_a(i)
                if B:
                    v_lo(0)
                    diagonals()
                    v_lo(1)
                    diag_r()
                    metric_l()
                    distances()
                    v_lo(2)
                    kernel_l()
                    v_lo(3)
                    kernel_g()
                    kernel_sum()
                if A:
                    ht_lo(0)
                    ht_lo(1)
                if B:
                    kt_lo()
                if A:
                    ht_lo(2)
                    ht_lo(3)
                if B:
                    for i in range(GRP):
                        residual_b(i)

            dve.sem_inc(xw_lo_ok, 1)
            dve.sem_inc(v_lo_ok, GRP)
            dve.sem_inc(kt_lo_ok, 1)
            dve.sem_inc(yb_ok, GRP)
            turns(dve, turn)


def last_layers(nc, s, x, out):
    nb = x.shape[0]
    groups = nb // GRP
    with ExitStack() as ctx:
        sb, ps, sem = scope(nc, ctx)
        xin = sb("xin", [P, GRP, N])
        xw_hi, xw_lo = sb("xw_hi", [P, 2, N], F32R), sb("xw_lo", [P, 2, N], F32R)
        ya, xa = sb("ya", [P, 2, N]), sb("xa", [P, 2, N])
        x_hi, x_lo = sb("x_hi", [P, GRP, N], F32R), sb("x_lo", [P, GRP, N], F32R)
        xb = sb("xb", [P, GRP, N])
        yb, xo = sb("yb", [P, 2, N]), sb("xo", [P, GRP, N])
        st_a, mv_a = sb("st_a", [P, 2, 6]), sb("mv_a", [P, 2, 2])
        ve_a, nm_a, rs_a, nb_a = (sb(n, [P, 2]) for n in ("ve_a", "nm_a", "rs_a", "nb_a"))
        st_b, mv_b = sb("st_b", [P, 2, 6]), sb("mv_b", [P, 2, 2])
        ve_b, nm_b, rs_b, nb_b = (sb(n, [P, 2]) for n in ("ve_b", "nm_b", "rs_b", "nb_b"))
        xw_ps, l2_ps, l3_ps = [ps("xw_ps0"), ps("xw_ps1")], [ps("l2_ps0"), ps("l2_ps1")], [ps("l3_ps0"), ps("l3_ps1")]

        x_loaded = [sem(f"x_in{i}") for i in range(GRP)]
        stored = [sem(f"stored{i}") for i in range(GRP)]
        passed = sem("passed")
        xw_made, xw_hi_ok, xw_lo_ok, l2_made, l3_made = (
            sem(n) for n in ("xw_made", "xw_hi_ok", "xw_lo_ok", "l2_made", "l3_made"))
        ya_ok, st_a_ok, rs_a_ok, xa_ok, x_hi_ok, x_lo_ok, xb_ok = (
            sem(n) for n in ("ya_ok", "st_a_ok", "rs_a_ok", "xa_ok", "x_hi_ok", "x_lo_ok", "xb_ok"))
        yb_ok, st_b_ok, rs_b_ok, xo_ok = (sem(n) for n in ("yb_ok", "st_b_ok", "rs_b_ok", "xo_ok"))
        block = ctx.enter_context(nc.Block())

        def turns(eng, turn):
            turn(None, 0)
            with eng.Fori(0, groups - 1) as g:
                turn(g, g + 1)
            turn(groups - 1, None)

        @block.sync
        def _(sp):
            def load(b, i):
                sp.dma_start(xin[:, i, :], x[bass.ds(b, 1)].rearrange("a p n -> p (a n)")).then_inc(x_loaded[i], 16)

            def store(b, i):
                sp.dma_start(out[bass.ds(b, 1)].rearrange("a p n -> p (a n)"), xo[:, i, :]).then_inc(stored[i], 16)

            for i in range(GRP):
                load(i, i)
            for i in range(GRP):
                sp.wait_ge(ya_ok, i + 1)
                load(GRP + i, i)
            with sp.Fori(0, groups - 2) as g:
                for i in range(GRP):
                    at = sp.snap(g * GRP + 2 * GRP + i)
                    sp.wait_ge(ya_ok, GRP * g + GRP + i + 1)
                    load(at, i)
                    at = sp.snap(g * GRP + i)
                    sp.wait_ge(xo_ok, 2 + GRP * g + i + 1)
                    store(at, i)
            for g in (groups - 2, groups - 1):
                for i in range(GRP):
                    sp.wait_ge(xo_ok, 2 + GRP * g + i + 1)
                    store(g * GRP + i, i)
            for i in range(GRP):
                sp.wait_ge(stored[i], 16 * (groups + 1))

        @block.tensor
        def _(pe):
            def turn(g, ga):
                def xw(i):
                    pe.wait_ge(x_loaded[i], 16 * (ga + 1))
                    pe.wait_ge(xw_lo_ok, GRP * ga + i + 1)
                    for c in range(CH):
                        mm = nc.tensor.matmul(xw_ps[i % 2][:, c * P:(c + 1) * P], xin[:, i, c * P:(c + 1) * P],
                                              s.adj[:], start=True, stop=True)
                    mm.then_inc(xw_made, 1)

                def l2(i):
                    pe.wait_ge(xw_hi_ok, GRP * ga + i + 1)
                    pe.wait_ge(xw_lo_ok, 2 + GRP * ga + i + 1)
                    if not first(ga) or i >= 2:
                        pe.wait_ge(ya_ok, GRP * ga + i - 1)
                    xwp, anp = (xw_hi, xw_lo), (s.an_hi, s.an_lo)
                    for c in range(CH):
                        for n, (a, b) in enumerate(HILO):
                            mm = nc.tensor.matmul(l2_ps[i % 2][:], xwp[a][:, i % 2, c * P:(c + 1) * P], anp[b][:, c, :],
                                                  start=(c == 0 and n == 0), stop=(c == CH - 1 and n == 2))
                    mm.then_inc(l2_made, 1)

                def l3(i):
                    pe.wait_ge(x_hi_ok, GRP * g + i + 1)
                    pe.wait_ge(x_lo_ok, GRP * g + i + 1)
                    pe.wait_ge(yb_ok, GRP * g + i + 1)
                    wp, xp = (s.adj2_hi, s.adj2_lo), (x_hi, x_lo)
                    for n, (a, b) in enumerate(HILO):
                        mm = nc.tensor.matmul(l3_ps[i % 2][:], wp[a][:], xp[b][:, i, :], start=(n == 0), stop=(n == 2))
                    mm.then_inc(l3_made, 1)

                if ga is not None:
                    xw(0)
                for i in range(GRP):
                    if ga is not None and i + 1 < GRP:
                        xw(i + 1)
                    if g is not None:
                        l3(i)
                    if ga is not None:
                        l2(i)

            turns(pe, turn)

        @block.scalar
        def _(act):
            def turn(g, ga):
                def xw_hi_(i):
                    act.wait_ge(xw_made, GRP * ga + i + 1)
                    act.wait_ge(l2_made, GRP * ga + i + 1)
                    nc.scalar.activation(xw_hi[:, i % 2, :], xw_ps[i % 2][:], ACT.Copy).then_inc(xw_hi_ok, 1)

                def norm_a(ga, i):
                    j = slice(i % 2, i % 2 + 1)
                    act.wait_ge(rs_a_ok, 2 * (GRP * ga + i + 1))
                    act.wait_ge(xb_ok, 2 + GRP * ga + i + 1)
                    nc.scalar.activation(xa[:, i % 2, :], ya[:, i % 2, :], ACT.Identity, scale=rs_a[:, j],
                                         bias=nb_a[:, j]).then_inc(xa_ok, 1)
                    act.wait_ge(xa_ok, GRP * ga + i + 1)
                    act.wait_ge(l3_made, GRP * ga + i + 1)
                    nc.scalar.activation(x_hi[:, i, :], xa[:, i % 2, :], ACT.Copy).then_inc(x_hi_ok, 1)

                def norm_b(i):
                    j = slice(i % 2, i % 2 + 1)
                    act.wait_ge(rs_b_ok, 2 * (GRP * g + i + 1))
                    act.wait_ge(stored[i], 16 * (g + 1))
                    nc.scalar.activation(xo[:, i, :], yb[:, i % 2, :], ACT.Identity, scale=rs_b[:, j],
                                         bias=nb_b[:, j]).then_inc(xo_ok, 1)

                if ga is not None:
                    xw_hi_(0)
                for i in range(GRP):
                    if ga is not None and i + 1 < GRP:
                        xw_hi_(i + 1)
                    if i:
                        if ga is not None:
                            norm_a(ga, i - 1)
                    elif g is not None:
                        norm_a(g, GRP - 1)
                    if g is not None:
                        norm_b(i)

            act.sem_inc(l2_made, 2)
            act.sem_inc(l3_made, GRP)
            act.sem_inc(xo_ok, 2)
            for i in range(GRP):
                act.sem_inc(stored[i], 16)
            turns(act, turn)

        @block.gpsimd
        def _(pool):
            def turn(g, ga):
                def root(ga, i):
                    j = slice(i % 2, i % 2 + 1)
                    inverse_root(nc, pool, rs_a[:, j], nb_a[:, j], ve_a[:, j], nm_a[:, j],
                                 s.neghalf[:, 0:1], st_a_ok, rs_a_ok, GRP * ga + i + 1)

                def pass_on(ga, i):
                    pool.wait_ge(x_hi_ok, GRP * ga + i + 1)
                    nc.gpsimd.tensor_tensor(x_lo[:, i, :], xa[:, i % 2, :], x_hi[:, i, :].bitcast(F32),
                                            ALU.subtract).then_inc(x_lo_ok, 1)
                    if not first(ga):
                        pool.wait_ge(yb_ok, GRP * ga + i - 1)
                    nc.gpsimd.tensor_tensor(xb[:, i, :], xa[:, i % 2, :], s.b3[:], ALU.add).then_inc(xb_ok, 1)

                for i in range(GRP):
                    before = (ga, i - 1) if i else (g, GRP - 1)
                    j = slice(i % 2, i % 2 + 1)
                    if before[0] is not None:
                        root(*before)
                    if g is not None:
                        inverse_root(nc, pool, rs_b[:, j], nb_b[:, j], ve_b[:, j], nm_b[:, j],
                                     s.neghalf[:, 0:1], st_b_ok, rs_b_ok, GRP * g + i + 1)
                    if before[0] is not None:
                        pass_on(*before)

            pool.sem_inc(xb_ok, 4)
            turns(pool, turn)

        @block.vector
        def _(dve):
            def turn(g, ga):
                def xw_lo_(i):
                    dve.wait_ge(xw_hi_ok, GRP * ga + i + 1)
                    nc.vector.tensor_tensor(xw_lo[:, i % 2, :], xw_ps[i % 2][:], xw_hi[:, i % 2, :].bitcast(F32),
                                            ALU.subtract).then_inc(xw_lo_ok, 1)

                def residual_a(i):
                    j = slice(i % 2, i % 2 + 1)
                    dve.wait_ge(l2_made, 2 + GRP * ga + i + 1)
                    if not first(ga) or i >= 2:
                        dve.wait_ge(xa_ok, GRP * ga + i - 1)
                    nc.vector.scalar_tensor_tensor(out=ya[:, i % 2, :], in0=l2_ps[i % 2][:], scalar=s.b2[:, 0:1],
                                                   in1=xin[:, i, :], op0=ALU.add, op1=ALU.add).then_inc(ya_ok, 1)
                    statistics(nc, dve, ya[:, i % 2, :], st_a[:, i % 2, :], mv_a[:, i % 2, :], ve_a[:, j], nm_a[:, j],
                               ya_ok, st_a_ok, GRP * ga + i + 1, passed)

                def residual_b(i):
                    j = slice(i % 2, i % 2 + 1)
                    dve.wait_ge(l3_made, GRP + GRP * g + i + 1)
                    dve.wait_ge(xb_ok, 4 + GRP * g + i + 1)
                    dve.wait_ge(xo_ok, GRP * g + i + 1)
                    nc.vector.tensor_tensor(yb[:, i % 2, :], l3_ps[i % 2][:], xb[:, i, :], ALU.add).then_inc(yb_ok, 1)
                    dve.wait_ge(yb_ok, 2 + GRP * g + i + 1)
                    statistics(nc, dve, yb[:, i % 2, :], st_b[:, i % 2, :], mv_b[:, i % 2, :], ve_b[:, j], nm_b[:, j],
                               yb_ok, st_b_ok, GRP * g + i + 1, passed)

                if ga is not None:
                    xw_lo_(0)
                for i in range(GRP):
                    if ga is not None and i + 1 < GRP:
                        xw_lo_(i + 1)
                    if g is not None:
                        residual_b(i)
                    if ga is not None:
                        residual_a(i)

            dve.sem_inc(xw_lo_ok, 2)
            dve.sem_inc(yb_ok, 2)
            turns(dve, turn)


def adj_resnorm_kernel(nc, x, adj, bias0, w_lang, w_grav, w_v, w_o, gate, log_sigma, bias2, bias3, out):
    nb = x.shape[0]
    assert x.shape[1:] == (P, N) and nb % SGRP == 0 and nb <= P
    between = nc.dram_tensor("between", [nb, P, N], F32, kind="Internal").ap()
    spill_hi = nc.dram_tensor("spill_hi", [nb, N], F32, kind="Internal").ap()
    spill_lo = nc.dram_tensor("spill_lo", [nb, N], F32, kind="Internal").ap()
    s = Shared()
    s.nb = nb
    with ExitStack() as ctx:
        constants(nc, ctx, s, adj, bias0, bias2, bias3, gate, log_sigma)
        n2 = ctx.enter_context(nc.sbuf_tensor("n2", [P, CH, nb + GRP], F32))


        def adjacency(squares, source, before_choice):
            with ExitStack() as psum_room, ExitStack() as choice_room:
                _, ps, _ = scope(nc, psum_room)
                hh, hl = [ps(f"hh{k}") for k in range(3)], [ps(f"hl{k}") for k in range(CH)]
                with ExitStack() as x_room:
                    sb, _, _ = scope(nc, x_room)
                    xres, rows = sb("xres", [P, nb, N]), sb("rows", [2 * SGRP, nb // SGRP, N], F32R)
                    if source is None:
                        first_norms(nc, s, x, xres, squares)
                    norm_rows(nc, s, squares, rows, spill_hi, spill_lo)
                    similarity(nc, s, xres, rows, hh, hl, source)
                weights = before_choice()
                sb, _, _ = scope(nc, choice_room)
                sim, work = sb("sim", [P, CH, N]), sb("work", [P, CH, 8 + N])
                whole_similarity(nc, s, hh, hl, sim, work)
                psum_room.close()
                choose(nc, s, work, weights)
                normal_adjacency(nc, s, sim, work)

        with ExitStack() as weight_room:
            sb, _, _ = scope(nc, weight_room)
            dst = {}

            def weights():
                for k in ("lang", "grav"):
                    dst[k] = [sb(f"u_{k}_{p}", [P, TRI_W], F32R) for p in ("hi", "lo")]
                dst["ov"] = [sb(f"wov_{p}", [P, CH, N], F32R) for p in ("hi", "lo")]
                return {"lang": w_lang, "grav": w_grav, "v": w_v, "o": w_o}, dst

            adjacency(n2[:, :, 0:nb], None, weights)
            gnn_layer_pair(nc, s, x, between, dst["lang"], dst["grav"], dst["ov"], n2)
        adjacency(n2[:, :, GRP:GRP + nb], between, lambda: None)
        last_layers(nc, s, between, out)


_INS = ["x", "adj", "L0_gnn_bias", "L1_gnn_W_lang", "L1_gnn_W_grav", "L1_gnn_W_V", "L1_gnn_W_O",
        "L1_gnn_gate_logit", "L1_gnn_log_sigma", "L2_gnn_bias", "L3_gnn_bias"]


def kernel(**inputs):
    import concourse.bacc as _bacc
    from concourse.bass_utils import run_bass_kernel_spmd as _run

    nc = _bacc.Bacc("TRN2", target_bir_lowering=False, num_devices=1)
    arrays, args = {}, []
    for name in _INS:
        a = np.ascontiguousarray(inputs[name])
        if a.ndim == 0:
            a = a.reshape(1, 1)
        arrays[f"in_{name}"] = a
        args.append(nc.dram_tensor(f"in_{name}", a.shape, mybir.dt.from_np(a.dtype), kind="ExternalInput").ap())
    shape = inputs["x"].shape
    out = nc.dram_tensor("out_0", shape, F32, kind="ExternalOutput").ap()
    adj_resnorm_kernel(nc, *args, out)
    r = _run(nc, [arrays], core_ids=[0])
    return r.results[0]["out_0"]
```

```python
from contextlib import ExitStack
from itertools import count

import numpy as np

import concourse.bass as bass
from concourse import mybir

F32 = mybir.dt.float32
F32R = mybir.dt.float32r
ALU = mybir.AluOpType
ACT = mybir.ActivationFunctionType
AX = mybir.AxisListType

P = 128
N = 512
CH = N // P
GRP = 4
SGRP = 8
TOP = max(int(N * 0.3), 1)
LN_EPS = 1e-5
NORM_EPS = 1e-12
EPS = 1e-8
NEVER = -2.0 ** 126
CHOSEN = -2.0 ** 127
TRI = [0, 512, 896, 1152]
TRI_W = 1280

SERIAL = count()



def own_step(eng, passed):
    eng.sem_inc(passed, 1)


class Shared:
    pass


def scope(nc, ctx):
    own = lambda name: f"{name}_{next(SERIAL)}"
    sb = lambda name, shape, dt=F32: ctx.enter_context(nc.sbuf_tensor(own(name), shape, dt))
    ps = lambda name, shape=(P, 512): ctx.enter_context(nc.psum_tensor(own(name), list(shape), F32))
    taken = []

    def sem(name):
        taken.append(nc.alloc_semaphore(own(name)))
        return taken[-1]

    def give_back():
        if taken:
            nc.clear_and_free_semaphores(taken)
            nc.all_engine_barrier()

    ctx.callback(give_back)
    return sb, ps, sem


def over(ap, n):
    return ap.unsqueeze(1).broadcast_to([P, n, ap.shape[1]])


def along(ap, m):
    return ap.unsqueeze(2).broadcast_to([P, ap.shape[1], m])


def constants(nc, ctx, s, adj, bias0, bias2, bias3, gate, log_sigma):
    sb, _, _ = scope(nc, ctx)
    s.ident, s.ones, s.negones = sb("ident", [P, P]), sb("ones", [P, P]), sb("negones", [P, P])
    s.zeros_r = sb("zeros_r", [P, N], F32R)
    s.sel = sb("sel", [2 * SGRP, SGRP, P], F32R)
    s.pick = sb("pick", [P, SGRP, SGRP])
    s.neghalf = sb("neghalf", [P, GRP])
    s.adj, s.adj_ne = sb("adj_sb", [P, P]), sb("adj_ne", [P, P])
    s.adj2, s.adj2_hi, s.adj2_lo = sb("adj2", [P, P]), sb("adj2_hi", [P, P], F32R), sb("adj2_lo", [P, P], F32R)
    s.b0, s.b2, s.b3 = sb("b0", [P, 1]), sb("b2", [P, 1]), sb("b3", [P, N])
    s.w_l, s.w_g, s.inv_s2 = sb("w_l", [P, 1]), sb("w_g", [P, 1]), sb("inv_s2", [P, 1])
    s.an_hi, s.an_lo = sb("an_hi", [P, CH, N], F32R), sb("an_lo", [P, CH, N], F32R)
    with ExitStack() as c2:
        sb, _, sem = scope(nc, c2)
        sel_a, sel_b = sb("sel_a", [2 * SGRP, SGRP, P]), sb("sel_b", [2 * SGRP, SGRP, P])
        gate_sb, lsig_sb, egate = sb("gate_sb", [P, 1]), sb("lsig_sb", [P, 1]), sb("egate", [P, 2])
        loaded, filled, shaped = sem("c_loaded"), sem("c_filled"), sem("c_shaped")
        act_done, dve_done = sem("c_act_done"), sem("c_dve_done")
        block = c2.enter_context(nc.Block())

        @block.sync
        def _(sp):
            sp.dma_start(s.adj[:], adj).then_inc(loaded, 16)
            sp.dma_start(s.b0[:], bias0.rearrange("(p a) -> p a", a=1)).then_inc(loaded, 16)
            sp.dma_start(s.b2[:], bias2.rearrange("(p a) -> p a", a=1)).then_inc(loaded, 16)
            sp.dma_start(s.b3[:], bias3.rearrange("(a n) -> a n", a=1).broadcast_to([P, N])).then_inc(loaded, 16)
            sp.dma_start(gate_sb[:], gate.broadcast_to([P, 1])).then_inc(loaded, 16)
            sp.dma_start(lsig_sb[:], log_sigma.broadcast_to([P, 1])).then_inc(loaded, 16)

        @block.gpsimd
        def _(pool):
            nc.gpsimd.memset(s.ident[:], 0.0).then_inc(filled, 1)
            nc.gpsimd.memset(s.ones[:], 1.0).then_inc(filled, 1)
            nc.gpsimd.memset(s.negones[:], -1.0).then_inc(filled, 1)
            nc.gpsimd.memset(s.neghalf[:], -0.5).then_inc(filled, 1)
            nc.gpsimd.memset(sel_a[:], 0.0).then_inc(filled, 1)
            nc.gpsimd.memset(sel_b[:], 0.0).then_inc(filled, 1)
            nc.gpsimd.memset(s.pick[:], 0.0).then_inc(filled, 1)
            pool.wait_ge(filled, 7)
            nc.gpsimd.affine_select(out=s.pick[:], in_=s.pick[:], compare_op=ALU.not_equal, fill=1.0,
                                    base=0, pattern=[[1, SGRP], [-1, SGRP]], channel_multiplier=0).then_inc(shaped, 1)
            nc.gpsimd.affine_select(out=s.ident[:], in_=s.ident[:], compare_op=ALU.not_equal, fill=1.0,
                                    base=0, pattern=[[-1, P]], channel_multiplier=1).then_inc(shaped, 1)
            for part, base in ((sel_a, 0), (sel_b, -SGRP)):
                nc.gpsimd.affine_select(out=part[:], in_=part[:], compare_op=ALU.not_equal, fill=1.0,
                                        base=base, pattern=[[-1, SGRP], [0, P]],
                                        channel_multiplier=1).then_inc(shaped, 1)

        @block.scalar
        def _(act):
            act.wait_ge(loaded, 96)
            nc.scalar.activation(egate[:, 0:1], gate_sb[:], ACT.Exp, scale=-1.0).then_inc(act_done, 1)
            nc.scalar.activation(s.inv_s2[:], lsig_sb[:], ACT.Exp, scale=-2.0).then_inc(act_done, 1)

        @block.vector
        def _(dve):
            nc.vector.memset(s.zeros_r[:].bitcast(F32), 0.0)
            dve.wait_ge(shaped, 4)
            nc.vector.tensor_tensor(s.sel[:], sel_a[:], sel_b[:], ALU.add)
            dve.wait_ge(loaded, 96)
            nc.vector.scalar_tensor_tensor(out=s.adj_ne[:], in0=s.ident[:], scalar=-1.0, in1=s.ones[:],
                                           op0=ALU.mult, op1=ALU.add).then_inc(dve_done, 1)
            nc.vector.tensor_tensor(s.adj2[:], s.adj[:], s.adj[:], ALU.mult).then_inc(dve_done, 1)
            dve.wait_ge(dve_done, 2)
            nc.vector.tensor_tensor(s.adj_ne[:], s.adj_ne[:], s.adj[:], ALU.mult)
            nc.vector.tensor_copy(s.adj2_hi[:], s.adj2[:]).then_inc(dve_done, 1)
            dve.wait_ge(dve_done, 3)
            nc.vector.tensor_tensor(s.adj2_lo[:], s.adj2[:], s.adj2_hi[:].bitcast(F32), ALU.subtract)
            dve.wait_ge(act_done, 2)
            nc.vector.tensor_scalar(egate[:, 1:2], egate[:, 0:1], 1.0, None, ALU.add).then_inc(dve_done, 1)
            dve.wait_ge(dve_done, 4)
            nc.vector.reciprocal(s.w_l[:], egate[:, 1:2]).then_inc(dve_done, 1)
            dve.wait_ge(dve_done, 5)
            nc.vector.tensor_scalar(s.w_g[:], s.w_l[:], -1.0, 1.0, ALU.mult, ALU.add)


def first_norms(nc, s, x, xres, n2):
    nb = x.shape[0]
    with ExitStack() as ctx:
        sb, ps, sem = scope(nc, ctx)
        sq = sb("sq", [P, 4, N])
        kept = sb("kept", [SGRP, nb // SGRP, N])
        sums = [ps(f"sums{k}") for k in range(2)]
        loaded = [sem(f"x_loaded{k}") for k in range(4)]
        squared, used, summed = sem("squared"), sem("used"), sem("summed")
        out, stored, passed = sem("out"), sem("stored"), sem("passed")
        xv = x.rearrange("b l n -> l b n")
        block = ctx.enter_context(nc.Block())
        turns = nb // SGRP

        @block.sync
        def _(sp):
            with sp.Fori(0, turns) as t:
                for k in range(4):
                    pair = sp.snap(8 * t + 2 * k)
                    sp.wait_ge(squared, 8 * t + 2 * k + 2)
                    sp.dma_start(xres[:, bass.ds(pair, 2), :], xv[:, bass.ds(pair, 2), :]).then_inc(loaded[k], 16)
            sp.wait_ge(out, 2 + turns)
            sp.dma_start(n2.rearrange("(g j) n -> j g n", j=SGRP), kept[:]).then_inc(stored, 16)
            sp.wait_ge(stored, 16)

        def pairs_of_turns(eng, turn):
            with eng.Fori(0, turns // 2) as h:
                turn(2 * h, 0)
                turn(2 * h + 1, 1)
            if turns % 2:
                turn(turns - 1, 0)

        @block.scalar
        def _(act):
            def turn(t, bank):
                for k in range(SGRP):
                    if k % 2 == 0:
                        act.wait_ge(loaded[k // 2], 16 * (t + 1))
                    act.wait_ge(used, 8 * t + k + 1)
                    nc.scalar.activation(sq[:, k % 4, :], xres[:, bass.ds(8 * t + k, 1), :].rearrange("p a n -> p (a n)"),
                                         ACT.Square).then_inc(squared, 1)

            act.sem_inc(squared, 8)
            pairs_of_turns(act, turn)

        @block.tensor
        def _(pe):
            def turn(t, bank):
                pe.wait_ge(out, t + 1)
                for k in range(SGRP):
                    pe.wait_ge(squared, 8 + 8 * t + k + 1)
                    mm = nc.tensor.matmul(sums[bank][0:SGRP, :], s.pick[:, k, :], sq[:, k % 4, :],
                                          start=(k == 0), stop=(k == SGRP - 1))
                    if k == SGRP - 1:
                        mm.then_inc(summed, 1)
                        pe.wait_ge(summed, t + 1)
                        pe.sem_inc(used, 1)
                    else:
                        mm.then_inc(used, 1)

            pe.sem_inc(used, 4)
            pairs_of_turns(pe, turn)

        @block.vector
        def _(dve):
            def turn(t, bank):
                dve.wait_ge(summed, t + 1)
                nc.vector.tensor_copy(kept[:, bass.ds(t, 1), :].rearrange("p a n -> p (a n)"),
                                      sums[bank][0:SGRP, :]).then_inc(out, 1)

            dve.sem_inc(out, 2)
            pairs_of_turns(dve, turn)


def norm_rows(nc, s, n2, rows, spill_hi, spill_lo):
    nb = n2.shape[0]
    w = nb * N // P
    flat = lambda dram: dram.rearrange("b n -> (b n)").rearrange("(p w) -> p w", w=w)
    with ExitStack() as ctx:
        sb, ps, sem = scope(nc, ctx)
        nrm, inv = sb("nrm", [P, w]), sb("inv", [P, w])
        r_hi, r_lo = sb("r_hi", [P, w], F32R), sb("r_lo", [P, w], F32R)
        loaded, rooted, dve_done, spilt, back = (sem(x) for x in ("n_loaded", "rooted", "r_dve", "spilt", "back"))
        block = ctx.enter_context(nc.Block())

        @block.scalar
        def _(act):
            act.wait_ge(loaded, 16)
            nc.scalar.activation(nrm[:], nrm[:], ACT.Sqrt).then_inc(rooted, 1)

        @block.vector
        def _(dve):
            dve.wait_ge(rooted, 1)
            nc.vector.tensor_scalar(nrm[:], nrm[:], NORM_EPS, None, ALU.max).then_inc(dve_done, 1)
            dve.wait_ge(dve_done, 1)
            nc.vector.reciprocal(inv[:], nrm[:]).then_inc(dve_done, 1)
            dve.wait_ge(dve_done, 2)
            nc.vector.tensor_copy(r_hi[:], inv[:]).then_inc(dve_done, 1)
            dve.wait_ge(dve_done, 3)
            nc.vector.tensor_tensor(r_lo[:], inv[:], r_hi[:].bitcast(F32), ALU.subtract).then_inc(dve_done, 1)

        @block.sync
        def _(sp):
            sp.dma_start(nrm[:], flat(n2)).then_inc(loaded, 16)
            sp.wait_ge(dve_done, 4)
            sp.dma_start(flat(spill_hi), r_hi[:].bitcast(F32)).then_inc(spilt, 16)
            sp.dma_start(flat(spill_lo), r_lo[:].bitcast(F32)).then_inc(spilt, 16)
            sp.wait_ge(spilt, 32)
            for k, spill in enumerate((spill_hi, spill_lo)):
                sp.dma_start(rows[k * SGRP:(k + 1) * SGRP].bitcast(F32),
                             spill.rearrange("(g j) n -> j g n", j=SGRP)).then_inc(back, 16)
            sp.wait_ge(back, 32)


def similarity(nc, s, xres, rows, hh, hl, source):
    nb = xres.shape[1]
    hh_at = [hh[0][:, 0:512], hh[1][:, 0:384], hh[2][:, 0:256], hh[1][:, 384:512]]
    with ExitStack() as ctx:
        sb, ps, sem = scope(nc, ctx)
        xn, hi, lo = sb("xn", [P, 4, N]), sb("xn_hi", [P, 4, N], F32R), sb("xn_lo", [P, 4, N], F32R)
        scale = ps("scale")
        loaded = [sem(f"x_loaded{k}") for k in range(4)]
        scale_ready, normed, hi_ready, lo_ready = (sem(x) for x in ("scale_ready", "normed", "hi_ready", "lo_ready"))
        summed = sem("summed")
        passed = sem("passed")
        block = ctx.enter_context(nc.Block())

        if source is not None:
            sv = source.rearrange("b l n -> l b n")

            @block.sync
            def _(sp):
                with sp.Fori(0, nb // 8) as t:
                    for k in range(4):
                        pair = sp.snap(8 * t + 2 * k)
                        sp.wait_ge(normed, 8 * t + 2 * k + 2)
                        sp.dma_start(xres[:, bass.ds(pair, 2), :], sv[:, bass.ds(pair, 2), :]).then_inc(loaded[k], 16)

        @block.vector
        def _(dve):
            dve.sem_inc(normed, 8)
            with dve.Fori(0, nb // SGRP) as t:
                for k in range(SGRP):
                    if source is not None and k % 2 == 0:
                        dve.wait_ge(loaded[k // 2], 16 * (t + 1))
                    dve.wait_ge(scale_ready, 8 * t + k + 1)
                    dve.wait_ge(summed, 8 * t + k + 1)
                    nc.vector.tensor_tensor(xn[:, k % 4, :],
                                            xres[:, bass.ds(8 * t + k, 1), :].rearrange("p a n -> p (a n)"),
                                            scale[:], ALU.mult).then_inc(normed, 1)

        @block.scalar
        def _(act):
            with act.Fori(0, nb // SGRP) as t:
                for k in range(SGRP):
                    act.wait_ge(normed, 8 + 8 * t + k + 1)
                    nc.scalar.activation(hi[:, k % 4, :], xn[:, k % 4, :], ACT.Copy).then_inc(hi_ready, 1)

        @block.gpsimd
        def _(pool):
            with pool.Fori(0, nb // SGRP) as t:
                for k in range(SGRP):
                    pool.wait_ge(hi_ready, 8 * t + k + 1)
                    nc.gpsimd.tensor_tensor(lo[:, k % 4, :], xn[:, k % 4, :], hi[:, k % 4, :].bitcast(F32),
                                            ALU.subtract).then_inc(lo_ready, 1)

        @block.tensor
        def _(pe):
            def spread(t, k):
                pe.wait_ge(normed, 8 + 8 * t + k)
                own_step(pe, passed)
                g = t + k // SGRP if k >= SGRP else t
                nc.tensor.matmul(scale[:], s.sel[:, k % SGRP, :], rows[:, bass.ds(g, 1), :].rearrange("p a n -> p (a n)"),
                                 start=True, stop=True).then_inc(scale_ready, 1)

            def sums(t, k):
                pe.wait_ge(hi_ready, 8 * t + k + 1)
                h, l = hi[:, k % 4, :], lo[:, k % 4, :]
                for c in range(CH):
                    nc.tensor.matmul(hh_at[c], h[:, c * P:(c + 1) * P], h[:, c * P:N], start=False, stop=False,
                                     skip_group_check=True)
                pe.wait_ge(lo_ready, 8 * t + k + 1)
                for c in range(CH):
                    mm = nc.tensor.matmul(hl[c][:], h[:, c * P:(c + 1) * P], l, start=False, stop=False,
                                          skip_group_check=True)
                mm.then_inc(summed, 1)

            pe.sem_inc(summed, 4)
            for bank in (*hh, *hl):
                nc.tensor.matmul(bank[:], s.zeros_r[:, 0:P], s.zeros_r[:], start=True, stop=False,
                                 skip_group_check=True)
            spread(0, 0)
            spread(0, 1)
            turns = nb // SGRP
            with pe.Fori(0, turns - 1) as t:
                for k in range(SGRP):
                    spread(t, k + 2)
                    sums(t, k)
            for k in range(SGRP):
                if k + 2 < SGRP:
                    spread(turns - 1, k + 2)
                sums(turns - 1, k)


def whole_similarity(nc, s, hh, hl, sim, work):
    nb = s.nb
    hh_at = [hh[0][:, 0:512], hh[1][:, 0:384], hh[2][:, 0:256], hh[1][:, 384:512]]
    with ExitStack() as ctx:
        sb, ps, sem = scope(nc, ctx)
        hl_sb, part = sb("hl_sb", [P, CH, N]), sb("part", [P, CH, N])
        turn = ps("turn")
        hl_out, parted, turned, upper, low_turned, lower = (
            sem(x) for x in ("hl_out", "parted", "turned", "upper", "low_turned", "lower"))
        masked, padded = sem("masked"), sem("padded")
        block = ctx.enter_context(nc.Block())

        @block.scalar
        def _(act):
            for c in range(CH):
                nc.scalar.activation(hl_sb[:, c, :], hl[c][:], ACT.Copy, scale=1.0 / nb).then_inc(hl_out, 1)
            for c in range(1, CH):
                act.wait_ge(low_turned, c)
                nc.scalar.activation(sim[:, c, 0:c * P], turn[:, 0:c * P], ACT.Copy).then_inc(lower, 1)

        @block.tensor
        def _(pe):
            pe.wait_ge(hl_out, CH)
            for c in range(CH):
                if c:
                    pe.wait_ge(upper, c)
                for j in range(c, CH):
                    mm = nc.tensor.transpose(turn[:, j * P:(j + 1) * P], hl_sb[:, j, c * P:(c + 1) * P], s.ident[:])
                mm.then_inc(turned, 1)
            pe.wait_ge(upper, CH)
            for c in range(1, CH):
                if c > 1:
                    pe.wait_ge(lower, c - 1)
                for j in range(c):
                    mm = nc.tensor.transpose(turn[:, j * P:(j + 1) * P], sim[:, j, c * P:(c + 1) * P], s.ident[:])
                mm.then_inc(low_turned, 1)

        @block.vector
        def _(dve):
            nc.vector.memset(work[:, :, 0:8], NEVER).then_inc(padded, 1)
            for c in range(CH):
                dve.wait_ge(hl_out, c + 1)
                nc.vector.scalar_tensor_tensor(out=part[:, c, c * P:N], in0=hh_at[c], scalar=1.0 / nb,
                                               in1=hl_sb[:, c, c * P:N], op0=ALU.mult,
                                               op1=ALU.add).then_inc(parted, 1)
            for c in range(CH):
                dve.wait_ge(turned, c + 1)
                dve.wait_ge(parted, c + 1)
                nc.vector.tensor_tensor(sim[:, c, c * P:N], turn[:, c * P:N], part[:, c, c * P:N],
                                        ALU.add).then_inc(upper, 1)
            dve.wait_ge(upper, CH)
            dve.wait_ge(lower, CH - 1)
            for c in range(CH):
                nc.vector.tensor_copy(work[:, c, 8:8 + N], sim[:, c, :]).then_inc(masked, 1)
            for c in range(CH):
                dve.wait_ge(masked, c + 1)
                nc.vector.scalar_tensor_tensor(out=work[:, c, 8 + c * P:8 + (c + 1) * P], in0=s.ident[:],
                                               scalar=NEVER, in1=sim[:, c, c * P:(c + 1) * P],
                                               op0=ALU.mult, op1=ALU.add)


def choose(nc, s, work, weights):
    rounds, rest = TOP // 8, TOP % 8
    with ExitStack() as ctx:
        sb, ps, sem = scope(nc, ctx)
        best = sb("best", [P, CH, 8])
        found, marked, passed = sem("found"), sem("marked"), sem("passed")
        if weights is not None:
            w_dram, dst = weights
            raw = {k: sb(f"raw_{k}", [P, CH, N]) for k in w_dram}
            wo_t = sb("wo_t", [P, CH, N])
            tmp = sb("tmp", [P, 2, N])
            banks = [ps(f"prep{k}") for k in range(2)]
            w_loaded, made, out, hi_ready, lo_ready = (
                sem(x) for x in ("w_loaded", "made", "out", "w_hi_ready", "w_lo_ready"))
        block = ctx.enter_context(nc.Block())

        @block.vector
        def _(dve):
            def mark(c):
                nc.vector.match_replace(work[:, c, :], best[:, c, :], work[:, c, :], CHOSEN).then_inc(marked, 1)

            dve.sem_inc(marked, CH)
            with dve.Fori(0, rounds) as r:
                for c in range(CH):
                    dve.wait_ge(marked, CH * r + c + 1)
                    own_step(dve, passed)
                    nc.vector.max(best[:, c, :], work[:, c, :]).then_inc(found, 1)
                for c in range(CH):
                    dve.wait_ge(found, CH * r + c + 1)
                    own_step(dve, passed)
                    mark(c)
            if rest:
                for c in range(CH):
                    dve.wait_ge(marked, CH * rounds + c + 1)
                    nc.vector.max(best[:, c, :], work[:, c, :]).then_inc(found, 1)
                dve.wait_ge(found, CH * (rounds + 1))
                nc.vector.memset(best[:, :, rest:8], NEVER).then_inc(found, 1)
                dve.wait_ge(found, CH * (rounds + 1) + 1)
                for c in range(CH):
                    mark(c)

        if weights is None:
            return

        jobs = [("turn", None, c) for c in range(CH)]
        jobs += [(name, name, c) for name in ("lang", "grav") for c in range(CH)]
        jobs += [("ov", "ov", c) for c in range(CH)]

        @block.sync
        def _(sp):
            for k in w_dram:
                sp.dma_start(raw[k][:], w_dram[k].rearrange("(c p) n -> p c n", p=P)).then_inc(w_loaded, 16)

        @block.tensor
        def _(pe):
            pe.wait_ge(w_loaded, 16 * len(w_dram))
            for n, (kind, _, c) in enumerate(jobs):
                bank = banks[n % 2]
                if n >= 2:
                    pe.wait_ge(out, n - 1)
                if kind == "turn":
                    for j in range(CH):
                        mm = nc.tensor.transpose(bank[:, j * P:(j + 1) * P], raw["o"][:, j, c * P:(c + 1) * P], s.ident[:])
                elif kind == "ov":
                    for j in range(CH):
                        mm = nc.tensor.matmul(bank[:], raw["v"][:, j, c * P:(c + 1) * P], wo_t[:, j, :],
                                              start=(j == 0), stop=(j == CH - 1))
                else:
                    for j in range(CH):
                        mm = nc.tensor.matmul(bank[:, 0:N - c * P], raw[kind][:, j, c * P:(c + 1) * P],
                                              raw[kind][:, j, c * P:N], start=(j == 0), stop=(j == CH - 1))
                mm.then_inc(made, 1)

        @block.scalar
        def _(act):
            k = 0
            for n, (kind, name, c) in enumerate(jobs):
                bank = banks[n % 2]
                act.wait_ge(made, n + 1)
                if kind == "turn":
                    nc.scalar.activation(wo_t[:, c, :], bank[:], ACT.Copy).then_inc(out, 1)
                    continue
                w = N - c * P if name != "ov" else N
                if k >= 2:
                    act.wait_ge(lo_ready, k - 1)
                if name == "ov":
                    nc.scalar.activation(tmp[:, k % 2, :], bank[:], ACT.Copy).then_inc(out, 1)
                    d = dst[name][0][:, c, :]
                else:
                    if w > P:
                        nc.scalar.activation(tmp[:, k % 2, P:w], bank[:, P:w], ACT.Copy)
                    nc.scalar.activation(tmp[:, k % 2, 0:P], bank[:, 0:P], ACT.Copy, scale=0.5).then_inc(out, 1)
                    d = dst[name][0][:, TRI[c]:TRI[c] + w]
                act.wait_ge(out, n + 1)
                nc.scalar.activation(d, tmp[:, k % 2, 0:w], ACT.Copy).then_inc(hi_ready, 1)
                k += 1

        @block.gpsimd
        def _(pool):
            k = 0
            for kind, name, c in jobs:
                if kind == "turn":
                    continue
                w = N - c * P if name != "ov" else N
                d = [x[:, c, :] if name == "ov" else x[:, TRI[c]:TRI[c] + w] for x in dst[name]]
                pool.wait_ge(hi_ready, k + 1)
                nc.gpsimd.tensor_tensor(d[1], tmp[:, k % 2, 0:w], d[0].bitcast(F32),
                                        ALU.subtract).then_inc(lo_ready, 1)
                k += 1


def normal_adjacency(nc, s, sim, work):
    with ExitStack() as ctx:
        sb, ps, sem = scope(nc, ctx)
        a, an, diag = sb("a", [P, CH, N]), sb("an", [P, CH, N]), sb("diag", [P, CH, P])
        deg, pos, dinv = sb("deg", [P, CH]), sb("pos", [P, CH]), sb("dinv", [P, CH])
        deg_ps, row = ps("deg_ps", [P, CH]), ps("row")
        chosen, summed, dve_done, rooted, spread, hi_ready = (
            sem(x) for x in ("chosen", "deg_summed", "n_dve", "n_rooted", "spread", "n_hi"))
        block = ctx.enter_context(nc.Block())

        @block.vector
        def _(dve):
            for c in range(CH):
                nc.vector.scalar_tensor_tensor(out=a[:, c, :], in0=work[:, c, 8:8 + N], scalar=CHOSEN,
                                               in1=sim[:, c, :], op0=ALU.is_equal,
                                               op1=ALU.mult).then_inc(chosen, 1)
            dve.wait_ge(summed, 1)
            nc.vector.tensor_scalar(deg[:], deg_ps[:], 1e-37, None, ALU.max).then_inc(dve_done, 1)
            nc.vector.tensor_scalar(pos[:], deg_ps[:], 0.0, None, ALU.is_gt).then_inc(dve_done, 1)
            dve.wait_ge(dve_done, 2)
            dve.wait_ge(rooted, 1)
            nc.vector.tensor_tensor(dinv[:], dinv[:], pos[:], ALU.mult).then_inc(dve_done, 1)
            dve.wait_ge(dve_done, 3)
            nc.vector.tensor_tensor(diag[:], over(s.ident[:], CH), along(dinv[:], P), ALU.mult).then_inc(dve_done, 1)
            dve.wait_ge(spread, 1)
            for c in range(CH):
                nc.vector.scalar_tensor_tensor(out=an[:, c, :], in0=a[:, c, :], scalar=dinv[:, c:c + 1],
                                               in1=row[:], op0=ALU.mult, op1=ALU.mult).then_inc(dve_done, 1)
            for c in range(CH):
                dve.wait_ge(hi_ready, c + 1)
                nc.vector.tensor_tensor(s.an_lo[:, c, :], an[:, c, :], s.an_hi[:, c, :].bitcast(F32), ALU.subtract)

        @block.gpsimd
        def _(pool):
            pool.wait_ge(dve_done, 2)
            nc.gpsimd.tensor_tensor(dinv[:], deg[:], s.neghalf[:], ALU.pow).then_inc(rooted, 1)

        @block.tensor
        def _(pe):
            pe.wait_ge(chosen, CH)
            for j in range(CH):
                for c in range(CH):
                    mm = nc.tensor.matmul(deg_ps[:, j:j + 1], a[:, c, j * P:(j + 1) * P], s.ones[:, 0:1],
                                          start=(c == 0), stop=(c == CH - 1))
            mm.then_inc(summed, 1)
            pe.wait_ge(dve_done, 4)
            nc.tensor.matmul(row[:], s.ones[:], diag[:].rearrange("p c n -> p (c n)"),
                             start=True, stop=True).then_inc(spread, 1)

        @block.scalar
        def _(act):
            for c in range(CH):
                act.wait_ge(dve_done, 5 + c)
                nc.scalar.activation(s.an_hi[:, c, :], an[:, c, :], ACT.Copy).then_inc(hi_ready, 1)


def first(g):
    return isinstance(g, int) and g == 0


def statistics(nc, dve, y, stats, mean_var, var_eps, neg_mean, y_ok, stats_ok, n, passed):
    dve.wait_ge(y_ok, n)
    nc.vector.bn_stats(stats, y).then_inc(stats_ok, 1)
    dve.wait_ge(stats_ok, 3 * n - 2)
    own_step(dve, passed)
    nc.vector.bn_aggr(mean_var, stats).then_inc(stats_ok, 1)
    dve.wait_ge(stats_ok, 3 * n - 1)
    nc.vector.tensor_scalar(var_eps, mean_var[:, 1:2], LN_EPS, None, ALU.add)
    nc.vector.tensor_scalar(neg_mean, mean_var[:, 0:1], -1.0, None, ALU.mult).then_inc(stats_ok, 1)


def inverse_root(nc, pool, root, bias, var_eps, neg_mean, neghalf, stats_ok, root_ok, n):
    pool.wait_ge(stats_ok, 3 * n)
    nc.gpsimd.tensor_tensor(root, var_eps, neghalf, ALU.pow).then_inc(root_ok, 1)
    pool.wait_ge(root_ok, 2 * n - 1)
    nc.gpsimd.tensor_tensor(bias, neg_mean, root, ALU.mult).then_inc(root_ok, 1)


HILO = [(0, 0), (0, 1), (1, 0)]


def gnn_layer_pair(nc, s, x, out, u_l, u_g, wov, n2):
    nb = x.shape[0]
    groups = nb // GRP
    with ExitStack() as ctx:
        sb, ps, sem = scope(nc, ctx)
        xin = sb("xin", [P, GRP, N])
        xw_hi, xw_lo = sb("xw_hi", [P, 2, N], F32R), sb("xw_lo", [P, 2, N], F32R)
        ya, xa, xb = sb("ya", [P, 2, N]), sb("xa", [P, GRP, N]), sb("xb", [P, GRP, N])
        st_a, mv_a = sb("st_a", [P, 2, 6]), sb("mv_a", [P, 2, 2])
        ve_a, nm_a, rs_a, nb_a = (sb(n, [P, 2]) for n in ("ve_a", "nm_a", "rs_a", "nb_a"))
        ht = [sb(f"ht_{p}", [P, CH, GRP, P], F32R) for p in ("hi", "lo")]
        y = [sb(f"y_{p}", [P, 2, GRP, 2, P], F32R) for p in ("hi", "lo")]
        v = [sb(f"v_{p}", [P, GRP, N], F32R) for p in ("hi", "lo")]
        m = sb("m", [P, GRP, 2, P])
        prod = sb("prod", [P, GRP, 2, P])
        mnn, q_l, r_l = sb("mnn", [P, GRP, 2]), sb("q_l", [P, GRP]), sb("r_l", [P, GRP])
        dg_r = sb("dg_r", [P, GRP, P])
        a_l, a_g = sb("a_l", [P, GRP, P]), sb("a_g", [P, GRP, P])
        k_l, k_g = sb("k_l", [P, GRP, P]), sb("k_g", [P, GRP, P])
        deg, small = sb("deg_lg", [P, 2, GRP]), sb("small", [P, 8, GRP])
        kt = [sb(f"kt_{p}", [P, GRP, P], F32R) for p in ("hi", "lo")]
        yb, xo, sq = sb("yb", [P, 2, N]), sb("xo", [P, GRP, N]), sb("sq2", [P, GRP, N])
        st_b, mv_b = sb("st_b", [P, 2, 6]), sb("mv_b", [P, 2, 2])
        ve_b, nm_b, rs_b, nb_b = (sb(n, [P, 2]) for n in ("ve_b", "nm_b", "rs_b", "nb_b"))
        sums = sb("sums", [GRP, N])

        tr, yp, mp = [ps("tr0"), ps("tr1")], [ps("y_l"), ps("y_g")], [ps("m0"), ps("m1")]
        ht_ps = xw_ps, l0_ps = ps("xw_ps"), ps("l0_ps")

        x_loaded = [sem(f"x_in{i}") for i in range(GRP)]
        xw_made, xw_hi_ok, xw_lo_ok, l0_made = (sem(n) for n in ("xw_made", "xw_hi_ok", "xw_lo_ok", "l0_made"))
        ya_ok, st_a_ok, rs_a_ok, xa_ok, xb_ok = (
            sem(n) for n in ("ya_ok", "st_a_ok", "rs_a_ok", "xa_ok", "xb_ok"))
        ht_made, ht_hi_ok, ht_lo_ok = (sem(n) for n in ("ht_made", "ht_hi_ok", "ht_lo_ok"))
        y_made, y_hi_ok, y_lo_ok = (sem(n) for n in ("y_made", "y_hi_ok", "y_lo_ok"))
        m_made, m_ok, v_made, v_hi_ok, v_lo_ok = (sem(n) for n in ("m_made", "m_ok", "v_made", "v_hi_ok", "v_lo_ok"))
        prod_ok, mnn_ok, q_ok, r_ok, dgr_ok, ml_t, mg_t, r_row = (
            sem(n) for n in ("prod_ok", "mnn_ok", "q_ok", "r_ok", "dgr_ok", "ml_t", "mg_t", "r_row"))
        sl_ok, ul_ok, kl_ok, tg_ok, cl_ok, eg_ok, kg_ok, sm_ok, ka_ok, k_ok = (
            sem(n) for n in ("sl_ok", "ul_ok", "kl_ok", "tg_ok", "cl_ok", "eg_ok", "kg_ok", "sm_ok", "ka_ok", "k_ok"))
        kt_made, kt_hi_ok, kt_lo_ok, l1_made = (sem(n) for n in ("kt_made", "kt_hi_ok", "kt_lo_ok", "l1_made"))
        yb_ok, st_b_ok, rs_b_ok, xo_ok, sq_ok = (
            sem(n) for n in ("yb_ok", "st_b_ok", "rs_b_ok", "xo_ok", "sq_ok"))
        n2_made, n2_out, n2_stored = sem("n2_made"), sem("n2_out"), sem("n2_stored")
        stored = [sem(f"stored{i}") for i in range(GRP)]
        passed = sem("passed")
        block = ctx.enter_context(nc.Block())

        def turns(eng, turn):
            turn(None, None, 0)
            turn(None, 0, 1)
            with eng.Fori(0, groups - 2) as gp:
                turn(gp, gp + 1, gp + 2)
            turn(groups - 2, groups - 1, None)
            turn(groups - 1, None, None)

        @block.sync
        def _(sp):
            def load(b, i):
                sp.dma_start(xin[:, i, :], x[bass.ds(b, 1)].rearrange("a p n -> p (a n)")).then_inc(x_loaded[i], 16)

            def store(b, i):
                sp.dma_start(out[bass.ds(b, 1)].rearrange("a p n -> p (a n)"), xo[:, i, :]).then_inc(stored[i], 16)

            def turn(gp, ga):
                for kind, i in (("store", 0), ("store", 1), ("load", 0), ("store", 2), ("store", 3),
                                ("load", 1), ("load", 2), ("load", 3)):
                    if kind == "load" and ga is not None:
                        at = sp.snap(GRP * (ga + 1) + i)
                        sp.wait_ge(ya_ok, GRP * ga + i + 1)
                        load(at, i)
                    elif kind == "store" and gp is not None:
                        at = sp.snap(GRP * gp + i)
                        sp.wait_ge(xo_ok, 2 + GRP * gp + i + 1)
                        store(at, i)
                if gp is not None:
                    at = sp.snap(GRP * gp)
                    sp.wait_ge(n2_out, 1 + gp + 1)
                    sp.dma_start(n2[bass.ds(at, GRP), :], sums[:]).then_inc(n2_stored, 16)

            for i in range(GRP):
                load(i, i)
            turn(None, 0)
            turn(None, 1)
            with sp.Fori(0, groups - 3) as gp:
                turn(gp, gp + 2)
            for gp in range(groups - 3, groups):
                turn(gp, None)
            for i in range(GRP):
                sp.wait_ge(stored[i], 16 * (groups + 1))
            sp.wait_ge(n2_stored, 16 * (groups + 1))

        @block.tensor
        def _(pe):
            def turn(gp, g, ga):
                def hturn(i):
                    pe.wait_ge(xa_ok, GRP * ga + i + 1)
                    if i == 0:
                        pe.wait_ge(xw_lo_ok, 1 + GRP * (ga + 1))
                    elif i == 1:
                        pe.wait_ge(ya_ok, GRP * (ga + 1))
                    else:
                        pe.wait_ge(ht_lo_ok, GRP * ga + i - 1)
                    for c in range(CH):
                        mm = nc.tensor.transpose(ht_ps[i % 2][:, c * P:(c + 1) * P], xa[:, i, c * P:(c + 1) * P], s.ident[:])
                    mm.then_inc(ht_made, 1)

                def xw(i):
                    pe.wait_ge(x_loaded[i], 16 * (ga + 1))
                    pe.wait_ge(xw_lo_ok, GRP * ga + i + 1)
                    if i == 0 and not first(ga):
                        pe.wait_ge(ht_lo_ok, GRP * ga - 1)
                    for c in range(CH):
                        mm = nc.tensor.matmul(xw_ps[:, c * P:(c + 1) * P], xin[:, i, c * P:(c + 1) * P], s.adj[:],
                                              start=True, stop=True)
                    mm.then_inc(xw_made, 1)

                def l0(i):
                    pe.wait_ge(xw_hi_ok, GRP * ga + i + 1)
                    pe.wait_ge(xw_lo_ok, 1 + GRP * ga + i + 1)
                    if not first(ga) or i:
                        pe.wait_ge(ya_ok, GRP * ga + i)
                    if i == 0 and not first(ga):
                        pe.wait_ge(ht_lo_ok, GRP * ga)
                    xwp, anp = (xw_hi, xw_lo), (s.an_hi, s.an_lo)
                    for c in range(CH):
                        for n, (a, b) in enumerate(HILO):
                            mm = nc.tensor.matmul(l0_ps[:], xwp[a][:, i % 2, c * P:(c + 1) * P], anp[b][:, c, :],
                                                  start=(c == 0 and n == 0), stop=(c == CH - 1 and n == 2))
                    mm.then_inc(l0_made, 1)

                def yprod(c):
                    if c == 0:
                        pe.wait_ge(ht_hi_ok, GRP * (g + 1))
                        pe.wait_ge(ht_lo_ok, GRP * (g + 1))
                    for k, u in enumerate((u_l, u_g)):
                        if c == 0:
                            pe.wait_ge(v_lo_ok, GRP * (g + 1))
                        else:
                            pe.wait_ge(y_lo_ok, 8 * g + 2 * (c - 1) + k + 1)
                        for r in range(c + 1):
                            for n, (a, b) in enumerate(HILO):
                                at = TRI[r] + (c - r) * P
                                mm = nc.tensor.matmul(yp[k][:], u[a][:, at:at + P],
                                                      ht[b][:, r, :, :].rearrange("p i n -> p (i n)"),
                                                      start=(r == 0 and n == 0), stop=(r == c and n == 2))
                        mm.then_inc(y_made, 1)

                def mprod(c):
                    pe.wait_ge(y_hi_ok, 8 * g + 2 * (c + 1))
                    pe.wait_ge(y_lo_ok, 8 * g + 2 * (c + 1))
                    if c == 0:
                        pe.wait_ge(yb_ok, GRP * (g + 1))
                    for i in range(GRP):
                        for n, (a, b) in enumerate(HILO):
                            mm = nc.tensor.matmul(mp[i // 2][:, (i % 2) * 256:(i % 2) * 256 + 256], ht[a][:, c, i, :],
                                                  y[b][:, c % 2, i, :, :].rearrange("p k n -> p (k n)"),
                                                  start=(c == 0 and n == 0 and i % 2 == 0),
                                                  stop=(c == CH - 1 and n == 2), skip_group_check=True)
                    mm.then_inc(m_made, 1)

                def vprod(i):
                    if i < 2:
                        pe.wait_ge(y_lo_ok, 8 * g + 6 + i + 1)
                    else:
                        pe.wait_ge(v_lo_ok, GRP + GRP * g + i - 1)
                    for c in range(CH):
                        for n, (a, b) in enumerate(HILO):
                            mm = nc.tensor.matmul(yp[i % 2][:], ht[a][:, c, i, :], wov[b][:, c, :],
                                                  start=(c == 0 and n == 0), stop=(c == CH - 1 and n == 2))
                    mm.then_inc(v_made, 1)

                def m_l_turned():
                    pe.wait_ge(m_ok, 2 * (g + 1))
                    pe.wait_ge(kt_lo_ok, g + 1)
                    for i in range(GRP):
                        mm = nc.tensor.transpose(tr[0][:, i * P:(i + 1) * P], m[:, i, 0, :], s.ident[:])
                    mm.then_inc(ml_t, 1)

                def m_g_turned():
                    pe.wait_ge(prod_ok, g + 1)
                    if gp is not None:
                        pe.wait_ge(n2_out, gp + 1)
                    for i in range(GRP):
                        nc.tensor.matmul(tr[1][:, i * P:(i + 1) * P], m[:, i, 1, :], s.ident[:],
                                         start=(i == 0), stop=False, skip_group_check=True)
                    nc.tensor.matmul(tr[1][:], s.negones[:], prod[:, :, 1, :],
                                     start=False, stop=True, skip_group_check=True).then_inc(mg_t, 1)

                def r_rows():
                    pe.wait_ge(dgr_ok, g + 1)
                    nc.tensor.matmul(mp[0][:], s.ones[:], dg_r[:].rearrange("p i n -> p (i n)"),
                                     start=True, stop=True).then_inc(r_row, 1)

                def k_turned():
                    pe.wait_ge(k_ok, GRP * (gp + 1))
                    for i in range(GRP):
                        mm = nc.tensor.transpose(tr[0][:, i * P:(i + 1) * P], k_g[:, i, :], s.ident[:])
                    mm.then_inc(kt_made, 1)

                def l1(i):
                    if i == 0:
                        pe.wait_ge(kt_hi_ok, gp + 1)
                        pe.wait_ge(kt_lo_ok, 1 + gp + 1)
                    if i >= 2:
                        pe.wait_ge(yb_ok, GRP + GRP * gp + i - 1)
                    for n, (a, b) in enumerate(HILO):
                        mm = nc.tensor.matmul(mp[i % 2][:], kt[a][:, i, :], v[b][:, i, :], start=(n == 0), stop=(n == 2))
                    mm.then_inc(l1_made, 1)

                def squares(half):
                    pe.wait_ge(sq_ok, GRP * gp + 2 * half + 2)
                    for i in (2 * half, 2 * half + 1):
                        mm = nc.tensor.matmul(tr[1][0:GRP, :], s.pick[:, i, 0:GRP], sq[:, i, :],
                                              start=(i == 0), stop=(i == GRP - 1))
                    if half:
                        mm.then_inc(n2_made, 1)

                A, B, C = ga is not None, g is not None, gp is not None
                if A:
                    xw(0)
                if C:
                    k_turned()
                if B:
                    yprod(0)
                if C:
                    l1(0)
                    l1(1)
                if A:
                    l0(0)
                if C:
                    l1(2)
                    l1(3)
                for i in range(1, GRP):
                    if A:
                        xw(i)
                    if B:
                        yprod(i)
                    if A:
                        l0(i)
                    if B:
                        mprod(i - 1)
                if B:
                    vprod(0)
                    mprod(3)
                    vprod(1)
                if A:
                    hturn(0)
                if B:
                    m_l_turned()
                    m_g_turned()
                    vprod(2)
                if A:
                    hturn(1)
                if B:
                    r_rows()
                    vprod(3)
                    pe.wait_ge(tg_ok, GRP * (g + 1))
                if A:
                    hturn(2)
                if C:
                    squares(0)
                if A:
                    hturn(3)
                if C:
                    squares(1)

            turns(pe, turn)

        @block.scalar
        def _(act):
            copy = lambda o, i: nc.scalar.activation(o, i, ACT.Copy)

            def turn(gp, g, ga):
                def ht_hi(i):
                    act.wait_ge(ht_made, GRP * ga + i + 1)
                    act.wait_ge(v_made, GRP * ga + i + 1)
                    act.wait_ge(m_made, 2 + GRP * ga)
                    copy(ht[0][:, :, i, :], ht_ps[i % 2][:].rearrange("p (c n) -> p c n", c=CH)).then_inc(ht_hi_ok, 1)

                def xw_hi_(i):
                    act.wait_ge(xw_made, GRP * ga + i + 1)
                    act.wait_ge(l0_made, GRP * ga + i + 1)
                    copy(xw_hi[:, i % 2, :], xw_ps[:]).then_inc(xw_hi_ok, 1)

                def norm_a(i):
                    act.wait_ge(rs_a_ok, 2 * (GRP * ga + i + 1))
                    act.wait_ge(xb_ok, GRP * ga + i + 1)
                    nc.scalar.activation(xa[:, i, :], ya[:, i % 2, :], ACT.Identity, scale=rs_a[:, i % 2:i % 2 + 1],
                                         bias=nb_a[:, i % 2:i % 2 + 1]).then_inc(xa_ok, 1)

                def y_hi(c):
                    for k in range(2):
                        act.wait_ge(y_made, 8 * g + 2 * c + k + 1)
                        act.wait_ge(m_made, CH * g + c + 1)
                        copy(y[0][:, c % 2, :, k, :], yp[k][:].rearrange("p (i n) -> p i n", i=GRP)).then_inc(y_hi_ok, 1)

                def v_hi(i):
                    act.wait_ge(v_made, GRP + GRP * g + i + 1)
                    copy(v[0][:, i, :], yp[i % 2][:]).then_inc(v_hi_ok, 1)

                def m_out():
                    act.wait_ge(m_made, 2 + CH * (g + 1))
                    for k in range(2):
                        copy(m[:, 2 * k:2 * k + 2, :, :].rearrange("p i k n -> p (i k n)"), mp[k][:]).then_inc(m_ok, 1)

                def exp_g():
                    act.wait_ge(cl_ok, g + 1)
                    nc.scalar.activation(a_g[:], a_g[:], ACT.Exp, scale=s.inv_s2[:, 0:1]).then_inc(eg_ok, 1)

                def kt_hi():
                    act.wait_ge(kt_made, gp + 1)
                    copy(kt[0][:].rearrange("p i n -> p (i n)"), tr[0][:]).then_inc(kt_hi_ok, 1)

                def norm_b(i):
                    act.wait_ge(rs_b_ok, 2 * (GRP * gp + i + 1))
                    act.wait_ge(stored[i], 16 * (gp + 1))
                    nc.scalar.activation(xo[:, i, :], yb[:, i % 2, :], ACT.Identity, scale=rs_b[:, i % 2:i % 2 + 1],
                                         bias=nb_b[:, i % 2:i % 2 + 1]).then_inc(xo_ok, 1)

                def square(i):
                    act.wait_ge(xo_ok, 2 + GRP * gp + i + 1)
                    nc.scalar.activation(sq[:, i, :], xo[:, i, :], ACT.Square).then_inc(sq_ok, 1)

                def sums_out():
                    act.wait_ge(n2_made, gp + 1)
                    act.wait_ge(n2_stored, 16 * (gp + 1))
                    copy(sums[:], tr[1][0:GRP, :]).then_inc(n2_out, 1)

                A, B, C = ga is not None, g is not None, gp is not None
                if A:
                    xw_hi_(0)
                if C:
                    kt_hi()
                if B:
                    y_hi(0)
                if C:
                    norm_b(0)
                    norm_b(1)
                    square(0)
                if A:
                    xw_hi_(1)
                if B:
                    y_hi(1)
                if A:
                    norm_a(0)
                if C:
                    norm_b(2)
                    square(1)
                    norm_b(3)
                    square(2)
                    square(3)
                if A:
                    xw_hi_(2)
                if B:
                    y_hi(2)
                if A:
                    norm_a(1)
                    xw_hi_(3)
                if B:
                    y_hi(3)
                if A:
                    norm_a(2)
                if B:
                    v_hi(0)
                    m_out()
                if A:
                    norm_a(3)
                if B:
                    v_hi(1)
                if A:
                    ht_hi(0)
                if B:
                    v_hi(2)
                    exp_g()
                if A:
                    ht_hi(1)
                if B:
                    v_hi(3)
                if A:
                    ht_hi(2)
                    ht_hi(3)
                if C:
                    sums_out()

            act.sem_inc(l0_made, 2)
            act.sem_inc(m_made, 2)
            act.sem_inc(v_made, GRP)
            act.sem_inc(xo_ok, 2)
            act.sem_inc(n2_out, 1)
            act.sem_inc(n2_stored, 16)
            for i in range(GRP):
                act.sem_inc(stored[i], 16)
            turns(act, turn)

        @block.gpsimd
        def _(pool):
            def turn(gp, g, ga):
                def keep(i):
                    if g is None:
                        return
                    pool.wait_ge(xa_ok, GRP * g + i + 1)
                    pool.wait_ge(yb_ok, GRP * g + i + 1)
                    own_step(pool, passed)
                    nc.gpsimd.tensor_copy(xb[:, i, :], xa[:, i, :]).then_inc(xb_ok, 1)

                def root_a(i):
                    j = slice(i % 2, i % 2 + 1)
                    if ga is not None:
                        inverse_root(nc, pool, rs_a[:, j], nb_a[:, j], ve_a[:, j], nm_a[:, j],
                                     s.neghalf[:, 0:1], st_a_ok, rs_a_ok, GRP * ga + i + 1)

                def root_b(i):
                    j = slice(i % 2, i % 2 + 1)
                    if gp is not None:
                        inverse_root(nc, pool, rs_b[:, j], nb_b[:, j], ve_b[:, j], nm_b[:, j],
                                     s.neghalf[:, 0:1], st_b_ok, rs_b_ok, GRP * gp + i + 1)

                root_b(0)
                root_b(1)
                keep(0)
                root_a(0)
                root_b(2)
                keep(1)
                root_b(3)
                root_a(1)
                keep(2)
                keep(3)
                root_a(2)
                root_a(3)
                if g is not None:
                    pool.wait_ge(q_ok, g + 1)
                    nc.gpsimd.tensor_tensor(r_l[:], q_l[:], s.neghalf[:], ALU.pow).then_inc(r_ok, 1)

            pool.sem_inc(xb_ok, GRP)
            turns(pool, turn)

        @block.vector
        def _(dve):
            def lo_part(lo, full, hi, done):
                nc.vector.tensor_tensor(lo, full, hi.bitcast(F32), ALU.subtract).then_inc(done, 1)

            def turn(gp, g, ga):
                def ht_lo(i):
                    dve.wait_ge(ht_hi_ok, GRP * ga + i + 1)
                    lo_part(ht[1][:, :, i, :], ht_ps[i % 2][:].rearrange("p (c n) -> p c n", c=CH), ht[0][:, :, i, :], ht_lo_ok)

                def xw_lo_(i):
                    dve.wait_ge(xw_hi_ok, GRP * ga + i + 1)
                    lo_part(xw_lo[:, i % 2, :], xw_ps[:], xw_hi[:, i % 2, :], xw_lo_ok)

                def residual_a(i):
                    dve.wait_ge(l0_made, 2 + GRP * ga + i + 1)
                    if not first(ga) or i >= 2:
                        dve.wait_ge(xa_ok, GRP * ga + i - 1)
                    nc.vector.scalar_tensor_tensor(out=ya[:, i % 2, :], in0=l0_ps[:], scalar=s.b0[:, 0:1],
                                                   in1=xin[:, i, :], op0=ALU.add, op1=ALU.add).then_inc(ya_ok, 1)
                    j = slice(i % 2, i % 2 + 1)
                    statistics(nc, dve, ya[:, i % 2, :], st_a[:, i % 2, :], mv_a[:, i % 2, :], ve_a[:, j], nm_a[:, j],
                               ya_ok, st_a_ok, GRP * ga + i + 1, passed)

                def y_lo(c):
                    for k in range(2):
                        dve.wait_ge(y_hi_ok, 8 * g + 2 * c + k + 1)
                        lo_part(y[1][:, c % 2, :, k, :], yp[k][:].rearrange("p (i n) -> p i n", i=GRP),
                                y[0][:, c % 2, :, k, :], y_lo_ok)

                def v_lo(i):
                    dve.wait_ge(v_hi_ok, GRP * g + i + 1)
                    lo_part(v[1][:, i, :], yp[i % 2][:], v[0][:, i, :], v_lo_ok)

                def diagonals():
                    dve.wait_ge(m_ok, 2 * (g + 1))
                    m8 = m[:].rearrange("p i k n -> p (i k) n")
                    nc.vector.tensor_tensor(prod[:].rearrange("p i k n -> p (i k) n"), m8, over(s.ident[:], 2 * GRP),
                                            ALU.mult).then_inc(prod_ok, 1)
                    dve.wait_ge(prod_ok, g + 1)
                    nc.vector.tensor_reduce(mnn[:].rearrange("p i k -> p (i k)"),
                                            prod[:].rearrange("p i k n -> p (i k) n"), AX.X, ALU.add).then_inc(mnn_ok, 1)
                    dve.wait_ge(mnn_ok, g + 1)
                    nc.vector.tensor_scalar(q_l[:], mnn[:, :, 0], 2.0, EPS * EPS, ALU.mult, ALU.max).then_inc(q_ok, 1)

                def diag_r():
                    dve.wait_ge(r_ok, g + 1)
                    nc.vector.tensor_tensor(dg_r[:], over(s.ident[:], GRP), along(r_l[:], P), ALU.mult).then_inc(dgr_ok, 1)

                def metric_l():
                    dve.wait_ge(ml_t, g + 1)
                    nc.vector.tensor_tensor(a_l[:], m[:, :, 0, :], tr[0][:].rearrange("p (i n) -> p i n", i=GRP),
                                            ALU.add).then_inc(sl_ok, 1)

                def kernel_l():
                    dve.wait_ge(r_row, g + 1)
                    dve.wait_ge(sl_ok, g + 1)
                    flat = a_l[:].rearrange("p i n -> p (i n)")
                    nc.vector.scalar_tensor_tensor(out=flat, in0=flat, scalar=0.0, in1=mp[0][:],
                                                   op0=ALU.max, op1=ALU.mult).then_inc(ul_ok, 1)
                    dve.wait_ge(ul_ok, g + 1)
                    for i in range(GRP):
                        nc.vector.tensor_tensor_reduce(out=k_l[:, i, :], in0=a_l[:, i, :], in1=s.adj_ne[:], scale=1.0,
                                                       scalar=0.0, op0=ALU.mult, op1=ALU.add,
                                                       accum_out=deg[:, 0, i:i + 1]).then_inc(kl_ok, 1)

                def distances():
                    dve.wait_ge(mg_t, g + 1)
                    for i in range(GRP):
                        nc.vector.scalar_tensor_tensor(out=a_g[:, i, :], in0=m[:, i, 1, :], scalar=mnn[:, i, 1:2],
                                                       in1=tr[1][:, i * P:(i + 1) * P], op0=ALU.subtract,
                                                       op1=ALU.add).then_inc(tg_ok, 1)
                    dve.wait_ge(tg_ok, GRP * (g + 1))
                    nc.vector.tensor_scalar(a_g[:], a_g[:], 0.0, None, ALU.min).then_inc(cl_ok, 1)

                def kernel_g():
                    dve.wait_ge(eg_ok, g + 1)
                    for i in range(GRP):
                        nc.vector.tensor_tensor_reduce(out=k_g[:, i, :], in0=a_g[:, i, :], in1=s.adj_ne[:], scale=1.0,
                                                       scalar=0.0, op0=ALU.mult, op1=ALU.add,
                                                       accum_out=deg[:, 1, i:i + 1]).then_inc(kg_ok, 1)

                def kernel_sum():
                    n = 6 * g
                    dve.wait_ge(kl_ok, GRP * (g + 1))
                    nc.vector.tensor_tensor(small[:, 0, :], r_l[:], deg[:, 0, :], ALU.mult).then_inc(sm_ok, 1)
                    dve.wait_ge(kg_ok, GRP * (g + 1))
                    nc.vector.tensor_scalar(small[:, 1, :], deg[:, 1, :], EPS, None, ALU.max).then_inc(sm_ok, 1)
                    dve.wait_ge(sm_ok, n + 1)
                    nc.vector.tensor_scalar(small[:, 0, :], small[:, 0, :], EPS, None, ALU.max).then_inc(sm_ok, 1)
                    dve.wait_ge(sm_ok, n + 3)
                    nc.vector.reciprocal(small[:, 2:4, :], small[:, 0:2, :]).then_inc(sm_ok, 1)
                    dve.wait_ge(sm_ok, n + 4)
                    nc.vector.scalar_tensor_tensor(out=small[:, 4, :], in0=r_l[:], scalar=s.w_l[:, 0:1],
                                                   in1=small[:, 2, :], op0=ALU.mult, op1=ALU.mult).then_inc(sm_ok, 1)
                    nc.vector.tensor_scalar(small[:, 5, :], small[:, 3, :], s.w_g[:, 0:1], None, ALU.mult).then_inc(sm_ok, 1)
                    dve.wait_ge(sm_ok, n + 6)
                    for i in range(GRP):
                        nc.vector.tensor_scalar(k_l[:, i, :], k_l[:, i, :], small[:, 4, i:i + 1], None,
                                                ALU.mult).then_inc(ka_ok, 1)
                    for i in range(GRP):
                        dve.wait_ge(ka_ok, GRP * g + i + 1)
                        nc.vector.scalar_tensor_tensor(out=k_g[:, i, :], in0=k_g[:, i, :], scalar=small[:, 5, i:i + 1],
                                                       in1=k_l[:, i, :], op0=ALU.mult, op1=ALU.add).then_inc(k_ok, 1)

                def kt_lo():
                    dve.wait_ge(kt_hi_ok, gp + 1)
                    lo_part(kt[1][:].rearrange("p i n -> p (i n)"), tr[0][:], kt[0][:].rearrange("p i n -> p (i n)"), kt_lo_ok)

                def residual_b(i):
                    dve.wait_ge(l1_made, GRP * gp + i + 1)
                    dve.wait_ge(xb_ok, GRP + GRP * gp + i + 1)
                    dve.wait_ge(xo_ok, GRP * gp + i + 1)
                    nc.vector.tensor_tensor(yb[:, i % 2, :], mp[i % 2][:], xb[:, i, :], ALU.add).then_inc(yb_ok, 1)
                    dve.wait_ge(yb_ok, GRP + GRP * gp + i + 1)
                    j = slice(i % 2, i % 2 + 1)
                    statistics(nc, dve, yb[:, i % 2, :], st_b[:, i % 2, :], mv_b[:, i % 2, :], ve_b[:, j], nm_b[:, j],
                               yb_ok, st_b_ok, GRP * gp + i + 1, passed)

                A, B, C = ga is not None, g is not None, gp is not None
                if A:
                    xw_lo_(0)
                if C:
                    kt_lo()
                if B:
                    y_lo(0)
                if C:
                    residual_b(0)
                    residual_b(1)
                if A:
                    residual_a(0)
                if C:
                    residual_b(2)
                if A:
                    xw_lo_(1)
                if B:
                    y_lo(1)
                if C:
                    residual_b(3)
                if A:
                    residual_a(1)
                for i in (2, 3):
                    if A:
                        xw_lo_(i)
                    if B:
                        y_lo(i)
                    if A:
                        residual_a(i)
                if B:
                    v_lo(0)
                    diagonals()
                    v_lo(1)
                    diag_r()
                    metric_l()
                    distances()
                if A:
                    ht_lo(0)
                if B:
                    v_lo(2)
                    kernel_l()
                if A:
                    ht_lo(1)
                if B:
                    v_lo(3)
                    kernel_g()
                    kernel_sum()
                if A:
                    ht_lo(2)
                    ht_lo(3)

            dve.sem_inc(xw_lo_ok, 1)
            dve.sem_inc(v_lo_ok, GRP)
            dve.sem_inc(kt_lo_ok, 1)
            dve.sem_inc(yb_ok, GRP)
            turns(dve, turn)


def last_layers(nc, s, x, out):
    nb = x.shape[0]
    groups = nb // GRP
    with ExitStack() as ctx:
        sb, ps, sem = scope(nc, ctx)
        xin = sb("xin", [P, GRP, N])
        xw_hi, xw_lo = sb("xw_hi", [P, 2, N], F32R), sb("xw_lo", [P, 2, N], F32R)
        ya, xa = sb("ya", [P, 2, N]), sb("xa", [P, 2, N])
        x_hi, x_lo = sb("x_hi", [P, GRP, N], F32R), sb("x_lo", [P, GRP, N], F32R)
        xb = sb("xb", [P, GRP, N])
        yb, xo = sb("yb", [P, 2, N]), sb("xo", [P, GRP, N])
        st_a, mv_a = sb("st_a", [P, 2, 6]), sb("mv_a", [P, 2, 2])
        ve_a, nm_a, rs_a, nb_a = (sb(n, [P, 2]) for n in ("ve_a", "nm_a", "rs_a", "nb_a"))
        st_b, mv_b = sb("st_b", [P, 2, 6]), sb("mv_b", [P, 2, 2])
        ve_b, nm_b, rs_b, nb_b = (sb(n, [P, 2]) for n in ("ve_b", "nm_b", "rs_b", "nb_b"))
        xw_ps, l2_ps, l3_ps = [ps("xw_ps0"), ps("xw_ps1")], [ps("l2_ps0"), ps("l2_ps1")], [ps("l3_ps0"), ps("l3_ps1")]

        x_loaded = [sem(f"x_in{i}") for i in range(GRP)]
        stored = [sem(f"stored{i}") for i in range(GRP)]
        passed = sem("passed")
        xw_made, xw_hi_ok, xw_lo_ok, l2_made, l3_made = (
            sem(n) for n in ("xw_made", "xw_hi_ok", "xw_lo_ok", "l2_made", "l3_made"))
        ya_ok, st_a_ok, rs_a_ok, xa_ok, x_hi_ok, x_lo_ok, xb_ok = (
            sem(n) for n in ("ya_ok", "st_a_ok", "rs_a_ok", "xa_ok", "x_hi_ok", "x_lo_ok", "xb_ok"))
        yb_ok, st_b_ok, rs_b_ok, xo_ok = (sem(n) for n in ("yb_ok", "st_b_ok", "rs_b_ok", "xo_ok"))
        block = ctx.enter_context(nc.Block())

        def turns(eng, turn):
            turn(None, 0)
            with eng.Fori(0, groups - 1) as g:
                turn(g, g + 1)
            turn(groups - 1, None)

        @block.sync
        def _(sp):
            def load(b, i):
                sp.dma_start(xin[:, i, :], x[bass.ds(b, 1)].rearrange("a p n -> p (a n)")).then_inc(x_loaded[i], 16)

            def store(b, i):
                sp.dma_start(out[bass.ds(b, 1)].rearrange("a p n -> p (a n)"), xo[:, i, :]).then_inc(stored[i], 16)

            for i in range(GRP):
                load(i, i)
            for i in range(GRP):
                sp.wait_ge(ya_ok, i + 1)
                load(GRP + i, i)
            with sp.Fori(0, groups - 2) as g:
                for i in range(GRP):
                    at = sp.snap(g * GRP + 2 * GRP + i)
                    sp.wait_ge(ya_ok, GRP * g + GRP + i + 1)
                    load(at, i)
                    at = sp.snap(g * GRP + i)
                    sp.wait_ge(xo_ok, 2 + GRP * g + i + 1)
                    store(at, i)
            for g in (groups - 2, groups - 1):
                for i in range(GRP):
                    sp.wait_ge(xo_ok, 2 + GRP * g + i + 1)
                    store(g * GRP + i, i)
            for i in range(GRP):
                sp.wait_ge(stored[i], 16 * (groups + 1))

        @block.tensor
        def _(pe):
            def turn(g, ga):
                def xw(i):
                    pe.wait_ge(x_loaded[i], 16 * (ga + 1))
                    pe.wait_ge(xw_lo_ok, GRP * ga + i + 1)
                    for c in range(CH):
                        mm = nc.tensor.matmul(xw_ps[i % 2][:, c * P:(c + 1) * P], xin[:, i, c * P:(c + 1) * P],
                                              s.adj[:], start=True, stop=True)
                    mm.then_inc(xw_made, 1)

                def l2(i):
                    pe.wait_ge(xw_hi_ok, GRP * ga + i + 1)
                    pe.wait_ge(xw_lo_ok, 2 + GRP * ga + i + 1)
                    if not first(ga) or i >= 2:
                        pe.wait_ge(ya_ok, GRP * ga + i - 1)
                    xwp, anp = (xw_hi, xw_lo), (s.an_hi, s.an_lo)
                    for c in range(CH):
                        for n, (a, b) in enumerate(HILO):
                            mm = nc.tensor.matmul(l2_ps[i % 2][:], xwp[a][:, i % 2, c * P:(c + 1) * P], anp[b][:, c, :],
                                                  start=(c == 0 and n == 0), stop=(c == CH - 1 and n == 2))
                    mm.then_inc(l2_made, 1)

                def l3(i):
                    pe.wait_ge(x_hi_ok, GRP * g + i + 1)
                    pe.wait_ge(x_lo_ok, GRP * g + i + 1)
                    pe.wait_ge(yb_ok, GRP * g + i + 1)
                    wp, xp = (s.adj2_hi, s.adj2_lo), (x_hi, x_lo)
                    for n, (a, b) in enumerate(HILO):
                        mm = nc.tensor.matmul(l3_ps[i % 2][:], wp[a][:], xp[b][:, i, :], start=(n == 0), stop=(n == 2))
                    mm.then_inc(l3_made, 1)

                if ga is not None:
                    xw(0)
                for i in range(GRP):
                    if ga is not None and i + 1 < GRP:
                        xw(i + 1)
                    if g is not None:
                        l3(i)
                    if ga is not None:
                        l2(i)

            turns(pe, turn)

        @block.scalar
        def _(act):
            def turn(g, ga):
                def xw_hi_(i):
                    act.wait_ge(xw_made, GRP * ga + i + 1)
                    act.wait_ge(l2_made, GRP * ga + i + 1)
                    nc.scalar.activation(xw_hi[:, i % 2, :], xw_ps[i % 2][:], ACT.Copy).then_inc(xw_hi_ok, 1)

                def norm_a(ga, i):
                    j = slice(i % 2, i % 2 + 1)
                    act.wait_ge(rs_a_ok, 2 * (GRP * ga + i + 1))
                    act.wait_ge(xb_ok, 2 + GRP * ga + i + 1)
                    nc.scalar.activation(xa[:, i % 2, :], ya[:, i % 2, :], ACT.Identity, scale=rs_a[:, j],
                                         bias=nb_a[:, j]).then_inc(xa_ok, 1)
                    act.wait_ge(xa_ok, GRP * ga + i + 1)
                    act.wait_ge(l3_made, GRP * ga + i + 1)
                    nc.scalar.activation(x_hi[:, i, :], xa[:, i % 2, :], ACT.Copy).then_inc(x_hi_ok, 1)

                def norm_b(i):
                    j = slice(i % 2, i % 2 + 1)
                    act.wait_ge(rs_b_ok, 2 * (GRP * g + i + 1))
                    act.wait_ge(stored[i], 16 * (g + 1))
                    nc.scalar.activation(xo[:, i, :], yb[:, i % 2, :], ACT.Identity, scale=rs_b[:, j],
                                         bias=nb_b[:, j]).then_inc(xo_ok, 1)

                if ga is not None:
                    xw_hi_(0)
                for i in range(GRP):
                    if ga is not None and i + 1 < GRP:
                        xw_hi_(i + 1)
                    if i:
                        if ga is not None:
                            norm_a(ga, i - 1)
                    elif g is not None:
                        norm_a(g, GRP - 1)
                    if g is not None:
                        norm_b(i)

            act.sem_inc(l2_made, 2)
            act.sem_inc(l3_made, GRP)
            act.sem_inc(xo_ok, 2)
            for i in range(GRP):
                act.sem_inc(stored[i], 16)
            turns(act, turn)

        @block.gpsimd
        def _(pool):
            def turn(g, ga):
                def root(ga, i):
                    j = slice(i % 2, i % 2 + 1)
                    inverse_root(nc, pool, rs_a[:, j], nb_a[:, j], ve_a[:, j], nm_a[:, j],
                                 s.neghalf[:, 0:1], st_a_ok, rs_a_ok, GRP * ga + i + 1)

                def pass_on(ga, i):
                    pool.wait_ge(x_hi_ok, GRP * ga + i + 1)
                    nc.gpsimd.tensor_tensor(x_lo[:, i, :], xa[:, i % 2, :], x_hi[:, i, :].bitcast(F32),
                                            ALU.subtract).then_inc(x_lo_ok, 1)
                    if not first(ga):
                        pool.wait_ge(yb_ok, GRP * ga + i - 1)
                    nc.gpsimd.tensor_tensor(xb[:, i, :], xa[:, i % 2, :], s.b3[:], ALU.add).then_inc(xb_ok, 1)

                for i in range(GRP):
                    before = (ga, i - 1) if i else (g, GRP - 1)
                    j = slice(i % 2, i % 2 + 1)
                    if before[0] is not None:
                        root(*before)
                    if g is not None:
                        inverse_root(nc, pool, rs_b[:, j], nb_b[:, j], ve_b[:, j], nm_b[:, j],
                                     s.neghalf[:, 0:1], st_b_ok, rs_b_ok, GRP * g + i + 1)
                    if before[0] is not None:
                        pass_on(*before)

            pool.sem_inc(xb_ok, 4)
            turns(pool, turn)

        @block.vector
        def _(dve):
            def turn(g, ga):
                def xw_lo_(i):
                    dve.wait_ge(xw_hi_ok, GRP * ga + i + 1)
                    nc.vector.tensor_tensor(xw_lo[:, i % 2, :], xw_ps[i % 2][:], xw_hi[:, i % 2, :].bitcast(F32),
                                            ALU.subtract).then_inc(xw_lo_ok, 1)

                def residual_a(i):
                    j = slice(i % 2, i % 2 + 1)
                    dve.wait_ge(l2_made, 2 + GRP * ga + i + 1)
                    if not first(ga) or i >= 2:
                        dve.wait_ge(xa_ok, GRP * ga + i - 1)
                    nc.vector.scalar_tensor_tensor(out=ya[:, i % 2, :], in0=l2_ps[i % 2][:], scalar=s.b2[:, 0:1],
                                                   in1=xin[:, i, :], op0=ALU.add, op1=ALU.add).then_inc(ya_ok, 1)
                    statistics(nc, dve, ya[:, i % 2, :], st_a[:, i % 2, :], mv_a[:, i % 2, :], ve_a[:, j], nm_a[:, j],
                               ya_ok, st_a_ok, GRP * ga + i + 1, passed)

                def residual_b(i):
                    j = slice(i % 2, i % 2 + 1)
                    dve.wait_ge(l3_made, GRP + GRP * g + i + 1)
                    dve.wait_ge(xb_ok, 4 + GRP * g + i + 1)
                    dve.wait_ge(xo_ok, GRP * g + i + 1)
                    nc.vector.tensor_tensor(yb[:, i % 2, :], l3_ps[i % 2][:], xb[:, i, :], ALU.add).then_inc(yb_ok, 1)
                    dve.wait_ge(yb_ok, 2 + GRP * g + i + 1)
                    statistics(nc, dve, yb[:, i % 2, :], st_b[:, i % 2, :], mv_b[:, i % 2, :], ve_b[:, j], nm_b[:, j],
                               yb_ok, st_b_ok, GRP * g + i + 1, passed)

                if ga is not None:
                    xw_lo_(0)
                for i in range(GRP):
                    if ga is not None and i + 1 < GRP:
                        xw_lo_(i + 1)
                    if g is not None:
                        residual_b(i)
                    if ga is not None:
                        residual_a(i)

            dve.sem_inc(xw_lo_ok, 2)
            dve.sem_inc(yb_ok, 2)
            turns(dve, turn)


def adj_resnorm_kernel(nc, x, adj, bias0, w_lang, w_grav, w_v, w_o, gate, log_sigma, bias2, bias3, out):
    nb = x.shape[0]
    assert x.shape[1:] == (P, N) and nb % SGRP == 0 and nb <= P
    between = nc.dram_tensor("between", [nb, P, N], F32, kind="Internal").ap()
    n2 = nc.dram_tensor("n2", [nb, N], F32, kind="Internal").ap()
    spill_hi = nc.dram_tensor("spill_hi", [nb, N], F32, kind="Internal").ap()
    spill_lo = nc.dram_tensor("spill_lo", [nb, N], F32, kind="Internal").ap()
    s = Shared()
    s.nb = nb
    with ExitStack() as ctx:
        constants(nc, ctx, s, adj, bias0, bias2, bias3, gate, log_sigma)

        def adjacency(source, before_choice):
            with ExitStack() as psum_room, ExitStack() as choice_room:
                _, ps, _ = scope(nc, psum_room)
                with ExitStack() as x_room:
                    sb, _, _ = scope(nc, x_room)
                    xres, rows = sb("xres", [P, nb, N]), sb("rows", [2 * SGRP, nb // SGRP, N], F32R)
                    if source is None:
                        first_norms(nc, s, x, xres, n2)
                    hh, hl = [ps(f"hh{k}") for k in range(3)], [ps(f"hl{k}") for k in range(CH)]
                    norm_rows(nc, s, n2, rows, spill_hi, spill_lo)
                    similarity(nc, s, xres, rows, hh, hl, source)
                weights = before_choice()
                sb, _, _ = scope(nc, choice_room)
                sim, work = sb("sim", [P, CH, N]), sb("work", [P, CH, 8 + N])
                whole_similarity(nc, s, hh, hl, sim, work)
                psum_room.close()
                choose(nc, s, work, weights)
                normal_adjacency(nc, s, sim, work)

        with ExitStack() as weight_room:
            sb, _, _ = scope(nc, weight_room)
            dst = {}

            def weights():
                for k in ("lang", "grav"):
                    dst[k] = [sb(f"u_{k}_{p}", [P, TRI_W], F32R) for p in ("hi", "lo")]
                dst["ov"] = [sb(f"wov_{p}", [P, CH, N], F32R) for p in ("hi", "lo")]
                return {"lang": w_lang, "grav": w_grav, "v": w_v, "o": w_o}, dst

            adjacency(None, weights)
            gnn_layer_pair(nc, s, x, between, dst["lang"], dst["grav"], dst["ov"], n2)
        adjacency(between, lambda: None)
        last_layers(nc, s, between, out)


_INS = ["x", "adj", "L0_gnn_bias", "L1_gnn_W_lang", "L1_gnn_W_grav", "L1_gnn_W_V", "L1_gnn_W_O",
        "L1_gnn_gate_logit", "L1_gnn_log_sigma", "L2_gnn_bias", "L3_gnn_bias"]


def kernel(**inputs):
    import concourse.bacc as _bacc
    from concourse.bass_utils import run_bass_kernel_spmd as _run

    nc = _bacc.Bacc("TRN2", target_bir_lowering=False, num_devices=1)
    arrays, args = {}, []
    for name in _INS:
        a = np.ascontiguousarray(inputs[name])
        if a.ndim == 0:
            a = a.reshape(1, 1)
        arrays[f"in_{name}"] = a
        args.append(nc.dram_tensor(f"in_{name}", a.shape, mybir.dt.from_np(a.dtype), kind="ExternalInput").ap())
    shape = inputs["x"].shape
    out = nc.dram_tensor("out_0", shape, F32, kind="ExternalOutput").ap()
    adj_resnorm_kernel(nc, *args, out)
    r = _run(nc, [arrays], core_ids=[0])
    return r.results[0]["out_0"]
```

```python
from contextlib import ExitStack
from itertools import count

import numpy as np

import concourse.bass as bass
from concourse import mybir

F32 = mybir.dt.float32
F32R = mybir.dt.float32r
ALU = mybir.AluOpType
ACT = mybir.ActivationFunctionType
AX = mybir.AxisListType

P = 128
N = 512
CH = N // P
GRP = 4
SGRP = 8
TOP = max(int(N * 0.3), 1)
LN_EPS = 1e-5
NORM_EPS = 1e-12
EPS = 1e-8
NEVER = -2.0 ** 126
CHOSEN = -2.0 ** 127
TRI = [0, 512, 896, 1152]
TRI_W = 1280

SERIAL = count()



def own_step(eng, passed):
    eng.sem_inc(passed, 1)


class Shared:
    pass


def scope(nc, ctx):
    own = lambda name: f"{name}_{next(SERIAL)}"
    sb = lambda name, shape, dt=F32: ctx.enter_context(nc.sbuf_tensor(own(name), shape, dt))
    ps = lambda name, shape=(P, 512): ctx.enter_context(nc.psum_tensor(own(name), list(shape), F32))
    taken = []

    def sem(name):
        taken.append(nc.alloc_semaphore(own(name)))
        return taken[-1]

    def give_back():
        if taken:
            nc.clear_and_free_semaphores(taken)
            nc.all_engine_barrier()

    ctx.callback(give_back)
    return sb, ps, sem


def over(ap, n):
    return ap.unsqueeze(1).broadcast_to([P, n, ap.shape[1]])


def along(ap, m):
    return ap.unsqueeze(2).broadcast_to([P, ap.shape[1], m])


def constants(nc, ctx, s):
    sb, _, _ = scope(nc, ctx)
    s.ident, s.ones, s.negones = sb("ident", [P, P]), sb("ones", [P, P]), sb("negones", [P, P])
    s.zeros_r = sb("zeros_r", [P, N], F32R)
    s.sel = sb("sel", [2 * SGRP, SGRP, P], F32R)
    s.pick = sb("pick", [P, SGRP, SGRP])
    s.pick_r = sb("pick_r", [P, SGRP, SGRP], F32R)
    s.neghalf = sb("neghalf", [P, GRP])
    s.adj, s.adj_ne = sb("adj_sb", [P, P]), sb("adj_ne", [P, P])
    s.res_w, s.res_w_hi, s.res_w_lo = sb("res_w", [P, P]), sb("res_w_hi", [P, P], F32R), sb("res_w_lo", [P, P], F32R)
    s.b0, s.b2, s.b3 = sb("b0", [P, 1]), sb("b2", [P, 1]), sb("b3", [P, N])
    s.w_l, s.w_g, s.inv_s2 = sb("w_l", [P, 1]), sb("w_g", [P, 1]), sb("inv_s2", [P, 1])
    s.an_hi, s.an_lo = sb("an_hi", [P, CH, N], F32R), sb("an_lo", [P, CH, N], F32R)
    with ExitStack() as c2:
        sb, _, sem = scope(nc, c2)
        sel_a, sel_b = sb("sel_a", [2 * SGRP, SGRP, P]), sb("sel_b", [2 * SGRP, SGRP, P])
        filled, shaped = sem("c_filled"), sem("c_shaped")
        block = c2.enter_context(nc.Block())

        @block.gpsimd
        def _(pool):
            nc.gpsimd.memset(s.ident[:], 0.0).then_inc(filled, 1)
            nc.gpsimd.memset(s.ones[:], 1.0).then_inc(filled, 1)
            nc.gpsimd.memset(s.negones[:], -1.0).then_inc(filled, 1)
            nc.gpsimd.memset(s.neghalf[:], -0.5).then_inc(filled, 1)
            nc.gpsimd.memset(sel_a[:], 0.0).then_inc(filled, 1)
            nc.gpsimd.memset(sel_b[:], 0.0).then_inc(filled, 1)
            nc.gpsimd.memset(s.pick[:], 0.0).then_inc(filled, 1)
            pool.wait_ge(filled, 7)
            nc.gpsimd.affine_select(out=s.pick[:], in_=s.pick[:], compare_op=ALU.not_equal, fill=1.0,
                                    base=0, pattern=[[1, SGRP], [-1, SGRP]], channel_multiplier=0).then_inc(shaped, 1)
            nc.gpsimd.affine_select(out=s.ident[:], in_=s.ident[:], compare_op=ALU.not_equal, fill=1.0,
                                    base=0, pattern=[[-1, P]], channel_multiplier=1).then_inc(shaped, 1)
            for part, base in ((sel_a, 0), (sel_b, -SGRP)):
                nc.gpsimd.affine_select(out=part[:], in_=part[:], compare_op=ALU.not_equal, fill=1.0,
                                        base=base, pattern=[[-1, SGRP], [0, P]],
                                        channel_multiplier=1).then_inc(shaped, 1)

        @block.vector
        def _(dve):
            nc.vector.memset(s.zeros_r[:].bitcast(F32), 0.0)
            dve.wait_ge(shaped, 4)
            nc.vector.tensor_tensor(s.sel[:], sel_a[:], sel_b[:], ALU.add)
            nc.vector.tensor_copy(s.pick_r[:], s.pick[:])


def small_inputs(nc, s, sb, sem, adj, bias0, bias2, bias3, gate, log_sigma):
    gate_sb, lsig_sb, egate = sb("gate_sb", [P, 1]), sb("lsig_sb", [P, 1]), sb("egate", [P, 2])
    loaded, act_done, dve_done = sem("c_loaded"), sem("c_act_done"), sem("c_dve_done")

    def load(sp):
        sp.dma_start(s.adj[:], adj).then_inc(loaded, 16)
        sp.dma_start(s.b0[:], bias0.rearrange("(p a) -> p a", a=1)).then_inc(loaded, 16)
        sp.dma_start(s.b2[:], bias2.rearrange("(p a) -> p a", a=1)).then_inc(loaded, 16)
        sp.dma_start(s.b3[:], bias3.rearrange("(a n) -> a n", a=1).broadcast_to([P, N])).then_inc(loaded, 16)
        sp.dma_start(gate_sb[:], gate.broadcast_to([P, 1])).then_inc(loaded, 16)
        sp.dma_start(lsig_sb[:], log_sigma.broadcast_to([P, 1])).then_inc(loaded, 16)

    def exponentials(act):
        act.wait_ge(loaded, 96)
        nc.scalar.activation(egate[:, 0:1], gate_sb[:], ACT.Exp, scale=-1.0).then_inc(act_done, 1)
        nc.scalar.activation(s.inv_s2[:], lsig_sb[:], ACT.Exp, scale=-2.0).then_inc(act_done, 1)

    def shape(dve):
        dve.wait_ge(loaded, 96)
        nc.vector.scalar_tensor_tensor(out=s.adj_ne[:], in0=s.ident[:], scalar=-1.0, in1=s.ones[:],
                                       op0=ALU.mult, op1=ALU.add).then_inc(dve_done, 1)
        nc.vector.tensor_tensor(s.res_w[:], s.adj[:], s.adj[:], ALU.mult).then_inc(dve_done, 1)
        dve.wait_ge(dve_done, 2)
        nc.vector.tensor_tensor(s.adj_ne[:], s.adj_ne[:], s.adj[:], ALU.mult)
        nc.vector.tensor_tensor(s.res_w[:], s.res_w[:], s.ident[:], ALU.add).then_inc(dve_done, 1)
        dve.wait_ge(dve_done, 3)
        nc.vector.tensor_copy(s.res_w_hi[:], s.res_w[:]).then_inc(dve_done, 1)
        dve.wait_ge(dve_done, 4)
        nc.vector.tensor_tensor(s.res_w_lo[:], s.res_w[:], s.res_w_hi[:].bitcast(F32), ALU.subtract)
        dve.wait_ge(act_done, 2)
        nc.vector.tensor_scalar(egate[:, 1:2], egate[:, 0:1], 1.0, None, ALU.add).then_inc(dve_done, 1)
        dve.wait_ge(dve_done, 5)
        nc.vector.reciprocal(s.w_l[:], egate[:, 1:2]).then_inc(dve_done, 1)
        dve.wait_ge(dve_done, 6)
        nc.vector.tensor_scalar(s.w_g[:], s.w_l[:], -1.0, 1.0, ALU.mult, ALU.add)

    return load, exponentials, shape


def first_norms(nc, s, x, xres, n2, small):
    nb = x.shape[0]
    with ExitStack() as ctx:
        sb, ps, sem = scope(nc, ctx)
        sq = sb("sq", [P, 4, N])
        kept = sb("kept", [SGRP, nb // SGRP, N])
        sums = [ps(f"sums{k}") for k in range(2)]
        loaded = [sem(f"x_loaded{k}") for k in range(4)]
        squared, used, summed = sem("squared"), sem("used"), sem("summed")
        out, stored, passed = sem("out"), sem("stored"), sem("passed")
        xv = x.rearrange("b l n -> l b n")
        load_small, exponentials, shape_small = small_inputs(nc, s, sb, sem, *small)
        block = ctx.enter_context(nc.Block())
        turns = nb // SGRP

        @block.sync
        def _(sp):
            with sp.Fori(0, turns) as t:
                for k in range(4):
                    pair = sp.snap(8 * t + 2 * k)
                    sp.wait_ge(squared, 8 * t + 2 * k + 2)
                    sp.dma_start(xres[:, bass.ds(pair, 2), :], xv[:, bass.ds(pair, 2), :]).then_inc(loaded[k], 16)
            load_small(sp)
            sp.wait_ge(out, 2 + turns)
            sp.dma_start(n2.rearrange("(g j) n -> j g n", j=SGRP), kept[:]).then_inc(stored, 16)
            sp.wait_ge(stored, 16)

        def pairs_of_turns(eng, turn):
            with eng.Fori(0, turns // 2) as h:
                turn(2 * h, 0)
                turn(2 * h + 1, 1)
            if turns % 2:
                turn(turns - 1, 0)

        @block.scalar
        def _(act):
            def turn(t, bank):
                for k in range(SGRP):
                    if k % 2 == 0:
                        act.wait_ge(loaded[k // 2], 16 * (t + 1))
                    act.wait_ge(used, 8 * t + k + 1)
                    nc.scalar.activation(sq[:, k % 4, :], xres[:, bass.ds(8 * t + k, 1), :].rearrange("p a n -> p (a n)"),
                                         ACT.Square).then_inc(squared, 1)

            act.sem_inc(squared, 8)
            pairs_of_turns(act, turn)
            exponentials(act)

        @block.tensor
        def _(pe):
            def turn(t, bank):
                pe.wait_ge(out, t + 1)
                for k in range(SGRP):
                    pe.wait_ge(squared, 8 + 8 * t + k + 1)
                    mm = nc.tensor.matmul(sums[bank][0:SGRP, :], s.pick[:, k, :], sq[:, k % 4, :],
                                          start=(k == 0), stop=(k == SGRP - 1))
                    if k == SGRP - 1:
                        mm.then_inc(summed, 1)
                        pe.wait_ge(summed, t + 1)
                        pe.sem_inc(used, 1)
                    else:
                        mm.then_inc(used, 1)

            pe.sem_inc(used, 4)
            pairs_of_turns(pe, turn)

        @block.vector
        def _(dve):
            def turn(t, bank):
                dve.wait_ge(summed, t + 1)
                nc.vector.tensor_copy(kept[:, bass.ds(t, 1), :].rearrange("p a n -> p (a n)"),
                                      sums[bank][0:SGRP, :]).then_inc(out, 1)

            dve.sem_inc(out, 2)
            pairs_of_turns(dve, turn)
            shape_small(dve)


def norm_rows(nc, s, n2, rows, spill_hi, spill_lo):
    nb = n2.shape[0]
    w = nb * N // P
    flat = lambda dram: dram.rearrange("b n -> (b n)").rearrange("(p w) -> p w", w=w)
    with ExitStack() as ctx:
        sb, ps, sem = scope(nc, ctx)
        nrm, inv = sb("nrm", [P, w]), sb("inv", [P, w])
        r_hi, r_lo = sb("r_hi", [P, w], F32R), sb("r_lo", [P, w], F32R)
        loaded, rooted, dve_done, spilt, back = (sem(x) for x in ("n_loaded", "rooted", "r_dve", "spilt", "back"))
        block = ctx.enter_context(nc.Block())

        @block.scalar
        def _(act):
            act.wait_ge(loaded, 16)
            nc.scalar.activation(nrm[:], nrm[:], ACT.Sqrt).then_inc(rooted, 1)

        @block.vector
        def _(dve):
            dve.wait_ge(rooted, 1)
            nc.vector.tensor_scalar(nrm[:], nrm[:], NORM_EPS, None, ALU.max).then_inc(dve_done, 1)
            dve.wait_ge(dve_done, 1)
            nc.vector.reciprocal(inv[:], nrm[:]).then_inc(dve_done, 1)
            dve.wait_ge(dve_done, 2)
            nc.vector.tensor_copy(r_hi[:], inv[:]).then_inc(dve_done, 1)
            dve.wait_ge(dve_done, 3)
            nc.vector.tensor_tensor(r_lo[:], inv[:], r_hi[:].bitcast(F32), ALU.subtract).then_inc(dve_done, 1)

        @block.sync
        def _(sp):
            sp.dma_start(nrm[:], flat(n2)).then_inc(loaded, 16)
            sp.wait_ge(dve_done, 4)
            sp.dma_start(flat(spill_hi), r_hi[:].bitcast(F32)).then_inc(spilt, 16)
            sp.dma_start(flat(spill_lo), r_lo[:].bitcast(F32)).then_inc(spilt, 16)
            sp.wait_ge(spilt, 32)
            for k, spill in enumerate((spill_hi, spill_lo)):
                sp.dma_start(rows[k * SGRP:(k + 1) * SGRP].bitcast(F32),
                             spill.rearrange("(g j) n -> j g n", j=SGRP)).then_inc(back, 16)
            sp.wait_ge(back, 32)


def similarity(nc, s, xres, rows, hh, hl, source):
    nb = xres.shape[1]
    hh_at = [hh[0][:, 0:512], hh[1][:, 0:384], hh[2][:, 0:256], hh[1][:, 384:512]]
    with ExitStack() as ctx:
        sb, ps, sem = scope(nc, ctx)
        xn, hi, lo = sb("xn", [P, 4, N]), sb("xn_hi", [P, 4, N], F32R), sb("xn_lo", [P, 4, N], F32R)
        scale = ps("scale")
        loaded = [sem(f"x_loaded{k}") for k in range(4)]
        scale_ready, normed, hi_ready, lo_ready = (sem(x) for x in ("scale_ready", "normed", "hi_ready", "lo_ready"))
        summed = sem("summed")
        passed = sem("passed")
        block = ctx.enter_context(nc.Block())

        if source is not None:
            sv = source.rearrange("b l n -> l b n")

            @block.sync
            def _(sp):
                with sp.Fori(0, nb // 8) as t:
                    for k in range(4):
                        pair = sp.snap(8 * t + 2 * k)
                        sp.wait_ge(normed, 8 * t + 2 * k + 2)
                        sp.dma_start(xres[:, bass.ds(pair, 2), :], sv[:, bass.ds(pair, 2), :]).then_inc(loaded[k], 16)

        @block.vector
        def _(dve):
            dve.sem_inc(normed, 8)
            with dve.Fori(0, nb // SGRP) as t:
                for k in range(SGRP):
                    if source is not None and k % 2 == 0:
                        dve.wait_ge(loaded[k // 2], 16 * (t + 1))
                    dve.wait_ge(scale_ready, 8 * t + k + 1)
                    dve.wait_ge(summed, 8 * t + k + 1)
                    nc.vector.tensor_tensor(xn[:, k % 4, :],
                                            xres[:, bass.ds(8 * t + k, 1), :].rearrange("p a n -> p (a n)"),
                                            scale[:], ALU.mult).then_inc(normed, 1)

        @block.scalar
        def _(act):
            with act.Fori(0, nb // SGRP) as t:
                for k in range(SGRP):
                    act.wait_ge(normed, 8 + 8 * t + k + 1)
                    nc.scalar.activation(hi[:, k % 4, :], xn[:, k % 4, :], ACT.Copy).then_inc(hi_ready, 1)

        @block.gpsimd
        def _(pool):
            with pool.Fori(0, nb // SGRP) as t:
                for k in range(SGRP):
                    pool.wait_ge(hi_ready, 8 * t + k + 1)
                    nc.gpsimd.tensor_tensor(lo[:, k % 4, :], xn[:, k % 4, :], hi[:, k % 4, :].bitcast(F32),
                                            ALU.subtract).then_inc(lo_ready, 1)

        @block.tensor
        def _(pe):
            def spread(t, k):
                pe.wait_ge(normed, 8 + 8 * t + k)
                own_step(pe, passed)
                g = t + k // SGRP if k >= SGRP else t
                nc.tensor.matmul(scale[:], s.sel[:, k % SGRP, :], rows[:, bass.ds(g, 1), :].rearrange("p a n -> p (a n)"),
                                 start=True, stop=True).then_inc(scale_ready, 1)

            def sums(t, k):
                pe.wait_ge(hi_ready, 8 * t + k + 1)
                h, l = hi[:, k % 4, :], lo[:, k % 4, :]
                for c in range(CH):
                    nc.tensor.matmul(hh_at[c], h[:, c * P:(c + 1) * P], h[:, c * P:N], start=False, stop=False,
                                     skip_group_check=True)
                pe.wait_ge(lo_ready, 8 * t + k + 1)
                for c in range(CH):
                    mm = nc.tensor.matmul(hl[c][:], h[:, c * P:(c + 1) * P], l, start=False, stop=False,
                                          skip_group_check=True)
                mm.then_inc(summed, 1)

            pe.sem_inc(summed, 4)
            for bank in (*hh, *hl):
                nc.tensor.matmul(bank[:], s.zeros_r[:, 0:P], s.zeros_r[:], start=True, stop=False,
                                 skip_group_check=True)
            spread(0, 0)
            spread(0, 1)
            turns = nb // SGRP
            with pe.Fori(0, turns - 1) as t:
                for k in range(SGRP):
                    spread(t, k + 2)
                    sums(t, k)
            for k in range(SGRP):
                if k + 2 < SGRP:
                    spread(turns - 1, k + 2)
                sums(turns - 1, k)


def whole_similarity(nc, s, hh, hl, sim, work):
    nb = s.nb
    hh_at = [hh[0][:, 0:512], hh[1][:, 0:384], hh[2][:, 0:256], hh[1][:, 384:512]]
    with ExitStack() as ctx:
        sb, ps, sem = scope(nc, ctx)
        hl_sb, part = sb("hl_sb", [P, CH, N]), sb("part", [P, CH, N])
        turn = ps("turn")
        hl_out, parted, turned, upper, low_turned, lower = (
            sem(x) for x in ("hl_out", "parted", "turned", "upper", "low_turned", "lower"))
        masked, padded = sem("masked"), sem("padded")
        block = ctx.enter_context(nc.Block())

        @block.scalar
        def _(act):
            for c in range(CH):
                nc.scalar.activation(hl_sb[:, c, :], hl[c][:], ACT.Copy, scale=1.0 / nb).then_inc(hl_out, 1)
            for c in range(1, CH):
                act.wait_ge(low_turned, c)
                nc.scalar.activation(sim[:, c, 0:c * P], turn[:, 0:c * P], ACT.Copy).then_inc(lower, 1)

        @block.tensor
        def _(pe):
            pe.wait_ge(hl_out, CH)
            for c in range(CH):
                if c:
                    pe.wait_ge(upper, c)
                for j in range(c, CH):
                    mm = nc.tensor.transpose(turn[:, j * P:(j + 1) * P], hl_sb[:, j, c * P:(c + 1) * P], s.ident[:])
                mm.then_inc(turned, 1)
            pe.wait_ge(upper, CH)
            for c in range(1, CH):
                if c > 1:
                    pe.wait_ge(lower, c - 1)
                for j in range(c):
                    mm = nc.tensor.transpose(turn[:, j * P:(j + 1) * P], sim[:, j, c * P:(c + 1) * P], s.ident[:])
                mm.then_inc(low_turned, 1)

        @block.vector
        def _(dve):
            nc.vector.memset(work[:, :, 0:8], NEVER).then_inc(padded, 1)
            for c in range(CH):
                dve.wait_ge(hl_out, c + 1)
                nc.vector.scalar_tensor_tensor(out=part[:, c, c * P:N], in0=hh_at[c], scalar=1.0 / nb,
                                               in1=hl_sb[:, c, c * P:N], op0=ALU.mult,
                                               op1=ALU.add).then_inc(parted, 1)
            for c in range(CH):
                dve.wait_ge(turned, c + 1)
                dve.wait_ge(parted, c + 1)
                nc.vector.tensor_tensor(sim[:, c, c * P:N], turn[:, c * P:N], part[:, c, c * P:N],
                                        ALU.add).then_inc(upper, 1)
            dve.wait_ge(upper, CH)
            dve.wait_ge(lower, CH - 1)
            for c in range(CH):
                nc.vector.tensor_copy(work[:, c, 8:8 + N], sim[:, c, :]).then_inc(masked, 1)
            for c in range(CH):
                dve.wait_ge(masked, c + 1)
                nc.vector.scalar_tensor_tensor(out=work[:, c, 8 + c * P:8 + (c + 1) * P], in0=s.ident[:],
                                               scalar=NEVER, in1=sim[:, c, c * P:(c + 1) * P],
                                               op0=ALU.mult, op1=ALU.add)


def choose(nc, s, work, weights, xres):
    rounds, rest = TOP // 8, TOP % 8
    with ExitStack() as ctx:
        sb, ps, sem = scope(nc, ctx)
        best = sb("best", [P, CH, 8])
        found, marked, passed = sem("found"), sem("marked"), sem("passed")
        if weights is not None:
            w_dram, dst = weights
            raw = {k: sb(f"raw_{k}", [P, CH, N]) for k in w_dram}
            wo_t = sb("wo_t", [P, CH, N])
            tmp = sb("tmp", [P, 2, N])
            banks = [ps(f"prep{k}") for k in range(2)]
            w_loaded, made, out, hi_ready, lo_ready = (
                sem(x) for x in ("w_loaded", "made", "out", "w_hi_ready", "w_lo_ready"))
        block = ctx.enter_context(nc.Block())

        @block.vector
        def _(dve):
            def mark(c):
                nc.vector.match_replace(work[:, c, :], best[:, c, :], work[:, c, :], CHOSEN).then_inc(marked, 1)

            dve.sem_inc(marked, CH)
            with dve.Fori(0, rounds) as r:
                for c in range(CH):
                    dve.wait_ge(marked, CH * r + c + 1)
                    own_step(dve, passed)
                    nc.vector.max(best[:, c, :], work[:, c, :]).then_inc(found, 1)
                for c in range(CH):
                    dve.wait_ge(found, CH * r + c + 1)
                    own_step(dve, passed)
                    mark(c)
            if rest:
                for c in range(CH):
                    dve.wait_ge(marked, CH * rounds + c + 1)
                    nc.vector.max(best[:, c, :], work[:, c, :]).then_inc(found, 1)
                dve.wait_ge(found, CH * (rounds + 1))
                nc.vector.memset(best[:, :, rest:8], NEVER).then_inc(found, 1)
                dve.wait_ge(found, CH * (rounds + 1) + 1)
                for c in range(CH):
                    mark(c)

        if weights is None:
            nb = xres.shape[1]
            x_at = sb("x_at", [P, 4, N])
            xw_ps = [ps(f"xw_ps{k}") for k in range(4)]
            x_there, xw_made = sem("x_there"), sem("xw_made")

            @block.tensor
            def _(pe):
                with pe.Fori(0, nb // 4) as q:
                    for k in range(4):
                        pe.wait_ge(x_there, 4 * q + k + 1)
                        for c in range(CH):
                            mm = nc.tensor.matmul(xw_ps[k][:, c * P:(c + 1) * P], x_at[:, k, c * P:(c + 1) * P],
                                                  s.adj[:], start=True, stop=True)
                        mm.then_inc(xw_made, 1)

            @block.scalar
            def _(act):
                def batch(b):
                    return xres[:, bass.ds(b, 1), :].rearrange("p a n -> p (a n)")

                def bring(b, k):
                    nc.scalar.activation(x_at[:, k, :], batch(b), ACT.Copy).then_inc(x_there, 1)

                def take(b, k):
                    act.wait_ge(xw_made, b + 1)
                    nc.scalar.activation(batch(b), xw_ps[k][:], ACT.Copy)

                for k in range(4):
                    bring(k, k)
                with act.Fori(0, nb // 4 - 1) as q:
                    for k in range(4):
                        take(4 * q + k, k)
                        bring(4 * q + 4 + k, k)
                for k in range(4):
                    take(nb - 4 + k, k)

            return

        jobs = [("turn", None, c) for c in range(CH)]
        jobs += [(name, name, c) for name in ("lang", "grav") for c in range(CH)]
        jobs += [("ov", "ov", c) for c in range(CH)]

        @block.sync
        def _(sp):
            for k in w_dram:
                sp.dma_start(raw[k][:], w_dram[k].rearrange("(c p) n -> p c n", p=P)).then_inc(w_loaded, 16)

        @block.tensor
        def _(pe):
            pe.wait_ge(w_loaded, 16 * len(w_dram))
            for n, (kind, _, c) in enumerate(jobs):
                bank = banks[n % 2]
                if n >= 2:
                    pe.wait_ge(out, n - 1)
                if kind == "turn":
                    for j in range(CH):
                        mm = nc.tensor.transpose(bank[:, j * P:(j + 1) * P], raw["o"][:, j, c * P:(c + 1) * P], s.ident[:])
                elif kind == "ov":
                    for j in range(CH):
                        mm = nc.tensor.matmul(bank[:], raw["v"][:, j, c * P:(c + 1) * P], wo_t[:, j, :],
                                              start=(j == 0), stop=(j == CH - 1))
                else:
                    for j in range(CH):
                        mm = nc.tensor.matmul(bank[:, 0:N - c * P], raw[kind][:, j, c * P:(c + 1) * P],
                                              raw[kind][:, j, c * P:N], start=(j == 0), stop=(j == CH - 1))
                mm.then_inc(made, 1)

        @block.scalar
        def _(act):
            k = 0
            for n, (kind, name, c) in enumerate(jobs):
                bank = banks[n % 2]
                act.wait_ge(made, n + 1)
                if kind == "turn":
                    nc.scalar.activation(wo_t[:, c, :], bank[:], ACT.Copy).then_inc(out, 1)
                    continue
                w = N - c * P if name != "ov" else N
                if k >= 2:
                    act.wait_ge(lo_ready, k - 1)
                if name == "ov":
                    nc.scalar.activation(tmp[:, k % 2, :], bank[:], ACT.Copy).then_inc(out, 1)
                    d = dst[name][0][:, c, :]
                else:
                    if w > P:
                        nc.scalar.activation(tmp[:, k % 2, P:w], bank[:, P:w], ACT.Copy)
                    nc.scalar.activation(tmp[:, k % 2, 0:P], bank[:, 0:P], ACT.Copy, scale=0.5).then_inc(out, 1)
                    d = dst[name][0][:, TRI[c]:TRI[c] + w]
                act.wait_ge(out, n + 1)
                nc.scalar.activation(d, tmp[:, k % 2, 0:w], ACT.Copy).then_inc(hi_ready, 1)
                k += 1

        @block.gpsimd
        def _(pool):
            k = 0
            for kind, name, c in jobs:
                if kind == "turn":
                    continue
                w = N - c * P if name != "ov" else N
                d = [x[:, c, :] if name == "ov" else x[:, TRI[c]:TRI[c] + w] for x in dst[name]]
                pool.wait_ge(hi_ready, k + 1)
                nc.gpsimd.tensor_tensor(d[1], tmp[:, k % 2, 0:w], d[0].bitcast(F32),
                                        ALU.subtract).then_inc(lo_ready, 1)
                k += 1


def normal_adjacency(nc, s, sim, work):
    with ExitStack() as ctx:
        sb, ps, sem = scope(nc, ctx)
        a, an, diag = sb("a", [P, CH, N]), sb("an", [P, CH, N]), sb("diag", [P, CH, P])
        deg, pos, dinv = sb("deg", [P, CH]), sb("pos", [P, CH]), sb("dinv", [P, CH])
        deg_ps, row = ps("deg_ps", [P, CH]), ps("row")
        chosen, summed, dve_done, rooted, spread, hi_ready = (
            sem(x) for x in ("chosen", "deg_summed", "n_dve", "n_rooted", "spread", "n_hi"))
        block = ctx.enter_context(nc.Block())

        @block.vector
        def _(dve):
            for c in range(CH):
                nc.vector.scalar_tensor_tensor(out=a[:, c, :], in0=work[:, c, 8:8 + N], scalar=CHOSEN,
                                               in1=sim[:, c, :], op0=ALU.is_equal,
                                               op1=ALU.mult).then_inc(chosen, 1)
            dve.wait_ge(summed, 1)
            nc.vector.tensor_scalar(deg[:], deg_ps[:], 1e-37, None, ALU.max).then_inc(dve_done, 1)
            nc.vector.tensor_scalar(pos[:], deg_ps[:], 0.0, None, ALU.is_gt).then_inc(dve_done, 1)
            dve.wait_ge(dve_done, 2)
            dve.wait_ge(rooted, 1)
            nc.vector.tensor_tensor(dinv[:], dinv[:], pos[:], ALU.mult).then_inc(dve_done, 1)
            dve.wait_ge(dve_done, 3)
            nc.vector.tensor_tensor(diag[:], over(s.ident[:], CH), along(dinv[:], P), ALU.mult).then_inc(dve_done, 1)
            dve.wait_ge(spread, 1)
            for c in range(CH):
                nc.vector.scalar_tensor_tensor(out=an[:, c, :], in0=a[:, c, :], scalar=dinv[:, c:c + 1],
                                               in1=row[:], op0=ALU.mult, op1=ALU.mult).then_inc(dve_done, 1)
            for c in range(CH):
                dve.wait_ge(hi_ready, c + 1)
                nc.vector.tensor_tensor(s.an_lo[:, c, :], an[:, c, :], s.an_hi[:, c, :].bitcast(F32), ALU.subtract)

        @block.gpsimd
        def _(pool):
            pool.wait_ge(dve_done, 2)
            nc.gpsimd.tensor_tensor(dinv[:], deg[:], s.neghalf[:], ALU.pow).then_inc(rooted, 1)

        @block.tensor
        def _(pe):
            for c in range(CH):
                pe.wait_ge(chosen, c + 1)
                for j in range(CH):
                    mm = nc.tensor.matmul(deg_ps[:, j:j + 1], a[:, c, j * P:(j + 1) * P], s.ones[:, 0:1],
                                          start=(c == 0 and j == 0), stop=(c == CH - 1 and j == CH - 1),
                                          skip_group_check=True)
            mm.then_inc(summed, 1)
            pe.wait_ge(dve_done, 4)
            nc.tensor.matmul(row[:], s.ones[:], diag[:].rearrange("p c n -> p (c n)"),
                             start=True, stop=True).then_inc(spread, 1)

        @block.scalar
        def _(act):
            for c in range(CH):
                act.wait_ge(dve_done, 5 + c)
                nc.scalar.activation(s.an_hi[:, c, :], an[:, c, :], ACT.Copy).then_inc(hi_ready, 1)


def first(g):
    return isinstance(g, int) and g == 0


def statistics(nc, dve, y, stats, mean_var, var_eps, neg_mean, y_ok, stats_ok, n, passed):
    dve.wait_ge(y_ok, n)
    nc.vector.bn_stats(stats, y).then_inc(stats_ok, 1)
    dve.wait_ge(stats_ok, 3 * n - 2)
    own_step(dve, passed)
    nc.vector.bn_aggr(mean_var, stats).then_inc(stats_ok, 1)
    dve.wait_ge(stats_ok, 3 * n - 1)
    nc.vector.tensor_scalar(var_eps, mean_var[:, 1:2], LN_EPS, None, ALU.add)
    nc.vector.tensor_scalar(neg_mean, mean_var[:, 0:1], -1.0, None, ALU.mult).then_inc(stats_ok, 1)


def inverse_root(nc, pool, root, bias, var_eps, neg_mean, neghalf, stats_ok, root_ok, n):
    pool.wait_ge(stats_ok, 3 * n)
    nc.gpsimd.tensor_tensor(root, var_eps, neghalf, ALU.pow).then_inc(root_ok, 1)
    pool.wait_ge(root_ok, 2 * n - 1)
    nc.gpsimd.tensor_tensor(bias, neg_mean, root, ALU.mult).then_inc(root_ok, 1)


HILO = [(0, 0), (0, 1), (1, 0)]


def gnn_layer_pair(nc, s, x, out, u_l, u_g, wov, n2):
    nb = x.shape[0]
    groups = nb // GRP
    with ExitStack() as ctx:
        sb, ps, sem = scope(nc, ctx)
        xin = sb("xin", [P, GRP, N])
        xw_hi, xw_lo = sb("xw_hi", [P, 2, N], F32R), sb("xw_lo", [P, 2, N], F32R)
        ya, xa, xb = sb("ya", [P, 2, N]), sb("xa", [P, GRP, N]), sb("xb", [P, GRP, N])
        st_a, mv_a = sb("st_a", [P, 2, 6]), sb("mv_a", [P, 2, 2])
        ve_a, nm_a, rs_a, nb_a = (sb(n, [P, 2]) for n in ("ve_a", "nm_a", "rs_a", "nb_a"))
        ht = [sb(f"ht_{p}", [P, CH, GRP, P], F32R) for p in ("hi", "lo")]
        y = [sb(f"y_{p}", [P, 2, GRP, 2, P], F32R) for p in ("hi", "lo")]
        v = [sb(f"v_{p}", [P, GRP, N], F32R) for p in ("hi", "lo")]
        m = sb("m", [P, GRP, 2, P])
        prod = sb("prod", [P, GRP, 2, P])
        mnn, q_l, r_l = sb("mnn", [P, GRP, 2]), sb("q_l", [P, GRP]), sb("r_l", [P, GRP])
        dg_r = sb("dg_r", [P, GRP, P])
        a_l, a_g = sb("a_l", [P, GRP, P]), sb("a_g", [P, GRP, P])
        k_l, k_g = sb("k_l", [P, GRP, P]), sb("k_g", [P, GRP, P])
        deg, small = sb("deg_lg", [P, 2, GRP]), sb("small", [P, 8, GRP])
        kt = [sb(f"kt_{p}", [P, GRP, P], F32R) for p in ("hi", "lo")]
        xo = sb("xo", [P, GRP, N])
        sq_hi, sq_lo = sb("sq_hi", [P, GRP, N], F32R), sb("sq_lo", [P, GRP, N], F32R)
        sq = sb("sq2", [P, GRP, N])
        st_b, mv_b = sb("st_b", [P, GRP, 6]), sb("mv_b", [P, GRP, 2])
        ve_b, nm_b, rs_b, nb_b = (sb(n, [P, GRP]) for n in ("ve_b", "nm_b", "rs_b", "nb_b"))
        sums = sb("sums", [GRP, N])

        tr, yp, mp = [ps("tr0"), ps("tr1")], [ps("y_l"), ps("y_g")], [ps("m0"), ps("m1")]
        ht_ps = xw_ps, l0_ps = ps("xw_ps"), ps("l0_ps")

        x_loaded = [sem(f"x_in{i}") for i in range(GRP)]
        xw_made, xw_hi_ok, xw_lo_ok, l0_made = (sem(n) for n in ("xw_made", "xw_hi_ok", "xw_lo_ok", "l0_made"))
        ya_ok, st_a_ok, rs_a_ok, xa_ok, xb_ok = (
            sem(n) for n in ("ya_ok", "st_a_ok", "rs_a_ok", "xa_ok", "xb_ok"))
        ht_made, ht_hi_ok, ht_lo_ok = (sem(n) for n in ("ht_made", "ht_hi_ok", "ht_lo_ok"))
        y_made, y_hi_ok, y_lo_ok = (sem(n) for n in ("y_made", "y_hi_ok", "y_lo_ok"))
        m_made, m_ok, v_made, v_hi_ok, v_lo_ok = (sem(n) for n in ("m_made", "m_ok", "v_made", "v_hi_ok", "v_lo_ok"))
        prod_ok, mnn_ok, q_ok, r_ok, dgr_ok, ml_t, mg_t, r_row = (
            sem(n) for n in ("prod_ok", "mnn_ok", "q_ok", "r_ok", "dgr_ok", "ml_t", "mg_t", "r_row"))
        sl_ok, ul_ok, kl_ok, tg_ok, cl_ok, eg_ok, kg_ok, sm_ok, ka_ok, k_ok = (
            sem(n) for n in ("sl_ok", "ul_ok", "kl_ok", "tg_ok", "cl_ok", "eg_ok", "kg_ok", "sm_ok", "ka_ok", "k_ok"))
        kt_made, kt_hi_ok, kt_lo_ok, l1_made = (sem(n) for n in ("kt_made", "kt_hi_ok", "kt_lo_ok", "l1_made"))
        yb_ok, st_b_ok, rs_b_ok, xo_ok, sq_ok = (
            sem(n) for n in ("yb_ok", "st_b_ok", "rs_b_ok", "xo_ok", "sq_ok"))
        sq_hi_ok, sq_lo_ok = sem("sq_hi_ok"), sem("sq_lo_ok")
        cf_ok, sg_ok = sem("cf_ok"), sem("sg_ok")
        n2_made, n2_out, n2_stored = sem("n2_made"), sem("n2_out"), sem("n2_stored")
        stored = [sem(f"stored{i}") for i in range(GRP)]
        passed = sem("passed")
        block = ctx.enter_context(nc.Block())

        def turns(eng, turn):
            turn(None, None, 0)
            turn(None, 0, 1)
            with eng.Fori(0, groups - 2) as gp:
                turn(gp, gp + 1, gp + 2)
            turn(groups - 2, groups - 1, None)
            turn(groups - 1, None, None)

        @block.sync
        def _(sp):
            def load(b, i):
                sp.dma_start(xin[:, i, :], x[bass.ds(b, 1)].rearrange("a p n -> p (a n)")).then_inc(x_loaded[i], 16)

            def store(b, i):
                sp.dma_start(out[bass.ds(b, 1)].rearrange("a p n -> p (a n)"), xo[:, i, :]).then_inc(stored[i], 16)

            def turn(gp, ga):
                for kind, i in (("store", 0), ("store", 1), ("load", 0), ("store", 2), ("store", 3),
                                ("load", 1), ("load", 2), ("load", 3)):
                    if kind == "load" and ga is not None:
                        at = sp.snap(GRP * (ga + 1) + i)
                        sp.wait_ge(ya_ok, GRP * ga + i + 1)
                        load(at, i)
                    elif kind == "store" and gp is not None:
                        at = sp.snap(GRP * gp + i)
                        sp.wait_ge(xo_ok, GRP * gp + i + 1)
                        store(at, i)
                if gp is not None:
                    at = sp.snap(GRP * gp)
                    sp.wait_ge(n2_out, 1 + gp + 1)
                    sp.dma_start(n2[bass.ds(at, GRP), :], sums[:]).then_inc(n2_stored, 16)

            for i in range(GRP):
                load(i, i)
            turn(None, 0)
            turn(None, 1)
            with sp.Fori(0, groups - 3) as gp:
                turn(gp, gp + 2)
            for gp in range(groups - 3, groups):
                turn(gp, None)
            for i in range(GRP):
                sp.wait_ge(stored[i], 16 * (groups + 1))
            sp.wait_ge(n2_stored, 16 * (groups + 1))

        @block.tensor
        def _(pe):
            def turn(gp, g, ga):
                def hturn(i):
                    pe.wait_ge(xa_ok, GRP * ga + i + 1)
                    if i == 0:
                        pe.wait_ge(xw_lo_ok, 1 + GRP * (ga + 1))
                    elif i == 1:
                        pe.wait_ge(ya_ok, GRP * (ga + 1))
                    else:
                        pe.wait_ge(ht_lo_ok, GRP * ga + i - 1)
                    for c in range(CH):
                        mm = nc.tensor.transpose(ht_ps[i % 2][:, c * P:(c + 1) * P], xa[:, i, c * P:(c + 1) * P], s.ident[:])
                    mm.then_inc(ht_made, 1)

                def xw(i):
                    pe.wait_ge(x_loaded[i], 16 * (ga + 1))
                    pe.wait_ge(xw_lo_ok, GRP * ga + i + 1)
                    if i == 0 and not first(ga):
                        pe.wait_ge(ht_lo_ok, GRP * ga - 1)
                    for c in range(CH):
                        mm = nc.tensor.matmul(xw_ps[:, c * P:(c + 1) * P], xin[:, i, c * P:(c + 1) * P], s.adj[:],
                                              start=True, stop=True)
                    mm.then_inc(xw_made, 1)

                def l0(i):
                    pe.wait_ge(xw_hi_ok, GRP * ga + i + 1)
                    pe.wait_ge(xw_lo_ok, 1 + GRP * ga + i + 1)
                    if not first(ga) or i:
                        pe.wait_ge(ya_ok, GRP * ga + i)
                    if i == 0 and not first(ga):
                        pe.wait_ge(ht_lo_ok, GRP * ga)
                    xwp, anp = (xw_hi, xw_lo), (s.an_hi, s.an_lo)
                    for c in range(CH):
                        for n, (a, b) in enumerate(HILO):
                            mm = nc.tensor.matmul(l0_ps[:], xwp[a][:, i % 2, c * P:(c + 1) * P], anp[b][:, c, :],
                                                  start=(c == 0 and n == 0), stop=(c == CH - 1 and n == 2))
                    mm.then_inc(l0_made, 1)

                def yprod(c):
                    if c == 0:
                        pe.wait_ge(ht_hi_ok, GRP * (g + 1))
                        pe.wait_ge(ht_lo_ok, GRP * (g + 1))
                    for k, u in enumerate((u_l, u_g)):
                        if c == 0:
                            pe.wait_ge(v_lo_ok, GRP * (g + 1))
                        else:
                            pe.wait_ge(y_lo_ok, 8 * g + 2 * (c - 1) + k + 1)
                        for r in range(c + 1):
                            for n, (a, b) in enumerate(HILO):
                                at = TRI[r] + (c - r) * P
                                mm = nc.tensor.matmul(yp[k][:], u[a][:, at:at + P],
                                                      ht[b][:, r, :, :].rearrange("p i n -> p (i n)"),
                                                      start=(r == 0 and n == 0), stop=(r == c and n == 2))
                        mm.then_inc(y_made, 1)

                def mprod(c):
                    pe.wait_ge(y_hi_ok, 8 * g + 2 * (c + 1))
                    pe.wait_ge(y_lo_ok, 8 * g + 2 * (c + 1))
                    if c == 0:
                        pe.wait_ge(yb_ok, GRP * (g + 1))
                    for i in range(GRP):
                        for n, (a, b) in enumerate(HILO):
                            mm = nc.tensor.matmul(mp[i // 2][:, (i % 2) * 256:(i % 2) * 256 + 256], ht[a][:, c, i, :],
                                                  y[b][:, c % 2, i, :, :].rearrange("p k n -> p (k n)"),
                                                  start=(c == 0 and n == 0 and i % 2 == 0),
                                                  stop=(c == CH - 1 and n == 2), skip_group_check=True)
                    mm.then_inc(m_made, 1)

                def vprod(i):
                    if i < 2:
                        pe.wait_ge(y_lo_ok, 8 * g + 6 + i + 1)
                    else:
                        pe.wait_ge(v_lo_ok, GRP + GRP * g + i - 1)
                    for c in range(CH):
                        for n, (a, b) in enumerate(HILO):
                            mm = nc.tensor.matmul(yp[i % 2][:], ht[a][:, c, i, :], wov[b][:, c, :],
                                                  start=(c == 0 and n == 0), stop=(c == CH - 1 and n == 2))
                    mm.then_inc(v_made, 1)

                def m_l_turned():
                    pe.wait_ge(m_ok, 2 * (g + 1))
                    pe.wait_ge(kt_lo_ok, g + 1)
                    for i in range(GRP):
                        mm = nc.tensor.transpose(tr[0][:, i * P:(i + 1) * P], m[:, i, 0, :], s.ident[:])
                    mm.then_inc(ml_t, 1)

                def m_g_turned():
                    pe.wait_ge(prod_ok, g + 1)
                    if gp is not None:
                        pe.wait_ge(n2_out, gp + 1)
                    for i in range(GRP):
                        nc.tensor.matmul(tr[1][:, i * P:(i + 1) * P], m[:, i, 1, :], s.ident[:],
                                         start=(i == 0), stop=False, skip_group_check=True)
                    nc.tensor.matmul(tr[1][:], s.negones[:], prod[:, :, 1, :],
                                     start=False, stop=True, skip_group_check=True).then_inc(mg_t, 1)

                def r_rows():
                    pe.wait_ge(dgr_ok, g + 1)
                    nc.tensor.matmul(mp[0][:], s.ones[:], dg_r[:].rearrange("p i n -> p (i n)"),
                                     start=True, stop=True).then_inc(r_row, 1)

                def k_turned():
                    pe.wait_ge(k_ok, GRP * (gp + 1))
                    for i in range(GRP):
                        mm = nc.tensor.transpose(tr[0][:, i * P:(i + 1) * P], k_g[:, i, :], s.ident[:])
                    mm.then_inc(kt_made, 1)

                def l1(i):
                    if i == 0:
                        pe.wait_ge(kt_hi_ok, gp + 1)
                        pe.wait_ge(kt_lo_ok, 1 + gp + 1)
                    if i >= 2:
                        pe.wait_ge(yb_ok, GRP + GRP * gp + i - 1)
                    for n, (a, b) in enumerate(HILO):
                        mm = nc.tensor.matmul(mp[i % 2][:], kt[a][:, i, :], v[b][:, i, :], start=(n == 0), stop=(n == 2))
                    mm.then_inc(l1_made, 1)

                def squares(half):
                    pe.wait_ge(sq_lo_ok, GRP * gp + 2 * half + 2)
                    for i in (2 * half, 2 * half + 1):
                        for n, part in enumerate((sq_hi, sq_lo)):
                            mm = nc.tensor.matmul(tr[1][0:GRP, :], s.pick_r[:, i, 0:GRP], part[:, i, :],
                                                  start=(i == 0 and n == 0), stop=(i == GRP - 1 and n == 1))
                    if half:
                        mm.then_inc(n2_made, 1)

                A, B, C = ga is not None, g is not None, gp is not None
                if A:
                    xw(0)
                if B:
                    yprod(0)
                if A:
                    l0(0)
                    xw(1)
                if C:
                    k_turned()
                if B:
                    yprod(1)
                if C:
                    l1(0)
                    l1(1)
                if A:
                    l0(1)
                if C:
                    l1(2)
                    l1(3)
                if A:
                    xw(2)
                if B:
                    yprod(2)
                    mprod(0)
                if A:
                    l0(2)
                if B:
                    mprod(1)
                if A:
                    xw(3)
                if B:
                    yprod(3)
                if A:
                    l0(3)
                if B:
                    mprod(2)
                if B:
                    vprod(0)
                    mprod(3)
                    vprod(1)
                if A:
                    hturn(0)
                if B:
                    m_l_turned()
                    m_g_turned()
                    vprod(2)
                if A:
                    hturn(1)
                if B:
                    r_rows()
                    vprod(3)
                    pe.wait_ge(tg_ok, GRP * (g + 1))
                if A:
                    hturn(2)
                if C:
                    squares(0)
                if A:
                    hturn(3)
                if C:
                    squares(1)

            turns(pe, turn)

        @block.scalar
        def _(act):
            copy = lambda o, i: nc.scalar.activation(o, i, ACT.Copy)

            def turn(gp, g, ga):
                def ht_hi(i):
                    act.wait_ge(ht_made, GRP * ga + i + 1)
                    act.wait_ge(v_made, GRP * ga + i + 1)
                    act.wait_ge(m_made, 2 + GRP * ga)
                    copy(ht[0][:, :, i, :], ht_ps[i % 2][:].rearrange("p (c n) -> p c n", c=CH)).then_inc(ht_hi_ok, 1)

                def xw_hi_(i):
                    act.wait_ge(xw_made, GRP * ga + i + 1)
                    act.wait_ge(l0_made, GRP * ga + i + 1)
                    copy(xw_hi[:, i % 2, :], xw_ps[:]).then_inc(xw_hi_ok, 1)

                def norm_a(i):
                    act.wait_ge(rs_a_ok, 2 * (GRP * ga + i + 1))
                    act.wait_ge(xb_ok, GRP * ga + i + 1)
                    nc.scalar.activation(xa[:, i, :], ya[:, i % 2, :], ACT.Identity, scale=rs_a[:, i % 2:i % 2 + 1],
                                         bias=nb_a[:, i % 2:i % 2 + 1]).then_inc(xa_ok, 1)

                def y_hi(c):
                    for k in range(2):
                        act.wait_ge(y_made, 8 * g + 2 * c + k + 1)
                        act.wait_ge(m_made, CH * g + c + 1)
                        copy(y[0][:, c % 2, :, k, :], yp[k][:].rearrange("p (i n) -> p i n", i=GRP)).then_inc(y_hi_ok, 1)

                def v_hi(i):
                    act.wait_ge(v_made, GRP + GRP * g + i + 1)
                    copy(v[0][:, i, :], yp[i % 2][:]).then_inc(v_hi_ok, 1)

                def m_out():
                    act.wait_ge(m_made, 2 + CH * (g + 1))
                    for k in range(2):
                        copy(m[:, 2 * k:2 * k + 2, :, :].rearrange("p i k n -> p (i k n)"), mp[k][:]).then_inc(m_ok, 1)

                def exp_g():
                    act.wait_ge(cl_ok, g + 1)
                    nc.scalar.activation(a_g[:], a_g[:], ACT.Exp, scale=s.inv_s2[:, 0:1]).then_inc(eg_ok, 1)

                def kt_hi():
                    act.wait_ge(kt_made, gp + 1)
                    copy(kt[0][:].rearrange("p i n -> p (i n)"), tr[0][:]).then_inc(kt_hi_ok, 1)

                def norm_b(i):
                    act.wait_ge(rs_b_ok, 2 * (GRP * gp + i + 1))
                    nc.scalar.activation(xo[:, i, :], xo[:, i, :], ACT.Identity, scale=rs_b[:, i:i + 1],
                                         bias=nb_b[:, i:i + 1]).then_inc(xo_ok, 1)

                def square(i):
                    act.wait_ge(xo_ok, GRP * gp + i + 1)
                    nc.scalar.activation(sq[:, i, :], xo[:, i, :], ACT.Square).then_inc(sq_ok, 1)
                    act.wait_ge(sq_ok, GRP * gp + i + 1)
                    copy(sq_hi[:, i, :], sq[:, i, :]).then_inc(sq_hi_ok, 1)

                def sums_out():
                    act.wait_ge(n2_made, gp + 1)
                    act.wait_ge(n2_stored, 16 * (gp + 1))
                    copy(sums[:], tr[1][0:GRP, :]).then_inc(n2_out, 1)

                A, B, C = ga is not None, g is not None, gp is not None
                if A:
                    xw_hi_(0)
                if B:
                    y_hi(0)
                if A:
                    xw_hi_(1)
                if C:
                    kt_hi()
                if B:
                    y_hi(1)
                if C:
                    norm_b(0)
                    norm_b(1)
                if A:
                    xw_hi_(2)
                    norm_a(0)
                if C:
                    square(0)
                    square(1)
                    norm_b(2)
                    norm_b(3)
                if B:
                    y_hi(2)
                if A:
                    norm_a(1)
                if C:
                    square(2)
                    square(3)
                if A:
                    xw_hi_(3)
                if B:
                    y_hi(3)
                if A:
                    norm_a(2)
                if B:
                    v_hi(0)
                    m_out()
                if A:
                    norm_a(3)
                if B:
                    v_hi(1)
                if A:
                    ht_hi(0)
                if B:
                    v_hi(2)
                    exp_g()
                if A:
                    ht_hi(1)
                if B:
                    v_hi(3)
                if A:
                    ht_hi(2)
                    ht_hi(3)
                if C:
                    sums_out()

            act.sem_inc(l0_made, 2)
            act.sem_inc(m_made, 2)
            act.sem_inc(v_made, GRP)
            act.sem_inc(n2_out, 1)
            act.sem_inc(n2_stored, 16)
            for i in range(GRP):
                act.sem_inc(stored[i], 16)
            turns(act, turn)

        @block.gpsimd
        def _(pool):
            def turn(gp, g, ga):
                def keep(i):
                    if g is None:
                        return
                    pool.wait_ge(xa_ok, GRP * g + i + 1)
                    pool.wait_ge(yb_ok, GRP * g + i + 1)
                    own_step(pool, passed)
                    nc.gpsimd.tensor_copy(xb[:, i, :], xa[:, i, :]).then_inc(xb_ok, 1)

                def root_a(i):
                    j = slice(i % 2, i % 2 + 1)
                    if ga is not None:
                        inverse_root(nc, pool, rs_a[:, j], nb_a[:, j], ve_a[:, j], nm_a[:, j],
                                     s.neghalf[:, 0:1], st_a_ok, rs_a_ok, GRP * ga + i + 1)

                def root_b(i):
                    j = slice(i, i + 1)
                    if gp is not None:
                        inverse_root(nc, pool, rs_b[:, j], nb_b[:, j], ve_b[:, j], nm_b[:, j],
                                     s.neghalf[:, 0:1], st_b_ok, rs_b_ok, GRP * gp + i + 1)

                root_a(0)
                root_b(0)
                root_b(1)
                keep(0)
                root_a(1)
                root_b(2)
                root_b(3)
                keep(1)
                keep(2)
                keep(3)
                root_a(2)
                if gp is not None:
                    for i in range(GRP):
                        pool.wait_ge(sq_hi_ok, GRP * gp + i + 1)
                        nc.gpsimd.tensor_tensor(sq_lo[:, i, :], sq[:, i, :], sq_hi[:, i, :].bitcast(F32),
                                                ALU.subtract).then_inc(sq_lo_ok, 1)
                root_a(3)
                if g is not None:
                    pool.wait_ge(q_ok, g + 1)
                    nc.gpsimd.tensor_tensor(r_l[:], q_l[:], s.neghalf[:], ALU.pow).then_inc(r_ok, 1)

            pool.sem_inc(xb_ok, GRP)
            turns(pool, turn)

        @block.vector
        def _(dve):
            def lo_part(lo, full, hi, done):
                nc.vector.tensor_tensor(lo, full, hi.bitcast(F32), ALU.subtract).then_inc(done, 1)

            def turn(gp, g, ga):
                def ht_lo(i):
                    dve.wait_ge(ht_hi_ok, GRP * ga + i + 1)
                    lo_part(ht[1][:, :, i, :], ht_ps[i % 2][:].rearrange("p (c n) -> p c n", c=CH), ht[0][:, :, i, :], ht_lo_ok)

                def xw_lo_(i):
                    dve.wait_ge(xw_hi_ok, GRP * ga + i + 1)
                    lo_part(xw_lo[:, i % 2, :], xw_ps[:], xw_hi[:, i % 2, :], xw_lo_ok)

                def residual_a(i):
                    dve.wait_ge(l0_made, 2 + GRP * ga + i + 1)
                    if not first(ga) or i >= 2:
                        dve.wait_ge(xa_ok, GRP * ga + i - 1)
                    nc.vector.scalar_tensor_tensor(out=ya[:, i % 2, :], in0=l0_ps[:], scalar=s.b0[:, 0:1],
                                                   in1=xin[:, i, :], op0=ALU.add, op1=ALU.add).then_inc(ya_ok, 1)

                def stats_a(i):
                    j = slice(i % 2, i % 2 + 1)
                    statistics(nc, dve, ya[:, i % 2, :], st_a[:, i % 2, :], mv_a[:, i % 2, :], ve_a[:, j], nm_a[:, j],
                               ya_ok, st_a_ok, GRP * ga + i + 1, passed)

                def y_lo(c):
                    for k in range(2):
                        dve.wait_ge(y_hi_ok, 8 * g + 2 * c + k + 1)
                        lo_part(y[1][:, c % 2, :, k, :], yp[k][:].rearrange("p (i n) -> p i n", i=GRP),
                                y[0][:, c % 2, :, k, :], y_lo_ok)

                def v_lo(i):
                    dve.wait_ge(v_hi_ok, GRP * g + i + 1)
                    lo_part(v[1][:, i, :], yp[i % 2][:], v[0][:, i, :], v_lo_ok)

                def diagonals():
                    dve.wait_ge(m_ok, 2 * (g + 1))
                    m8 = m[:].rearrange("p i k n -> p (i k) n")
                    nc.vector.tensor_tensor(prod[:].rearrange("p i k n -> p (i k) n"), m8, over(s.ident[:], 2 * GRP),
                                            ALU.mult).then_inc(prod_ok, 1)
                    dve.wait_ge(prod_ok, g + 1)
                    nc.vector.tensor_reduce(mnn[:].rearrange("p i k -> p (i k)"),
                                            prod[:].rearrange("p i k n -> p (i k) n"), AX.X, ALU.add).then_inc(mnn_ok, 1)
                    dve.wait_ge(mnn_ok, g + 1)
                    nc.vector.tensor_scalar(q_l[:], mnn[:, :, 0], 2.0, EPS * EPS, ALU.mult, ALU.max).then_inc(q_ok, 1)

                def diag_r():
                    dve.wait_ge(r_ok, g + 1)
                    nc.vector.tensor_tensor(dg_r[:], over(s.ident[:], GRP), along(r_l[:], P), ALU.mult).then_inc(dgr_ok, 1)

                def metric_l():
                    dve.wait_ge(ml_t, g + 1)
                    nc.vector.tensor_tensor(a_l[:], m[:, :, 0, :], tr[0][:].rearrange("p (i n) -> p i n", i=GRP),
                                            ALU.add).then_inc(sl_ok, 1)

                def kernel_l():
                    dve.wait_ge(r_row, g + 1)
                    dve.wait_ge(sl_ok, g + 1)
                    flat = a_l[:].rearrange("p i n -> p (i n)")
                    nc.vector.scalar_tensor_tensor(out=flat, in0=flat, scalar=0.0, in1=mp[0][:],
                                                   op0=ALU.max, op1=ALU.mult).then_inc(ul_ok, 1)
                    dve.wait_ge(ul_ok, g + 1)
                    for i in range(GRP):
                        nc.vector.tensor_tensor_reduce(out=k_l[:, i, :], in0=a_l[:, i, :], in1=s.adj_ne[:], scale=1.0,
                                                       scalar=0.0, op0=ALU.mult, op1=ALU.add,
                                                       accum_out=deg[:, 0, i:i + 1]).then_inc(kl_ok, 1)

                def distances():
                    dve.wait_ge(mg_t, g + 1)
                    for i in range(GRP):
                        nc.vector.scalar_tensor_tensor(out=a_g[:, i, :], in0=m[:, i, 1, :], scalar=mnn[:, i, 1:2],
                                                       in1=tr[1][:, i * P:(i + 1) * P], op0=ALU.subtract,
                                                       op1=ALU.add).then_inc(tg_ok, 1)
                    dve.wait_ge(tg_ok, GRP * (g + 1))
                    nc.vector.tensor_scalar(a_g[:], a_g[:], 0.0, None, ALU.min).then_inc(cl_ok, 1)

                def kernel_g():
                    dve.wait_ge(eg_ok, g + 1)
                    for i in range(GRP):
                        nc.vector.tensor_tensor_reduce(out=k_g[:, i, :], in0=a_g[:, i, :], in1=s.adj_ne[:], scale=1.0,
                                                       scalar=0.0, op0=ALU.mult, op1=ALU.add,
                                                       accum_out=deg[:, 1, i:i + 1]).then_inc(kg_ok, 1)

                def kernel_l_scaled():
                    n = 3 * gp
                    dve.wait_ge(kl_ok, GRP * (gp + 1))
                    nc.vector.tensor_tensor(small[:, 0, :], r_l[:], deg[:, 0, :], ALU.mult).then_inc(sm_ok, 1)
                    dve.wait_ge(sm_ok, n + 1)
                    nc.vector.tensor_scalar(small[:, 0, :], small[:, 0, :], EPS, None, ALU.max).then_inc(sm_ok, 1)
                    dve.wait_ge(sm_ok, n + 2)
                    nc.vector.reciprocal(small[:, 2, :], small[:, 0, :]).then_inc(sm_ok, 1)
                    dve.wait_ge(sm_ok, n + 3)
                    nc.vector.scalar_tensor_tensor(out=small[:, 4, :], in0=r_l[:], scalar=s.w_l[:, 0:1],
                                                   in1=small[:, 2, :], op0=ALU.mult, op1=ALU.mult).then_inc(cf_ok, 1)
                    dve.wait_ge(cf_ok, gp + 1)
                    for i in range(GRP):
                        nc.vector.tensor_scalar(k_l[:, i, :], k_l[:, i, :], small[:, 4, i:i + 1], None,
                                                ALU.mult).then_inc(ka_ok, 1)

                def kernel_sum():
                    n = 3 * gp
                    dve.wait_ge(kg_ok, GRP * (gp + 1))
                    nc.vector.tensor_scalar(small[:, 1, :], deg[:, 1, :], EPS, None, ALU.max).then_inc(sg_ok, 1)
                    dve.wait_ge(sg_ok, n + 1)
                    nc.vector.reciprocal(small[:, 3, :], small[:, 1, :]).then_inc(sg_ok, 1)
                    dve.wait_ge(sg_ok, n + 2)
                    nc.vector.tensor_scalar(small[:, 5, :], small[:, 3, :], s.w_g[:, 0:1], None, ALU.mult).then_inc(sg_ok, 1)
                    dve.wait_ge(sg_ok, n + 3)
                    for i in range(GRP):
                        dve.wait_ge(ka_ok, GRP * gp + i + 1)
                        nc.vector.scalar_tensor_tensor(out=k_g[:, i, :], in0=k_g[:, i, :], scalar=small[:, 5, i:i + 1],
                                                       in1=k_l[:, i, :], op0=ALU.mult, op1=ALU.add).then_inc(k_ok, 1)

                def kt_lo():
                    dve.wait_ge(kt_hi_ok, gp + 1)
                    lo_part(kt[1][:].rearrange("p i n -> p (i n)"), tr[0][:], kt[0][:].rearrange("p i n -> p (i n)"), kt_lo_ok)

                def residual_b(i):
                    dve.wait_ge(l1_made, GRP * gp + i + 1)
                    dve.wait_ge(xb_ok, GRP + GRP * gp + i + 1)
                    dve.wait_ge(stored[i], 16 * (gp + 1))
                    nc.vector.tensor_tensor(xo[:, i, :], mp[i % 2][:], xb[:, i, :], ALU.add).then_inc(yb_ok, 1)

                def stats_b(i):
                    dve.wait_ge(yb_ok, GRP + GRP * gp + i + 1)
                    j = slice(i, i + 1)
                    statistics(nc, dve, xo[:, i, :], st_b[:, i, :], mv_b[:, i, :], ve_b[:, j], nm_b[:, j],
                               yb_ok, st_b_ok, GRP * gp + i + 1, passed)

                A, B, C = ga is not None, g is not None, gp is not None
                if A:
                    xw_lo_(0)
                if C:
                    kernel_l_scaled()
                    kernel_sum()
                if B:
                    y_lo(0)
                if A:
                    residual_a(0)
                    xw_lo_(1)
                if C:
                    kt_lo()
                if A:
                    stats_a(0)
                if B:
                    y_lo(1)
                if C:
                    residual_b(0)
                    residual_b(1)
                    stats_b(0)
                    stats_b(1)
                if A:
                    residual_a(1)
                if C:
                    residual_b(2)
                    residual_b(3)
                if A:
                    xw_lo_(2)
                    stats_a(1)
                if C:
                    stats_b(2)
                    stats_b(3)
                if B:
                    y_lo(2)
                if A:
                    residual_a(2)
                    stats_a(2)
                    xw_lo_(3)
                if B:
                    y_lo(3)
                if A:
                    residual_a(3)
                    stats_a(3)
                if B:
                    v_lo(0)
                    diagonals()
                    v_lo(1)
                    diag_r()
                    metric_l()
                    distances()
                if A:
                    ht_lo(0)
                if B:
                    v_lo(2)
                    kernel_l()
                if A:
                    ht_lo(1)
                if B:
                    kernel_g()
                    v_lo(3)
                if A:
                    ht_lo(2)
                    ht_lo(3)

            dve.sem_inc(xw_lo_ok, 1)
            dve.sem_inc(v_lo_ok, GRP)
            dve.sem_inc(kt_lo_ok, 1)
            dve.sem_inc(yb_ok, GRP)
            turns(dve, turn)


def last_layers(nc, s, x, xw, out):
    nb = x.shape[0]
    groups = nb // GRP
    with ExitStack() as ctx:
        sb, ps, sem = scope(nc, ctx)
        xin = sb("xin", [P, GRP, N])
        xw_hi, xw_lo = sb("xw_hi", [P, 2, N], F32R), sb("xw_lo", [P, 2, N], F32R)
        xa = sb("xa", [P, GRP, N])
        x_hi, x_lo = sb("x_hi", [P, GRP, N], F32R), sb("x_lo", [P, GRP, N], F32R)
        xo = sb("xo", [P, GRP, N])
        st, mv = sb("st", [P, GRP, 2, 6]), sb("mv", [P, GRP, 2, 2])
        ve, nm, rs, nbias = (sb(n, [P, GRP, 2]) for n in ("ve", "nm", "rs", "nbias"))
        l2_ps, l3_ps = [ps("l2_ps0"), ps("l2_ps1")], [ps("l3_ps0"), ps("l3_ps1")]

        x_loaded = [sem(f"x_in{i}") for i in range(GRP)]
        stored = [sem(f"stored{i}") for i in range(GRP)]
        passed = sem("passed")
        xw_hi_ok, xw_lo_ok, l2_made, l3_made = (sem(n) for n in ("xw_hi_ok", "xw_lo_ok", "l2_made", "l3_made"))
        ya_ok, yb_ok, bn_a_ok, bn_b_ok, agg_ok, st_ok, rs_ok = (
            sem(n) for n in ("ya_ok", "yb_ok", "bn_a_ok", "bn_b_ok", "agg_ok", "st_ok", "rs_ok"))
        xa_ok, x_hi_ok, x_lo_ok, xo_ok = (sem(n) for n in ("xa_ok", "x_hi_ok", "x_lo_ok", "xo_ok"))
        block = ctx.enter_context(nc.Block())

        def turns(eng, turn):
            turn(None, None, 0, True)
            turn(None, 0, 1, True)
            with eng.Fori(0, groups - 3) as gp:
                turn(gp, gp + 1, gp + 2, True)
            turn(groups - 3, groups - 2, groups - 1, False)
            turn(groups - 2, groups - 1, None, False)

        def of_batch(ga, i):
            return xw[:, bass.ds(GRP * ga + i, 1), :].rearrange("p a n -> p (a n)")

        def of_step(g, ga, i):
            b = (g, i) if g is not None else None
            a = ((ga, i - 1) if ga is not None else None) if i else ((g, GRP - 1) if g is not None else None)
            kinds = slice(0 if a else 1, 2 if b else 1)
            return b, a, kinds, (GRP * ga if ga is not None else GRP * groups) + i + 1

        def step_before(gp, g, ga, i):
            if i:
                return (*of_step(g, ga, i - 1), i - 1)
            return (*of_step(gp, g, GRP - 1), GRP - 1) if g is not None else (None, None, None, 0, 0)

        def after(ga, i, more):
            if ga is None or (i + 1 == GRP and not more):
                return None
            return (ga, i + 1) if i + 1 < GRP else (ga + 1, 0)

        @block.sync
        def _(sp):
            def load(b, i):
                sp.dma_start(xin[:, i, :], x[bass.ds(b, 1)].rearrange("a p n -> p (a n)")).then_inc(x_loaded[i], 16)

            def store(b, i):
                sp.dma_start(out[bass.ds(b, 1)].rearrange("a p n -> p (a n)"), xo[:, i, :]).then_inc(stored[i], 16)

            for i in range(GRP):
                load(i, i)
            for i in range(GRP):
                sp.wait_ge(ya_ok, i + 1)
                load(GRP + i, i)
            with sp.Fori(0, groups - 2) as g:
                for i in range(GRP):
                    at = sp.snap(g * GRP + i)
                    sp.wait_ge(xo_ok, GRP * g + i + 1)
                    store(at, i)
                    at = sp.snap(g * GRP + 2 * GRP + i)
                    sp.wait_ge(ya_ok, GRP * g + GRP + i + 1)
                    load(at, i)
            for g in (groups - 2, groups - 1):
                for i in range(GRP):
                    sp.wait_ge(xo_ok, GRP * g + i + 1)
                    store(g * GRP + i, i)
            for i in range(GRP):
                sp.wait_ge(stored[i], 16 * (groups + 1))

        @block.tensor
        def _(pe):
            def turn(gp, g, ga, more):
                def l2(i):
                    pe.wait_ge(xw_hi_ok, GRP * ga + i + 1)
                    pe.wait_ge(xw_lo_ok, GRP * ga + i + 1)
                    if not first(ga) or i >= 2:
                        pe.wait_ge(ya_ok, GRP * ga + i - 1)
                    xwp, anp = (xw_hi, xw_lo), (s.an_hi, s.an_lo)
                    for c in range(CH):
                        for n, (a, b) in enumerate(HILO):
                            mm = nc.tensor.matmul(l2_ps[i % 2][:], xwp[a][:, i % 2, c * P:(c + 1) * P], anp[b][:, c, :],
                                                  start=(c == 0 and n == 0), stop=(c == CH - 1 and n == 2))
                    mm.then_inc(l2_made, 1)

                def l3(i):
                    pe.wait_ge(x_hi_ok, GRP * g + i + 1)
                    pe.wait_ge(x_lo_ok, GRP * g + i + 1)
                    pe.wait_ge(yb_ok, GRP * g + i + 1)
                    wp, xp = (s.res_w_hi, s.res_w_lo), (x_hi, x_lo)
                    for n, (a, b) in enumerate(HILO):
                        mm = nc.tensor.matmul(l3_ps[i % 2][:], wp[a][:], xp[b][:, i, :], start=(n == 0), stop=(n == 2))
                    mm.then_inc(l3_made, 1)

                for i in range(GRP):
                    if g is not None:
                        l3(i)
                    if ga is not None:
                        l2(i)

            turns(pe, turn)

        @block.scalar
        def _(act):
            def xw_hi_(ga, i):
                act.wait_ge(l2_made, GRP * ga + i + 1)
                nc.scalar.activation(xw_hi[:, i % 2, :], of_batch(ga, i), ACT.Copy).then_inc(xw_hi_ok, 1)

            def turn(gp, g, ga, more):
                for i in range(GRP):
                    following = after(ga, i, more)
                    if following:
                        xw_hi_(*following)
                    normalise(*step_before(gp, g, ga, i))

            def normalise(b, a, kinds, step, slot):
                if a or b:
                    act.wait_ge(rs_ok, 2 * step - 2)
                if b:
                    nc.scalar.activation(xo[:, slot, :], xo[:, slot, :], ACT.Identity,
                                         scale=rs[:, slot, 1:2], bias=nbias[:, slot, 1:2]).then_inc(xo_ok, 1)
                if a:
                    n = GRP * a[0] + a[1] + 1
                    nc.scalar.activation(xa[:, a[1], :], xa[:, a[1], :], ACT.Identity,
                                         scale=rs[:, slot, 0:1], bias=nbias[:, slot, 0:1]).then_inc(xa_ok, 1)
                    act.wait_ge(xa_ok, n)
                    act.wait_ge(l3_made, n)
                    nc.scalar.activation(x_hi[:, a[1], :], xa[:, a[1], :], ACT.Copy).then_inc(x_hi_ok, 1)

            act.sem_inc(l2_made, 2)
            act.sem_inc(l3_made, GRP)
            for i in range(GRP):
                act.sem_inc(stored[i], 16)
            xw_hi_(0, 0)
            turns(act, turn)
            normalise(*of_step(groups - 1, None, GRP - 1), GRP - 1)

        @block.gpsimd
        def _(pool):
            def xw_lo_(ga, i):
                pool.wait_ge(xw_hi_ok, GRP * ga + i + 1)
                nc.gpsimd.tensor_tensor(xw_lo[:, i % 2, :], of_batch(ga, i), xw_hi[:, i % 2, :].bitcast(F32),
                                        ALU.subtract).then_inc(xw_lo_ok, 1)

            def turn(gp, g, ga, more):
                for i in range(GRP):
                    following = after(ga, i, more)
                    if following:
                        xw_lo_(*following)
                    b, a, kinds, step = of_step(g, ga, i)
                    if a or b:
                        w = kinds.stop - kinds.start
                        pool.wait_ge(st_ok, step - 1)
                        nc.gpsimd.tensor_tensor(rs[:, i, kinds], ve[:, i, kinds], s.neghalf[:, 0:w],
                                                ALU.pow).then_inc(rs_ok, 1)
                        pool.wait_ge(rs_ok, 2 * step - 3)
                        nc.gpsimd.tensor_tensor(nbias[:, i, kinds], nm[:, i, kinds], rs[:, i, kinds],
                                                ALU.mult).then_inc(rs_ok, 1)
                    low_part(step_before(gp, g, ga, i)[1])

            def low_part(a):
                if a:
                    n = GRP * a[0] + a[1] + 1
                    pool.wait_ge(x_hi_ok, n)
                    nc.gpsimd.tensor_tensor(x_lo[:, a[1], :], xa[:, a[1], :], x_hi[:, a[1], :].bitcast(F32),
                                            ALU.subtract).then_inc(x_lo_ok, 1)

            xw_lo_(0, 0)
            turns(pool, turn)

        @block.vector
        def _(dve):
            def turn(gp, g, ga, more):
                for i in range(GRP):
                    b, a, kinds, step = of_step(g, ga, i)
                    if not (a or b):
                        continue
                    if b:
                        n_b = GRP * g + i + 1
                        dve.wait_ge(l3_made, GRP + n_b)
                        dve.wait_ge(stored[i], 16 * (g + 1))
                        nc.vector.tensor_tensor(xo[:, i, :], l3_ps[i % 2][:], s.b3[:], ALU.add).then_inc(yb_ok, 1)
                    if a:
                        n_a = GRP * a[0] + a[1] + 1
                        dve.wait_ge(l2_made, 2 + n_a)
                        dve.wait_ge(x_loaded[a[1]], 16 * (a[0] + 1))
                        nc.vector.scalar_tensor_tensor(out=xa[:, a[1], :], in0=l2_ps[a[1] % 2][:],
                                                       scalar=s.b2[:, 0:1], in1=xin[:, a[1], :],
                                                       op0=ALU.add, op1=ALU.add).then_inc(ya_ok, 1)
                    if b:
                        dve.wait_ge(yb_ok, 2 + n_b)
                        nc.vector.bn_stats(st[:, i, 1, :], xo[:, i, :]).then_inc(bn_b_ok, 1)
                    if a:
                        dve.wait_ge(ya_ok, n_a)
                        nc.vector.bn_stats(st[:, i, 0, :], xa[:, a[1], :]).then_inc(bn_a_ok, 1)
                    if b:
                        dve.wait_ge(bn_b_ok, n_b)
                        own_step(dve, passed)
                        agg = nc.vector.bn_aggr(mv[:, i, 1, :], st[:, i, 1, :])
                    if a:
                        dve.wait_ge(bn_a_ok, n_a)
                        own_step(dve, passed)
                        agg = nc.vector.bn_aggr(mv[:, i, 0, :], st[:, i, 0, :])
                    agg.then_inc(agg_ok, 1)
                    dve.wait_ge(agg_ok, step - 1)
                    nc.vector.tensor_scalar(ve[:, i, kinds], mv[:, i, kinds, 1], LN_EPS, None, ALU.add)
                    nc.vector.tensor_scalar(nm[:, i, kinds], mv[:, i, kinds, 0], -1.0, None, ALU.mult).then_inc(st_ok, 1)

            dve.sem_inc(yb_ok, 2)
            turns(dve, turn)


def adj_resnorm_kernel(nc, x, adj, bias0, w_lang, w_grav, w_v, w_o, gate, log_sigma, bias2, bias3, out):
    nb = x.shape[0]
    assert x.shape[1:] == (P, N) and nb % SGRP == 0 and nb <= P
    between = nc.dram_tensor("between", [nb, P, N], F32, kind="Internal").ap()
    n2 = nc.dram_tensor("n2", [nb, N], F32, kind="Internal").ap()
    spill_hi = nc.dram_tensor("spill_hi", [nb, N], F32, kind="Internal").ap()
    spill_lo = nc.dram_tensor("spill_lo", [nb, N], F32, kind="Internal").ap()
    s = Shared()
    s.nb = nb
    with ExitStack() as ctx:
        constants(nc, ctx, s)

        def similarities(xres, source, psum_room):
            with ExitStack() as row_room:
                sb, _, _ = scope(nc, row_room)
                rows = sb("rows", [2 * SGRP, nb // SGRP, N], F32R)
                if source is None:
                    first_norms(nc, s, x, xres, n2, (adj, bias0, bias2, bias3, gate, log_sigma))
                _, ps, _ = scope(nc, psum_room)
                hh, hl = [ps(f"hh{k}") for k in range(3)], [ps(f"hl{k}") for k in range(CH)]
                norm_rows(nc, s, n2, rows, spill_hi, spill_lo)
                similarity(nc, s, xres, rows, hh, hl, source)
            return hh, hl

        def adjacency(hh, hl, psum_room, weights, xres):
            with ExitStack() as choice_room:
                sb, _, _ = scope(nc, choice_room)
                sim, work = sb("sim", [P, CH, N]), sb("work", [P, CH, 8 + N])
                whole_similarity(nc, s, hh, hl, sim, work)
                psum_room.close()
                choose(nc, s, work, weights, xres)
                normal_adjacency(nc, s, sim, work)

        with ExitStack() as psum_room, ExitStack() as weight_room:
            with ExitStack() as x_room:
                sb, _, _ = scope(nc, x_room)
                hh, hl = similarities(sb("xres", [P, nb, N]), None, psum_room)
            sb, _, _ = scope(nc, weight_room)
            dst = {k: [sb(f"u_{k}_{p}", [P, TRI_W], F32R) for p in ("hi", "lo")] for k in ("lang", "grav")}
            dst["ov"] = [sb(f"wov_{p}", [P, CH, N], F32R) for p in ("hi", "lo")]
            adjacency(hh, hl, psum_room, ({"lang": w_lang, "grav": w_grav, "v": w_v, "o": w_o}, dst), None)
            gnn_layer_pair(nc, s, x, between, dst["lang"], dst["grav"], dst["ov"], n2)
        with ExitStack() as psum_room, ExitStack() as x_room:
            sb, _, _ = scope(nc, x_room)
            xres = sb("xres", [P, nb, N])
            hh, hl = similarities(xres, between, psum_room)
            adjacency(hh, hl, psum_room, None, xres)
            last_layers(nc, s, between, xres, out)


_INS = ["x", "adj", "L0_gnn_bias", "L1_gnn_W_lang", "L1_gnn_W_grav", "L1_gnn_W_V", "L1_gnn_W_O",
        "L1_gnn_gate_logit", "L1_gnn_log_sigma", "L2_gnn_bias", "L3_gnn_bias"]


def kernel(**inputs):
    import concourse.bacc as _bacc
    from concourse.bass_utils import run_bass_kernel_spmd as _run

    nc = _bacc.Bacc("TRN2", target_bir_lowering=False, num_devices=1)
    arrays, args = {}, []
    for name in _INS:
        a = np.ascontiguousarray(inputs[name])
        if a.ndim == 0:
            a = a.reshape(1, 1)
        arrays[f"in_{name}"] = a
        args.append(nc.dram_tensor(f"in_{name}", a.shape, mybir.dt.from_np(a.dtype), kind="ExternalInput").ap())
    shape = inputs["x"].shape
    out = nc.dram_tensor("out_0", shape, F32, kind="ExternalOutput").ap()
    adj_resnorm_kernel(nc, *args, out)
    r = _run(nc, [arrays], core_ids=[0])
    return r.results[0]["out_0"]
```
